# Optimizing a Trainium2 kernel written in Bass

```python
import numpy as np
import jax
import jax.numpy as jnp

def _softmax(x, axis=-1):
    return jax.nn.softmax(x, axis=axis)

def _gelu(x):
    return jax.nn.gelu(x, approximate=True)

def _silu(x):
    return jax.nn.silu(x)

def _sigmoid(x):
    return jax.nn.sigmoid(x)

def _layernorm(x, axis=-1, eps=1e-05):
    m = jnp.mean(x, axis=axis, keepdims=True)
    v = jnp.var(x, axis=axis, keepdims=True)
    return (x - m) / jnp.sqrt(v + eps)

def _scatter_add(tgt, idx, src, axis=0):
    return tgt.at[idx].add(src)

def _segment_sum(src, seg, n):
    return jax.ops.segment_sum(src, seg, n)
kernel_name = 'mk_audio_tower_d1_tok_aud1d768_r4_64a185'

def setup_inputs(seed: int=0):
    np.random.seed(seed)
    _w = jnp.asarray

    def _rec_inputs():
        import jax
        import jax.numpy as jnp
        _rk = jax.random.key(seed)
        x = -6.41493e-05 + 1.00002 * jax.random.normal(jax.random.fold_in(_rk, 1), (16, 80000), jnp.float32)
        return x
    x = _rec_inputs()

    def _L0_tok_setup():
        import jax, jax.numpy as jnp
        import numpy as np
        import math
        SR = 4000
        FRAME_LEN = 100
        FRAME_STEP = 160
        N_FILTERS = 40
        N_MFCC = 13
        EMBED = 192
        BATCH = 64
        AUDIO_LEN = 40000
        N_FFT_BINS = FRAME_LEN // 2 + 1

        def _mel_filterbank():
            low_mel = 2595.0 * math.log10(1.0 + 0.0 / 700.0)
            high_mel = 2595.0 * math.log10(1.0 + SR // 2 / 700.0)
            mel_points = np.linspace(low_mel, high_mel, N_FILTERS + 2)
            hz_points = 700.0 * (10.0 ** (mel_points / 2595.0) - 1.0)
            bin_points = np.floor((FRAME_LEN + 1) * hz_points / SR)
            filt = np.zeros((N_FILTERS, N_FFT_BINS), dtype=np.float32)
            for i in range(1, N_FILTERS + 1):
                l, c, r = (bin_points[i - 1], bin_points[i], bin_points[i + 1])
                for j in range(int(l), int(c)):
                    filt[i - 1, j] = (j - l) / (c - l)
                for j in range(int(c), int(r)):
                    filt[i - 1, j] = (r - j) / (r - c)
            return jnp.asarray(filt)

        def _dct_matrix():
            k = np.arange(N_MFCC)[:, None]
            j = np.arange(N_FILTERS)[None, :]
            m = np.cos(np.pi * k * (2 * j + 1) / (2 * N_FILTERS)) * math.sqrt(2.0 / N_FILTERS)
            return jnp.asarray(m.astype(np.float32))
        key = jax.random.key(seed)
        kx, kw = jax.random.split(key)
        x = jax.random.normal(kx, (BATCH, AUDIO_LEN), dtype=jnp.float32)
        bound = 1.0 / math.sqrt(N_MFCC)
        w_proj = jax.random.uniform(kw, (N_MFCC, EMBED), minval=-bound, maxval=bound, dtype=jnp.float32)
        b_proj = jnp.zeros((EMBED,), dtype=jnp.float32)
        return {'x': x, 'mel_filters': _mel_filterbank(), 'dct': _dct_matrix(), 'w_proj': w_proj, 'b_proj': b_proj}
    _L0_tok_all = _L0_tok_setup()
    _L0_tok_in = {k: v for k, v in _L0_tok_all.items() if k in ('mel_filters', 'dct', 'w_proj', 'b_proj')}
    del _L0_tok_all

    def _L0_attn_setup():
        import jax, jax.numpy as jnp
        import numpy as np
        import math
        N_LAYER, N_EMBD, LAYER_ID = (12, 192, 0)
        B, T, C = (32, 256, N_EMBD)

        def _init_params():
            r01 = LAYER_ID / (N_LAYER - 1)
            r1a0 = 1.0 - LAYER_ID / N_LAYER
            h = np.arange(C, dtype=np.float32)
            time_decay = (-5.0 + 8.0 * (h / (C - 1)) ** (0.7 + 1.3 * r01)).astype(np.float32)
            zigzag = np.array([(i + 1) % 3 - 1 for i in range(C)], dtype=np.float32) * 0.5
            time_first = (np.ones(C, dtype=np.float32) * math.log(0.3) + zigzag).astype(np.float32)
            xlin = (np.arange(C, dtype=np.float32) / C).reshape(1, 1, C)
            time_mix_k = np.power(xlin, r1a0).astype(np.float32)
            time_mix_v = (np.power(xlin, r1a0) + 0.3 * r01).astype(np.float32)
            time_mix_r = np.power(xlin, 0.5 * r1a0).astype(np.float32)
            return (time_decay, time_first, time_mix_k, time_mix_v, time_mix_r)

        def _wkv(w, u, k, v):

            def step(carry, kv):
                p, q, o = carry
                kt, vt = kv
                no = jnp.maximum(o, u + kt)
                A = jnp.exp(o - no)
                Bc = jnp.exp(u + kt - no)
                y = (A * p + Bc * vt) / (A * q + Bc)
                no2 = jnp.maximum(w + o, kt)
                A2 = jnp.exp(w + o - no2)
                B2 = jnp.exp(kt - no2)
                return ((A2 * p + B2 * vt, A2 * q + B2, no2), y)
            b = k.shape[0]
            init = (jnp.zeros((b, C), jnp.float32), jnp.zeros((b, C), jnp.float32), jnp.full((b, C), -1e+38, jnp.float32))
            kT = jnp.swapaxes(k, 0, 1)
            vT = jnp.swapaxes(v, 0, 1)
            _, ys = jax.lax.scan(step, init, (kT, vT))
            return jnp.swapaxes(ys, 0, 1)
        key = jax.random.key(seed)
        ks = jax.random.split(key, 5)
        td, tf, tmk, tmv, tmr = _init_params()
        scale = 0.02
        return {'x': jax.random.normal(ks[0], (B, T, C), dtype=jnp.float32), 'time_decay': jnp.asarray(td), 'time_first': jnp.asarray(tf), 'time_mix_k': jnp.asarray(tmk), 'time_mix_v': jnp.asarray(tmv), 'time_mix_r': jnp.asarray(tmr), 'Wk': jax.random.normal(ks[1], (C, C), dtype=jnp.float32) * scale, 'Wv': jax.random.normal(ks[2], (C, C), dtype=jnp.float32) * scale, 'Wr': jax.random.normal(ks[3], (C, C), dtype=jnp.float32) * scale, 'Wo': jax.random.normal(ks[4], (C, C), dtype=jnp.float32) * scale}
    _L0_attn_all = _L0_attn_setup()
    _L0_attn_in = {k: v for k, v in _L0_attn_all.items() if k in ('time_decay', 'time_first', 'time_mix_k', 'time_mix_v', 'time_mix_r', 'Wk', 'Wv', 'Wr', 'Wo')}
    del _L0_attn_all

    def _L0_ffn_setup():
        import jax, jax.numpy as jnp
        import numpy as np
        E = 8
        K = 2
        D = 192
        F = 4 * D
        key = jax.random.key(seed)
        ks = jax.random.split(key, 10)
        s_exp = 0.02
        return {'x': jax.random.normal(ks[0], (4, 256, D), jnp.float32), 'W1': jax.random.normal(ks[1], (E, F, D), jnp.float32) * s_exp, 'b1': jax.random.normal(ks[2], (E, F), jnp.float32) * s_exp, 'W2': jax.random.normal(ks[3], (E, D, F), jnp.float32) * s_exp, 'b2': jax.random.normal(ks[4], (E, D), jnp.float32) * s_exp, 'Wr1': jax.random.normal(ks[5], (D, D), jnp.float32) * s_exp, 'br1': jax.random.normal(ks[6], (D,), jnp.float32) * s_exp, 'Wr2': jax.random.normal(ks[7], (E, D), jnp.float32) * s_exp, 'br2': jax.random.normal(ks[8], (E,), jnp.float32) * s_exp}
    _L0_ffn_all = _L0_ffn_setup()
    _L0_ffn_in = {k: v for k, v in _L0_ffn_all.items() if k in ('W1', 'b1', 'W2', 'b2', 'Wr1', 'br1', 'Wr2', 'br2')}
    del _L0_ffn_all
    return {'x': x, 'L0_tok_mel_filters': _L0_tok_in['mel_filters'], 'L0_tok_dct': _L0_tok_in['dct'], 'L0_tok_w_proj': _L0_tok_in['w_proj'], 'L0_tok_b_proj': _L0_tok_in['b_proj'], 'L0_attn_time_decay': _L0_attn_in['time_decay'], 'L0_attn_time_first': _L0_attn_in['time_first'], 'L0_attn_time_mix_k': _L0_attn_in['time_mix_k'], 'L0_attn_time_mix_v': _L0_attn_in['time_mix_v'], 'L0_attn_time_mix_r': _L0_attn_in['time_mix_r'], 'L0_attn_Wk': _L0_attn_in['Wk'], 'L0_attn_Wv': _L0_attn_in['Wv'], 'L0_attn_Wr': _L0_attn_in['Wr'], 'L0_attn_Wo': _L0_attn_in['Wo'], 'L0_ffn_W1': _L0_ffn_in['W1'], 'L0_ffn_b1': _L0_ffn_in['b1'], 'L0_ffn_W2': _L0_ffn_in['W2'], 'L0_ffn_b2': _L0_ffn_in['b2'], 'L0_ffn_Wr1': _L0_ffn_in['Wr1'], 'L0_ffn_br1': _L0_ffn_in['br1'], 'L0_ffn_Wr2': _L0_ffn_in['Wr2'], 'L0_ffn_br2': _L0_ffn_in['br2']}

def reference(x, L0_tok_mel_filters, L0_tok_dct, L0_tok_w_proj, L0_tok_b_proj, L0_attn_time_decay, L0_attn_time_first, L0_attn_time_mix_k, L0_attn_time_mix_v, L0_attn_time_mix_r, L0_attn_Wk, L0_attn_Wv, L0_attn_Wr, L0_attn_Wo, L0_ffn_W1, L0_ffn_b1, L0_ffn_W2, L0_ffn_b2, L0_ffn_Wr1, L0_ffn_br1, L0_ffn_Wr2, L0_ffn_br2):
    import jax
    import jax.numpy as jnp

    def _L0_tok_ref(x, mel_filters, dct, w_proj, b_proj):
        import jax, jax.numpy as jnp
        import numpy as np
        import math
        SR = 4000
        FRAME_LEN = 100
        FRAME_STEP = 160
        N_FILTERS = 40
        N_MFCC = 13
        EMBED = 192
        BATCH = 64
        AUDIO_LEN = 40000
        N_FFT_BINS = FRAME_LEN // 2 + 1

        def _mel_filterbank():
            low_mel = 2595.0 * math.log10(1.0 + 0.0 / 700.0)
            high_mel = 2595.0 * math.log10(1.0 + SR // 2 / 700.0)
            mel_points = np.linspace(low_mel, high_mel, N_FILTERS + 2)
            hz_points = 700.0 * (10.0 ** (mel_points / 2595.0) - 1.0)
            bin_points = np.floor((FRAME_LEN + 1) * hz_points / SR)
            filt = np.zeros((N_FILTERS, N_FFT_BINS), dtype=np.float32)
            for i in range(1, N_FILTERS + 1):
                l, c, r = (bin_points[i - 1], bin_points[i], bin_points[i + 1])
                for j in range(int(l), int(c)):
                    filt[i - 1, j] = (j - l) / (c - l)
                for j in range(int(c), int(r)):
                    filt[i - 1, j] = (r - j) / (r - c)
            return jnp.asarray(filt)

        def _dct_matrix():
            k = np.arange(N_MFCC)[:, None]
            j = np.arange(N_FILTERS)[None, :]
            m = np.cos(np.pi * k * (2 * j + 1) / (2 * N_FILTERS)) * math.sqrt(2.0 / N_FILTERS)
            return jnp.asarray(m.astype(np.float32))
        B, T = x.shape
        n_frames = 1 + (T - FRAME_LEN) // FRAME_STEP
        idx = jnp.arange(n_frames)[:, None] * FRAME_STEP + jnp.arange(FRAME_LEN)[None, :]
        frames = x[:, idx]
        window = 0.54 - 0.46 * jnp.cos(2.0 * jnp.pi * jnp.arange(FRAME_LEN, dtype=jnp.float32) / (FRAME_LEN - 1))
        windowed = frames * window
        fft = jnp.fft.rfft(windowed, axis=-1)
        power = fft.real ** 2 + fft.imag ** 2
        mel_energies = jnp.einsum('bnf,mf->bnm', power, mel_filters)
        log_energies = jnp.log(mel_energies + 1e-06)
        mfcc = jnp.einsum('bnm,km->bnk', log_energies, dct)
        out = mfcc @ w_proj + b_proj
        return out

    def _L0_attn_ref(x, time_decay, time_first, time_mix_k, time_mix_v, time_mix_r, Wk, Wv, Wr, Wo):
        import jax, jax.numpy as jnp
        import numpy as np
        import math
        N_LAYER, N_EMBD, LAYER_ID = (12, 192, 0)
        B, T, C = (32, 256, N_EMBD)

        def _init_params():
            r01 = LAYER_ID / (N_LAYER - 1)
            r1a0 = 1.0 - LAYER_ID / N_LAYER
            h = np.arange(C, dtype=np.float32)
            time_decay = (-5.0 + 8.0 * (h / (C - 1)) ** (0.7 + 1.3 * r01)).astype(np.float32)
            zigzag = np.array([(i + 1) % 3 - 1 for i in range(C)], dtype=np.float32) * 0.5
            time_first = (np.ones(C, dtype=np.float32) * math.log(0.3) + zigzag).astype(np.float32)
            xlin = (np.arange(C, dtype=np.float32) / C).reshape(1, 1, C)
            time_mix_k = np.power(xlin, r1a0).astype(np.float32)
            time_mix_v = (np.power(xlin, r1a0) + 0.3 * r01).astype(np.float32)
            time_mix_r = np.power(xlin, 0.5 * r1a0).astype(np.float32)
            return (time_decay, time_first, time_mix_k, time_mix_v, time_mix_r)

        def _wkv(w, u, k, v):

            def step(carry, kv):
                p, q, o = carry
                kt, vt = kv
                no = jnp.maximum(o, u + kt)
                A = jnp.exp(o - no)
                Bc = jnp.exp(u + kt - no)
                y = (A * p + Bc * vt) / (A * q + Bc)
                no2 = jnp.maximum(w + o, kt)
                A2 = jnp.exp(w + o - no2)
                B2 = jnp.exp(kt - no2)
                return ((A2 * p + B2 * vt, A2 * q + B2, no2), y)
            b = k.shape[0]
            init = (jnp.zeros((b, C), jnp.float32), jnp.zeros((b, C), jnp.float32), jnp.full((b, C), -1e+38, jnp.float32))
            kT = jnp.swapaxes(k, 0, 1)
            vT = jnp.swapaxes(v, 0, 1)
            _, ys = jax.lax.scan(step, init, (kT, vT))
            return jnp.swapaxes(ys, 0, 1)
        xx = jnp.pad(x, ((0, 0), (1, 0), (0, 0)))[:, :-1, :]
        xk = x * time_mix_k + xx * (1.0 - time_mix_k)
        xv = x * time_mix_v + xx * (1.0 - time_mix_v)
        xr = x * time_mix_r + xx * (1.0 - time_mix_r)
        k = jnp.einsum('btc,oc->bto', xk, Wk)
        v = jnp.einsum('btc,oc->bto', xv, Wv)
        r = jnp.einsum('btc,oc->bto', xr, Wr)
        sr = jax.nn.sigmoid(r)
        y = _wkv(time_decay, time_first, k, v)
        return jnp.einsum('btc,oc->bto', sr * y, Wo)

    def _L0_ffn_ref(x, W1, b1, W2, b2, Wr1, br1, Wr2, br2):
        import jax, jax.numpy as jnp
        import numpy as np
        E = 8
        K = 2
        D = 192
        F = 4 * D
        h = jax.nn.relu(jnp.einsum('bsd,hd->bsh', x, Wr1) + br1)
        score = jnp.einsum('bsd,ed->bse', h, Wr2) + br2
        _, idx = jax.lax.top_k(score, K)
        mask = (jax.nn.one_hot(idx, E) > 0).any(axis=-2)
        w = jax.nn.softmax(jnp.where(mask, score, -jnp.inf), axis=-1)
        out = jnp.zeros_like(x)
        for e in range(E):
            mid = jax.nn.relu(jnp.einsum('bsd,fd->bsf', x, W1[e]) + b1[e])
            ye = jnp.einsum('bsf,df->bsd', mid, W2[e]) + b2[e]
            out = out + w[..., e:e + 1] * ye
        return out
    h = _L0_tok_ref(x, L0_tok_mel_filters, L0_tok_dct, L0_tok_w_proj, L0_tok_b_proj)
    h = h + _L0_attn_ref(_layernorm(h, axis=-1), L0_attn_time_decay, L0_attn_time_first, L0_attn_time_mix_k, L0_attn_time_mix_v, L0_attn_time_mix_r, L0_attn_Wk, L0_attn_Wv, L0_attn_Wr, L0_attn_Wo)
    h = h + _L0_ffn_ref(_layernorm(h, axis=-1), L0_ffn_W1, L0_ffn_b1, L0_ffn_W2, L0_ffn_b2, L0_ffn_Wr1, L0_ffn_br1, L0_ffn_Wr2, L0_ffn_br2)
    return h

_drawn_inputs = setup_inputs


def setup_inputs(seed=0):
    import zlib

    import numpy as np

    out = dict(_drawn_inputs(seed))
    spreads = {'L0_tok_b_proj': (0.0, 0.332)}
    factors = {'L0_attn_time_decay': 8.0,
     'L0_attn_time_first': 8.0,
     'L0_attn_time_mix_k': 8.0,
     'L0_attn_time_mix_v': 8.0,
     'L0_attn_time_mix_r': 8.0,
     'L0_attn_Wk': 8.0,
     'L0_attn_Wv': 6.955,
     'L0_attn_Wr': 8.0,
     'L0_attn_Wo': 7.556,
     'L0_ffn_W1': 3.391,
     'L0_ffn_b1': 27.416,
     'L0_ffn_W2': 2.79,
     'L0_ffn_b2': 30.18,
     'L0_ffn_Wr1': 3.766,
     'L0_ffn_br1': 42.61,
     'L0_ffn_Wr2': 6.606,
     'L0_ffn_br2': 18.693}
    for name, (base, spread) in spreads.items():
        noise = np.random.default_rng([zlib.crc32(name.encode()), seed]).standard_normal(out[name].shape)
        drawn = base * np.exp(spread * noise) if base else spread * noise
        out[name] = jnp.asarray(drawn.astype(out[name].dtype))
    for name, factor in factors.items():
        out[name] = (out[name] * factor).astype(out[name].dtype)
    return out
```

```python
from contextlib import ExitStack

import numpy as np

import concourse.bass as bass
from concourse import mybir

F32 = mybir.dt.float32
U32 = mybir.dt.uint32
I32 = mybir.dt.int32
ALU = mybir.AluOpType
ACT = mybir.ActivationFunctionType
AX = mybir.AxisListType

STREAMS, SAMPLES = 16, 80000
FRAME, HOP = 100, 160
FRAMES = 1 + (SAMPLES - FRAME) // HOP
BINS = FRAME // 2 + 1
MELS, COEFS = 40, 13
C = 192
CA, CB = 128, C - 128
PAIRS = STREAMS // 2
ROWS = 125
TILES = FRAMES // ROWS
G = 2 * TILES
TOKENS = STREAMS * FRAMES
E, F = 8, 768
FC = F // 128
ROWLEN = C + 4
ONE, WEIGHT, TOKEN = C, C + 1, C + 2
CONSTS = 12
SLOTS = TOKENS + 128
BLOCKS = (2 * TOKENS + E * 127) // 128
SPARE = E * SLOTS
NEG = -1e38
EPS = 1e-5


class Steps:

    def __init__(self, sem, names):
        self.sem, self.names = sem, names.split()

    def at(self, name, pair):
        return pair * len(self.names) + self.names.index(name) + 1

    def all(self, pairs):
        return pairs * len(self.names)


def wait(eng, sem, value):
    if not isinstance(value, int) or value > 0:
        eng.wait_ge(sem, value)


def before(eng, steps, pair):
    wait(eng, steps.sem, steps.all(pair))


def after(eng, steps, name, pair):
    if not isinstance(pair, int) or pair >= 0:
        eng.wait_ge(steps.sem, steps.at(name, pair))


def audio_tower(nc, x, dft, mel, dct, w_proj, b_proj, chan, w4, wo, wr2, br2, w1a, w1b, w2, b2, consts, out):
    slots = nc.dram_tensor("slots", (SPARE + 128, ROWLEN), F32, kind="Internal").ap()
    frames_v = x.rearrange("b (t q s) -> q (b t) s", q=ROWS, s=HOP)
    out_v = out[0:TOKENS, :].rearrange("(n q) c -> q n c", q=ROWS)

    with ExitStack() as top:
        def sem(name):
            return top.enter_context(nc.semaphore(name))

        def sb(ctx, name, shape, dt=F32):
            return ctx.enter_context(nc.sbuf_tensor(name, shape, dt))

        ps = top.enter_context(nc.psum_tensor("ps", [128, 8, 512], F32))

        def alone(eng):
            eng.sem_inc(passed, 1)

        ident = sb(top, "ident", [128, 128])
        expert_of = sb(top, "expert_of", [1, BLOCKS], I32)
        slot_of = sb(top, "slot_of", [1, BLOCKS], I32)

        weights_in = sem("weights_in")
        consts_set = sem("consts_set")
        passed = sem("passed")
        g_prod, g_set = sem("g_prod"), sem("g_set")
        frames_in = sem("frames_in")
        rows_out = sem("rows_out")
        scattered = sem("scattered")
        filled = sem("filled")
        counted, tables, fill_pos = sem("counted"), sem("tables"), sem("fill_pos")
        tok_pe = Steps(sem("tok_pe"), "frames0 frames1 dft0 dft1 mel0 mel1 h0 h1 h2 h3 xt0 xt1 xt2")
        tok_act = Steps(sem("tok_act"), "frames0 frames1 pow0 pow1 log0 log1 h0 h1 h2 h3 lnv rstd xt0 xt1 xt2")
        tok_vec = Steps(sem("tok_vec"), "stats aggr var n1 n2 n3 rstd norm tails")
        mix_vec = Steps(sem("mix_vec"), "diff v k r")
        mix_pe = Steps(sem("mix_pe"), "v k r")
        mix_act = Steps(sem("mix_act"), "v k r")
        wkv_vec = Steps(sem("wkv_vec"), "max lead clampA clampB clampC clampD q_scan p_scan aq den num newton1 newton2 z")
        wkv_act = Steps(sem("wkv_act"), "a2 b2 a b lnden rden")
        wkv_pool = Steps(sem("wkv_pool"), "b2v ap bv sn")
        att_pe = Steps(sem("att_pe"), "o0 o1 o2 o3 xt0 xt1 xt2 rh0 rh1 rh2 score rank")
        att_vec = Steps(sem("att_vec"), "h0 h1 h2 h3 stats aggr var n1 n2 n3 rstd norm tails")
        att_act = Steps(sem("att_act"), "lnv rstd xt0 xt1 xt2 copy rh0 rh1 rh2 ex")
        rt_vec = Steps(sem("rt_vec"), "score top index indexf hot mask c1 c2 c3 c4 c5 c6 c7 c8 gap "
                       "sum rec w1 w2 ids carry pos pick0 pos0 pick1 pos1 posu")

        with ExitStack() as ctx:
            dft_s = sb(ctx, "dft_s", [FRAME, 2 * BINS])
            mel_s = sb(ctx, "mel_s", [2 * BINS, MELS])
            dct_s = sb(ctx, "dct_s", [COEFS, MELS])
            wproj_s = sb(ctx, "wproj_s", [COEFS, C])
            proj_s = sb(ctx, "proj_s", [MELS + 1, C])
            chan_s = sb(ctx, "chan_s", [128, 12])
            negu_s = sb(ctx, "negu_s", [128, 2])
            w4_s = sb(ctx, "w4_s", [128, 4, 6, 128])
            wo_s = sb(ctx, "wo_s", [128, 3, C])
            wr2_s = sb(ctx, "wr2_s", [128, 3, E])
            br2_s = sb(ctx, "br2_s", [ROWS, E])
            before_s = sb(ctx, "before_s", [ROWS, ROWS])
            ones_s = sb(ctx, "ones_s", [ROWS, 128])
            lane_s = sb(ctx, "lane_s", [128, 4])
            eidx_s = sb(ctx, "eidx_s", [128, E])
            ebase_s = sb(ctx, "ebase_s", [128, E])
            wide_s = sb(ctx, "wide_s", [1, 64 + BLOCKS])
            eps_s = sb(ctx, "eps_s", [128, 2])
            fill_s = sb(ctx, "fill_s", [128, ROWLEN])

            fr = sb(ctx, "fr", [ROWS, G, FRAME])
            ft = sb(ctx, "ft", [FRAME, 2, FRAMES])
            pw = sb(ctx, "pw", [2 * BINS, 2, FRAMES])
            le = sb(ctx, "le", [64, 2, FRAMES])
            h = sb(ctx, "h", [ROWS, 3, G, C])
            xn = sb(ctx, "xn", [ROWS, G, C])
            tails1 = sb(ctx, "tails1", [ROWS, TILES, 2, CB])
            tails2 = sb(ctx, "tails2", [ROWS, TILES, 2, CB])
            st1 = sb(ctx, "st1", [ROWS, G, 6])
            mv1 = sb(ctx, "mv1", [ROWS, G, 2])
            nw1 = sb(ctx, "nw1", [ROWS, 5, G])
            st2 = sb(ctx, "st2", [ROWS, G, 6])
            mv2 = sb(ctx, "mv2", [ROWS, G, 2])
            nw2 = sb(ctx, "nw2", [ROWS, 5, G])
            xt = sb(ctx, "xt", [128, 3, FRAMES + 1])
            diff = sb(ctx, "diff", [128, 3, FRAMES])
            mixed = [sb(ctx, f"mixed{n}", [128, 3, FRAMES]) for n in "vkr"]
            vs = [sb(ctx, f"vs{n}", [128, 3, FRAMES]) for n in range(2)]
            ks = [sb(ctx, f"ks{n}", [128, 3, FRAMES]) for n in range(2)]
            sig = sb(ctx, "sig", [128, 3, FRAMES])
            om = sb(ctx, "om", [128, 3, FRAMES + 1])
            a2, b2_, a1, b1_ = (sb(ctx, n, [128, 3, FRAMES]) for n in ("a2", "b2_", "a1", "b1_"))
            pp = sb(ctx, "pp", [128, 3, FRAMES + 1])
            qq = sb(ctx, "qq", [128, 3, FRAMES + 1])
            z = sb(ctx, "z", [128, 3, FRAMES])
            xrow = sb(ctx, "xrow", [ROWS, 2, G, ROWLEN])
            x2t = sb(ctx, "x2t", [128, 3, FRAMES])
            rh = sb(ctx, "rh", [128, 3, FRAMES])
            score = sb(ctx, "score", [ROWS, G, E])
            top8 = sb(ctx, "top8", [ROWS, G, E])
            idx8 = sb(ctx, "idx8", [ROWS, G, E], U32)
            idxf = sb(ctx, "idxf", [ROWS, G, 2])
            hot = sb(ctx, "hot", [ROWS, 2, G, E])
            mask = sb(ctx, "mask", [ROWS, G, E])
            cum = sb(ctx, "cum", [ROWS, G + 1, E])
            tmp = sb(ctx, "tmp", [ROWS, 4, G])
            where = sb(ctx, "where", [ROWS, G, E])
            pick = sb(ctx, "pick", [ROWS, G, E])
            posf = sb(ctx, "posf", [ROWS, 2, G])
            posu = sb(ctx, "posu", [ROWS, 2, G], U32)
            tok_id = sb(ctx, "tok_id", [ROWS, G])
            cnt = sb(ctx, "cnt", [128, E])
            fposf = sb(ctx, "fposf", [128, E])
            fposu = sb(ctx, "fposu", [128, E], U32)
            gt = sb(ctx, "gt", [1, E, 64])
            nt = sb(ctx, "nt", [1, 4, E])
            def scratch(buf, n, inner):
                return buf[0:1, :, :].rearrange("p a b -> p (a b)")[:, 0:n * inner].rearrange("p (n i) -> p n i", i=inner)

            past, past2 = scratch(a2, BLOCKS, E), scratch(b2_, BLOCKS, E)
            tabf = scratch(a1, 4, BLOCKS)

            MIX = {"v": 0, "k": 1, "r": 2}
            MU = {"v": 0, "k": 2, "r": 4}
            DECAY, FIRST, BR1 = 6, 8, 10

            def blockcols(t, col):
                return t[:, col:col + 1], t[:, col + 1:col + 2]

            LOADS = [(ident[:, :], consts[:, 0:128]), (before_s[:, :], consts[0:ROWS, 128:128 + ROWS]),
                     (ones_s[:, :], consts[0:ROWS, 256:384]), (lane_s[:, :], consts[:, 384:388]),
                     (eidx_s[:, :], consts[:, 388:396]), (ebase_s[:, :], consts[:, 396:404]),
                     (wide_s[:, :], consts[0:1, 404:404 + 64 + BLOCKS]),
                     (tok_id[:, :], consts[0:ROWS, 604:604 + G]), (fill_s[:, :], consts[:, 612:612 + ROWLEN]),
                     (dft_s[:, :], dft), (mel_s[:, :], mel), (dct_s[:, :], dct), (wproj_s[:, :], w_proj),
                     (proj_s[MELS:MELS + 1, :], b_proj), (chan_s[:, :], chan),
                     (w4_s[:, :, :, :], w4), (wo_s[:, :, :], wo), (wr2_s[:, :, :], wr2), (br2_s[:, :], br2)]
            LOADED = 16 * len(LOADS)

            def each_two_pairs(eng, work):
                work(1)
                with eng.Fori(1, (PAIRS - 2) // 2) as n:
                    work(2 * n + 1)

            with nc.Block() as block:
                @block.sync
                def _(sp):
                    def load_frames(p):
                        after(sp, tok_pe, "frames1", p - 1)
                        sp.dma_start(fr[:, :, :], frames_v[:, bass.ds(p * G, G), 0:FRAME]).then_inc(frames_in, 16)

                    def store_rows(p):
                        wait(sp, rows_out, 16 * p)
                        sp.wait_ge(att_vec.sem, att_vec.at("h3", p))
                        sp.dma_start(out_v[:, bass.ds(p * G, G), :], h[:, p % 3, :, :] if isinstance(p, int)
                                     else h[:, bass.ds(p % 3, 1), :, :].rearrange("q o g c -> q (o g) c")
                                     ).then_inc(rows_out, 16)

                    load_frames(0)
                    for dst, src in LOADS:
                        sp.dma_start(dst, src).then_inc(weights_in, 16)
                    load_frames(1)
                    load_frames(2)
                    store_rows(0)
                    load_frames(3)
                    with sp.Fori(1, PAIRS - 3) as i:
                        store_rows(i)
                        load_frames(i + 3)
                    for p in range(PAIRS - 3, PAIRS):
                        store_rows(p)
                    sp.wait_ge(rows_out, 16 * PAIRS)

                @block.tensor
                def _(pe):
                    def stage_t(p):
                        pe.wait_ge(frames_in, 16 * (p + 1))
                        before(pe, att_act, p - 2)
                        for s in range(2):
                            for t in range(TILES):
                                mm = pe.transpose(ps[0:FRAME, 6 + s, t * ROWS:(t + 1) * ROWS],
                                                  fr[:, s * TILES + t, :], ident[0:ROWS, 0:ROWS])
                            mm.then_inc(tok_pe.sem, 1)
                        after(pe, mix_act, "k", p - 1)
                        for s in range(2):
                            after(pe, tok_act, f"frames{s}", p)
                            pe.matmul(ps[0:2 * BINS, 3 + s, 0:FRAMES], dft_s[:, :], ft[:, s, :],
                                      start=True, stop=True).then_inc(tok_pe.sem, 1)
                        for s in range(2):
                            after(pe, tok_act, f"pow{s}", p)
                            pe.matmul(ps[0:MELS, 6 + s, 0:FRAMES], mel_s[:, :], pw[:, s, :],
                                      start=True, stop=True).then_inc(tok_pe.sem, 1)
                        after(pe, mix_act, "r", p - 1)
                        for n, b in enumerate((0, 1, 2, 5)):
                            after(pe, tok_act, f"log{n // 2}", p)
                            for g in (2 * n, 2 * n + 1):
                                t = g % TILES
                                mm = pe.matmul(ps[0:ROWS, b, (g % 2) * C:(g % 2 + 1) * C],
                                               le[0:MELS + 1, n // 2, t * ROWS:(t + 1) * ROWS],
                                               proj_s[:, :], start=True, stop=True)
                            mm.then_inc(tok_pe.sem, 1)
                        pe.wait_ge(tok_vec.sem, tok_vec.at("tails", p))
                        transposes(xn, tails1, tok_pe)

                    def transposes(src, tails, steps):
                        for n, b in enumerate((3, 4, 6)):
                            for t in range(TILES):
                                piece = src[:, n * TILES + t, 0:CA] if n < 2 else tails[:, t, :, :]
                                mm = pe.transpose(ps[:, b, t * ROWS:(t + 1) * ROWS], piece, ident[0:ROWS, 0:ROWS])
                            mm.then_inc(steps.sem, 1)

                    def project(w, src, banks):
                        mms = []
                        for n, b in enumerate(banks):
                            parts = ((0, n), (1 + n, 2)) if n < 2 else ((3, 0), (4, 1), (5, 2))
                            for k, (piece, blk) in enumerate(parts):
                                mm = pe.matmul(ps[:, b, 0:FRAMES], w4_s[:, w, piece, :], src[:, blk, :],
                                               start=(k == 0), stop=(k == len(parts) - 1))
                            mms.append(mm)
                        return mms

                    def stage_k(p):
                        after(pe, tok_act, "h3", p)
                        before(pe, att_act, p - 1)
                        before(pe, rt_vec, p - 1)
                        after(pe, mix_vec, "v", p)
                        project(0, mixed[0], (0, 1, 2))[-1].then_inc(mix_pe.sem, 1)
                        after(pe, tok_act, "xt2", p)
                        after(pe, mix_vec, "k", p)
                        project(1, mixed[1], (3, 4, 5))[-1].then_inc(mix_pe.sem, 1)
                        after(pe, mix_act, "v", p)
                        after(pe, mix_vec, "r", p)
                        project(2, mixed[2], (0, 1, 2))[-1].then_inc(mix_pe.sem, 1)

                    def stage_w(p):
                        after(pe, wkv_vec, "z", p)
                        if not isinstance(p, int) or p + 2 < PAIRS:
                            after(pe, tok_act, "h3", p + 2)
                        else:
                            after(pe, mix_act, "r", PAIRS - 1)
                            after(pe, att_act, "rh2", p - 1)
                            after(pe, rt_vec, "pos", p - 1)
                        for n, b in enumerate((0, 1, 2, 5)):
                            for g in (2 * n, 2 * n + 1):
                                s, t = divmod(g, TILES)
                                dst = ps[0:ROWS, b, (g % 2) * C:(g % 2 + 1) * C]
                                pe.matmul(dst, z[:, s, t * ROWS:(t + 1) * ROWS], wo_s[:, 0, :], start=True, stop=False)
                                mm = pe.matmul(dst, z[:, 2, t * ROWS:(t + 1) * ROWS], wo_s[:, 1 + s, :],
                                               start=False, stop=True)
                            mm.then_inc(att_pe.sem, 1)
                        if not isinstance(p, int) or p + 2 < PAIRS:
                            after(pe, tok_act, "xt2", p + 2)
                        after(pe, att_vec, "tails", p)
                        transposes(xrow[:, 0, :, :], tails2, att_pe)
                        after(pe, att_act, "xt2", p)
                        for mm in project(3, x2t, (7, 0, 1)):
                            mm.then_inc(att_pe.sem, 1)
                        after(pe, att_act, "rh2", p)
                        for g in range(G):
                            s, t = divmod(g, TILES)
                            dst = ps[0:ROWS, 2, g * E:(g + 1) * E]
                            pe.matmul(dst, rh[:, s, t * ROWS:(t + 1) * ROWS], wr2_s[:, 0, :], start=True, stop=False)
                            mm = pe.matmul(dst, rh[:, 2, t * ROWS:(t + 1) * ROWS], wr2_s[:, 1 + s, :],
                                           start=False, stop=True)
                        mm.then_inc(att_pe.sem, 1)
                        after(pe, rt_vec, "c8", p)
                        dst = ps[0:ROWS, 5, 0:G * E]
                        pe.matmul(dst, before_s[:, :], mask[:, :, :], start=True, stop=False)
                        pe.matmul(dst, ones_s[:, 0:ROWS], cum[:, 0:G, :], start=False, stop=True).then_inc(att_pe.sem, 1)

                    pe.wait_ge(weights_in, LOADED)
                    pe.matmul(ps[0:MELS, 0, 0:C], dct_s[:, :], wproj_s[:, :], start=True, stop=True).then_inc(g_prod, 1)
                    pe.wait_ge(g_set, 1)
                    pe.wait_ge(consts_set, CONSTS)
                    stage_t(0)
                    stage_k(0)
                    stage_t(1)
                    def both(i):
                        for j in range(2):
                            stage_k(i + j)
                            stage_t(i + j + 1)
                            stage_w(i + j - 1)

                    each_two_pairs(pe, both)
                    stage_k(PAIRS - 1)
                    stage_w(PAIRS - 2)
                    stage_w(PAIRS - 1)
                    pe.wait_ge(rt_vec.sem, rt_vec.all(PAIRS))
                    pe.matmul(ps[:, 0, 0:E], ones_s[:, :], cum[:, G, :], start=True, stop=True).then_inc(counted, 1)

                @block.scalar
                def _(act):
                    def stage_t(p):
                        for s in range(2):
                            after(act, tok_pe, f"frames{s}", p)
                            act.activation(ft[:, s, :], ps[0:FRAME, 6 + s, 0:FRAMES], ACT.Copy).then_inc(tok_act.sem, 1)
                        for s in range(2):
                            after(act, tok_pe, f"dft{s}", p)
                            act.activation(pw[:, s, :], ps[0:2 * BINS, 3 + s, 0:FRAMES], ACT.Square).then_inc(tok_act.sem, 1)
                        for s in range(2):
                            after(act, tok_pe, f"mel{s}", p)
                            act.activation(le[0:MELS, s, :], ps[0:MELS, 6 + s, 0:FRAMES], ACT.Ln,
                                           bias=eps_s[0:MELS, 0:1]).then_inc(tok_act.sem, 1)
                        before(act, att_vec, p - 2)
                        wait(act, rows_out, 16 * (p - 2))
                        for n, b in enumerate((0, 1, 2, 5)):
                            after(act, tok_pe, f"h{n}", p)
                            dst = h[:, p % 3, 2 * n:2 * n + 2, :] if isinstance(p, int) else \
                                h[:, bass.ds(p % 3, 1), 2 * n:2 * n + 2, :].rearrange("q o g c -> q (o g) c")
                            act.activation(dst, ps[0:ROWS, b, 0:2 * C].rearrange("q (g c) -> q g c", g=2),
                                           ACT.Copy).then_inc(tok_act.sem, 1)
                        rsqrt_seed(tok_vec, tok_act, nw1, p)
                        for n, b in enumerate((3, 4, 6)):
                            after(act, tok_pe, f"xt{n}", p)
                            if n == 0:
                                after(act, mix_vec, "r", p - 1)
                            act.activation(xt[:, n, 1:FRAMES + 1], ps[:, b, 0:FRAMES], ACT.Copy).then_inc(tok_act.sem, 1)

                    def rsqrt_seed(vec, steps, nw, p):
                        after(act, vec, "var", p)
                        act.activation(nw[:, 1, :], nw[:, 0, :], ACT.Ln).then_inc(steps.sem, 1)
                        after(act, steps, "lnv", p)
                        act.activation(nw[:, 2, :], nw[:, 1, :], ACT.Exp, scale=-0.5).then_inc(steps.sem, 1)

                    def values(p, par):
                        before(act, wkv_vec, p - 1)
                        after(act, mix_pe, "v", p)
                        act.activation(vs[par][:, :, :], ps[:, 0:3, 0:FRAMES], ACT.Copy).then_inc(mix_act.sem, 1)

                    def keys(p, par):
                        after(act, mix_pe, "k", p)
                        act.activation(ks[par][:, :, :], ps[:, 3:6, 0:FRAMES], ACT.Copy).then_inc(mix_act.sem, 1)

                    def gates(p):
                        after(act, wkv_pool, "sn", p - 1)
                        after(act, mix_pe, "r", p)
                        act.activation(sig[:, :, :], ps[:, 0:3, 0:FRAMES], ACT.Sigmoid).then_inc(mix_act.sem, 1)

                    def update_factors(p):
                        after(act, wkv_vec, "clampA", p)
                        act.activation(a2[:, :, :], a2[:, :, :], ACT.Exp).then_inc(wkv_act.sem, 1)
                        after(act, wkv_vec, "clampB", p)
                        act.activation(b2_[:, :, :], b2_[:, :, :], ACT.Exp, scale=-1.0).then_inc(wkv_act.sem, 1)

                    def output_factors(p):
                        after(act, wkv_vec, "clampC", p)
                        act.activation(a1[:, :, :], a1[:, :, :], ACT.Exp).then_inc(wkv_act.sem, 1)
                        after(act, wkv_vec, "clampD", p)
                        act.activation(b1_[:, :, :], b1_[:, :, :], ACT.Exp, scale=-1.0).then_inc(wkv_act.sem, 1)

                    def reciprocal_seed(p):
                        after(act, wkv_vec, "den", p)
                        act.activation(b2_[:, :, :], a1[:, :, :], ACT.Ln).then_inc(wkv_act.sem, 1)
                        after(act, wkv_act, "lnden", p)
                        act.activation(b2_[:, :, :], b2_[:, :, :], ACT.Exp, scale=-1.0).then_inc(wkv_act.sem, 1)

                    def stage_w(p):
                        rsqrt_seed(att_vec, att_act, nw2, p)
                        for n, b in enumerate((3, 4, 6)):
                            after(act, att_pe, f"xt{n}", p)
                            act.activation(x2t[:, n, :], ps[:, b, 0:FRAMES], ACT.Copy).then_inc(att_act.sem, 1)
                        act.activation(xrow[:, 1, :, 0:C], xrow[:, 0, :, 0:C], ACT.Copy).then_inc(att_act.sem, 1)
                        for n, b in enumerate((7, 0, 1)):
                            after(act, att_pe, f"rh{n}", p)
                            act.activation(rh[:, n, :], ps[:, b, 0:FRAMES], ACT.Relu,
                                           bias=blockcols(chan_s, BR1)[n // 2]).then_inc(att_act.sem, 1)
                        after(act, rt_vec, "gap", p)
                        act.activation(tmp[:, 1, :], tmp[:, 0, :], ACT.Exp).then_inc(att_act.sem, 1)

                    act.wait_ge(g_prod, 1)
                    act.activation(proj_s[0:MELS, :], ps[0:MELS, 0, 0:C], ACT.Copy).then_inc(g_set, 1)
                    act.wait_ge(consts_set, CONSTS)
                    stage_t(0)
                    values(0, 0)
                    keys(0, 0)
                    gates(0)
                    stage_t(1)
                    def both(i):
                        for j in range(2):
                            p = i + j
                            update_factors(p - 1)
                            values(p, (1 + j) % 2)
                            output_factors(p - 1)
                            keys(p, (1 + j) % 2)
                            reciprocal_seed(p - 1)
                            gates(p)
                            stage_t(p + 1)
                            stage_w(p - 1)

                    each_two_pairs(act, both)
                    last = PAIRS - 1
                    update_factors(last - 1)
                    values(last, last % 2)
                    output_factors(last - 1)
                    keys(last, last % 2)
                    reciprocal_seed(last - 1)
                    gates(last)
                    stage_w(last - 1)
                    update_factors(last)
                    output_factors(last)
                    reciprocal_seed(last)
                    stage_w(last)

                @block.gpsimd
                def _(pool):
                    def wkv(p, par):
                        after(pool, wkv_act, "b2", p)
                        after(pool, wkv_vec, "q_scan", p)
                        pool.tensor_tensor(b2_[:, :, :], b2_[:, :, :], vs[par][:, :, :], ALU.mult).then_inc(wkv_pool.sem, 1)
                        after(pool, wkv_vec, "p_scan", p)
                        after(pool, wkv_act, "a", p)
                        pool.tensor_tensor(a2[:, :, :], a1[:, :, :], pp[:, :, 0:FRAMES], ALU.mult).then_inc(wkv_pool.sem, 1)
                        after(pool, wkv_vec, "den", p)
                        pool.tensor_tensor(b1_[:, :, :], b1_[:, :, :], vs[par][:, :, :], ALU.mult).then_inc(wkv_pool.sem, 1)
                        after(pool, wkv_vec, "num", p)
                        after(pool, mix_act, "r", p)
                        pool.tensor_tensor(b1_[:, :, :], a2[:, :, :], sig[:, :, :], ALU.mult).then_inc(wkv_pool.sem, 1)

                    def scatter(p):
                        pool.wait_ge(rt_vec.sem, rt_vec.at("posu", p))
                        pool.wait_ge(att_act.sem, att_act.at("copy", p))
                        alone(pool)
                        for k in range(2):
                            for g in range(G):
                                pool.indirect_dma_start(
                                    out=slots, out_offset=bass.IndirectOffsetOnAxis(posu[:, k, g:g + 1], 0),
                                    in_=xrow[:, k, g, :], in_offset=None, bounds_check=SPARE + 127,
                                    oob_is_err=True, compute_op=ALU.bypass).then_inc(scattered, 16)

                    wkv(0, 0)
                    def both(i):
                        for j in range(2):
                            scatter(i + j - 1)
                            wkv(i + j, (1 + j) % 2)

                    each_two_pairs(pool, both)
                    scatter(PAIRS - 2)
                    wkv(PAIRS - 1, (PAIRS - 1) % 2)
                    scatter(PAIRS - 1)
                    pool.wait_ge(fill_pos, 2)
                    for e in range(E):
                        pool.indirect_dma_start(
                            out=slots, out_offset=bass.IndirectOffsetOnAxis(fposu[:, e:e + 1], 0),
                            in_=fill_s[:, :], in_offset=None, bounds_check=SPARE + 127,
                            oob_is_err=True, compute_op=ALU.bypass).then_inc(filled, 16)
                    pool.dma_start(slots[SPARE:SPARE + 128, :], fill_s[:, :]).then_inc(filled, 16)
                    pool.wait_ge(filled, 16 * (E + 1))
                    pool.wait_ge(scattered, 16 * 2 * G * PAIRS)

                @block.vector
                def _(dve):
                    def norm_stats(src, st, mv, nw, steps, act_steps, p):
                        alone(dve)
                        for g in range(G):
                            mm = dve.bn_stats(st[:, g, :], src(g))
                        mm.then_inc(steps.sem, 1)
                        after(dve, steps, "stats", p)
                        alone(dve)
                        for g in range(G):
                            mm = dve.bn_aggr(mv[:, g, :], st[:, g, :])
                        mm.then_inc(steps.sem, 1)
                        after(dve, steps, "aggr", p)
                        dve.tensor_scalar(nw[:, 0, :], mv[:, :, 1], EPS, None, ALU.add).then_inc(steps.sem, 1)
                        after(dve, act_steps, "rstd", p)
                        dve.tensor_tensor(nw[:, 3, :], nw[:, 0, :], nw[:, 2, :], ALU.mult).then_inc(steps.sem, 1)
                        after(dve, steps, "n1", p)
                        dve.tensor_tensor(nw[:, 3, :], nw[:, 3, :], nw[:, 2, :], ALU.mult).then_inc(steps.sem, 1)
                        after(dve, steps, "n2", p)
                        dve.tensor_scalar(nw[:, 3, :], nw[:, 3, :], -0.5, 1.5, ALU.mult, ALU.add).then_inc(steps.sem, 1)
                        after(dve, steps, "n3", p)
                        dve.tensor_tensor(nw[:, 4, :], nw[:, 3, :], nw[:, 2, :], ALU.mult).then_inc(steps.sem, 1)
                        after(dve, steps, "rstd", p)

                    def hrow(p, g, n=1):
                        if isinstance(p, int):
                            return h[:, p % 3, g, :] if n == 1 else h[:, p % 3, g:g + n, :]
                        v = h[:, bass.ds(p % 3, 1), g:g + n, :]
                        return v.rearrange("q o g c -> q (o g c)") if n == 1 else v.rearrange("q o g c -> q (o g) c")

                    def stage_t(p):
                        after(dve, tok_act, "h3", p)
                        norm_stats(lambda g: hrow(p, g), st1, mv1, nw1, tok_vec, tok_act, p)
                        for g in range(G):
                            mm = dve.tensor_scalar(xn[:, g, :], hrow(p, g), mv1[:, g, 0:1], nw1[:, 4, g:g + 1],
                                                   ALU.subtract, ALU.mult)
                        mm.then_inc(tok_vec.sem, 1)
                        after(dve, tok_vec, "norm", p)
                        gather_tails(tails1, xn, tok_vec)

                    def gather_tails(tails, src, steps):
                        dve.tensor_copy(tails[:, :, :, :].rearrange("q t s c -> q s t c"),
                                        src[:, :, CA:C].rearrange("q (s t) c -> q s t c", s=2)).then_inc(steps.sem, 1)

                    def stage_k(p):
                        after(dve, tok_act, "xt2", p)
                        dve.tensor_tensor(diff[:, :, :], xt[:, :, 1:], xt[:, :, 0:FRAMES], ALU.subtract).then_inc(mix_vec.sem, 1)
                        after(dve, mix_vec, "diff", p)
                        after(dve, mix_pe, "r", p - 1)
                        for name in ("v", "k", "r"):
                            m, (mu_a, mu_b) = mixed[MIX[name]], blockcols(chan_s, MU[name])
                            dve.scalar_tensor_tensor(m[:, 0:2, :], diff[:, 0:2, :], mu_a, xt[:, 0:2, 0:FRAMES],
                                                     ALU.mult, ALU.add)
                            dve.scalar_tensor_tensor(m[:, 2, :], diff[:, 2, :], mu_b, xt[:, 2, 0:FRAMES],
                                                     ALU.mult, ALU.add).then_inc(mix_vec.sem, 1)

                    def wkv(p, par):
                        k = ks[par]
                        w, negu = blockcols(chan_s, DECAY), blockcols(negu_s, 0)
                        after(dve, mix_act, "k", p)
                        for n in range(3):
                            mm = dve.tensor_tensor_scan(om[:, n, 1:], w[n // 2].to_broadcast([128, FRAMES]), k[:, n, :],
                                                        NEG, ALU.add, ALU.max)
                        mm.then_inc(wkv_vec.sem, 1)
                        after(dve, wkv_vec, "max", p)
                        before(dve, att_pe, p)
                        dve.tensor_tensor(z[:, :, :], om[:, :, 0:FRAMES], k[:, :, :], ALU.subtract).then_inc(wkv_vec.sem, 1)
                        after(dve, wkv_vec, "lead", p)
                        for buf, add, op in ((a2, w, ALU.min), (b2_, w, ALU.max), (a1, negu, ALU.min), (b1_, negu, ALU.max)):
                            dve.tensor_scalar(buf[:, 0:2, :], z[:, 0:2, :], add[0], 0.0, ALU.add, op)
                            dve.tensor_scalar(buf[:, 2, :], z[:, 2, :], add[1], 0.0, ALU.add, op).then_inc(wkv_vec.sem, 1)
                        after(dve, wkv_act, "b2", p)
                        for n in range(3):
                            mm = dve.tensor_tensor_scan(qq[:, n, 1:], a2[:, n, :], b2_[:, n, :], 0.0, ALU.mult, ALU.add)
                        mm.then_inc(wkv_vec.sem, 1)
                        after(dve, wkv_pool, "b2v", p)
                        for n in range(3):
                            mm = dve.tensor_tensor_scan(pp[:, n, 1:], a2[:, n, :], b2_[:, n, :], 0.0, ALU.mult, ALU.add)
                        mm.then_inc(wkv_vec.sem, 1)
                        after(dve, wkv_act, "b", p)
                        after(dve, wkv_vec, "p_scan", p)
                        dve.tensor_tensor(b2_[:, :, :], a1[:, :, :], qq[:, :, 0:FRAMES], ALU.mult).then_inc(wkv_vec.sem, 1)
                        after(dve, wkv_vec, "aq", p)
                        after(dve, wkv_pool, "ap", p)
                        dve.tensor_tensor(a1[:, :, :], b2_[:, :, :], b1_[:, :, :], ALU.add).then_inc(wkv_vec.sem, 1)
                        after(dve, wkv_pool, "bv", p)
                        dve.tensor_tensor(a2[:, :, :], a2[:, :, :], b1_[:, :, :], ALU.add).then_inc(wkv_vec.sem, 1)
                        after(dve, wkv_act, "rden", p)
                        dve.tensor_tensor(z[:, :, :], a1[:, :, :], b2_[:, :, :], ALU.mult).then_inc(wkv_vec.sem, 1)
                        after(dve, wkv_vec, "newton1", p)
                        dve.scalar_tensor_tensor(z[:, :, :], z[:, :, :], 2.0, b2_[:, :, :], ALU.subtract, ALU.mult).then_inc(wkv_vec.sem, 1)
                        after(dve, wkv_vec, "newton2", p)
                        after(dve, wkv_pool, "sn", p)
                        dve.scalar_tensor_tensor(z[:, :, :], z[:, :, :], -1.0, b1_[:, :, :], ALU.mult, ALU.mult).then_inc(wkv_vec.sem, 1)
                    def stage_w(p):
                        for n, b in enumerate((0, 1, 2, 5)):
                            after(dve, att_pe, f"o{n}", p)
                            dve.tensor_tensor(hrow(p, 2 * n, 2), ps[0:ROWS, b, 0:2 * C].rearrange("q (g c) -> q g c", g=2),
                                              hrow(p, 2 * n, 2), ALU.add).then_inc(att_vec.sem, 1)
                        after(dve, att_vec, "h3", p)
                        norm_stats(lambda g: hrow(p, g), st2, mv2, nw2, att_vec, att_act, p)
                        wait(dve, scattered, 16 * 2 * G * p)
                        for g in range(G):
                            mm = dve.tensor_scalar(xrow[:, 0, g, 0:C], hrow(p, g), mv2[:, g, 0:1], nw2[:, 4, g:g + 1],
                                                   ALU.subtract, ALU.mult)
                        mm.then_inc(att_vec.sem, 1)
                        after(dve, att_vec, "norm", p)
                        gather_tails(tails2, xrow[:, 0, :, :], att_vec)

                    def route(p):
                        def done(name):
                            after(dve, rt_vec, name, p)

                        after(dve, att_pe, "score", p)
                        dve.tensor_tensor(score[:, :, :], ps[0:ROWS, 2, 0:G * E].rearrange("q (g e) -> q g e", g=G),
                                          br2_s[:, :].unsqueeze(1).to_broadcast([ROWS, G, E]), ALU.add).then_inc(rt_vec.sem, 1)
                        done("score")
                        alone(dve)
                        for g in range(G):
                            mm = dve.max(top8[:, g, :], score[:, g, :])
                        mm.then_inc(rt_vec.sem, 1)
                        done("top")
                        alone(dve)
                        for g in range(G):
                            mm = dve.max_index(idx8[:, g, :], top8[:, g, :], score[:, g, :])
                        mm.then_inc(rt_vec.sem, 1)
                        done("index")
                        dve.tensor_copy(idxf[:, :, :], idx8[:, :, 0:2]).then_inc(rt_vec.sem, 1)
                        done("indexf")
                        for k in range(2):
                            mm = dve.tensor_tensor(hot[:, k, :, :], eidx_s[0:ROWS, :].unsqueeze(1).to_broadcast([ROWS, G, E]),
                                                   idxf[:, :, k:k + 1].to_broadcast([ROWS, G, E]), ALU.is_equal)
                        mm.then_inc(rt_vec.sem, 1)
                        done("hot")
                        dve.tensor_tensor(mask[:, :, :], hot[:, 0, :, :], hot[:, 1, :, :], ALU.add).then_inc(rt_vec.sem, 1)
                        done("mask")
                        for g in range(G):
                            dve.tensor_tensor(cum[:, g + 1, :], cum[:, g, :], mask[:, g, :], ALU.add).then_inc(rt_vec.sem, 1)
                            done(f"c{g + 1}")
                        dve.tensor_tensor(tmp[:, 0, :], top8[:, :, 1], top8[:, :, 0], ALU.subtract).then_inc(rt_vec.sem, 1)
                        after(dve, att_act, "ex", p)
                        dve.tensor_scalar(tmp[:, 2, :], tmp[:, 1, :], 1.0, None, ALU.add).then_inc(rt_vec.sem, 1)
                        done("sum")
                        dve.reciprocal(tmp[:, 3, :], tmp[:, 2, :]).then_inc(rt_vec.sem, 1)
                        done("rec")
                        dve.tensor_copy(xrow[:, 0, :, WEIGHT], tmp[:, 3, :]).then_inc(rt_vec.sem, 1)
                        dve.tensor_tensor(xrow[:, 1, :, WEIGHT], tmp[:, 1, :], tmp[:, 3, :], ALU.mult).then_inc(rt_vec.sem, 1)
                        for k in range(2):
                            dve.tensor_copy(xrow[:, k, :, TOKEN], tok_id[:, :])
                        dve.tensor_scalar(tok_id[:, :], tok_id[:, :], float(G * ROWS), None, ALU.add).then_inc(rt_vec.sem, 1)
                        after(dve, att_pe, "rank", p)
                        dve.tensor_copy(cum[:, 0, :], cum[:, G, :]).then_inc(rt_vec.sem, 1)
                        dve.tensor_tensor(where[:, :, :], ps[0:ROWS, 5, 0:G * E].rearrange("q (g e) -> q g e", g=G),
                                          ebase_s[0:ROWS, :].unsqueeze(1).to_broadcast([ROWS, G, E]), ALU.add).then_inc(rt_vec.sem, 1)
                        for k in range(2):
                            done("pos" if k == 0 else "pos0")
                            dve.tensor_tensor(pick[:, :, :], hot[:, k, :, :], where[:, :, :], ALU.mult).then_inc(rt_vec.sem, 1)
                            done(f"pick{k}")
                            dve.tensor_reduce(posf[:, k, :], pick[:, :, :], AX.X, ALU.add).then_inc(rt_vec.sem, 1)
                        done("pos1")
                        dve.tensor_copy(posu[:, :, :], posf[:, :, :]).then_inc(rt_vec.sem, 1)

                    dve.memset(le[32:64, :, :], 1.0).then_inc(consts_set, 1)
                    dve.memset(xt[:, :, 0:1], 0.0).then_inc(consts_set, 1)
                    dve.memset(om[:, :, 0:1], NEG).then_inc(consts_set, 1)
                    dve.memset(pp[:, :, 0:1], 0.0).then_inc(consts_set, 1)
                    dve.memset(qq[:, :, 0:1], 0.0).then_inc(consts_set, 1)
                    dve.memset(cum[:, 0, :], 0.0).then_inc(consts_set, 1)
                    dve.memset(eps_s[:, 0:1], 1e-6).then_inc(consts_set, 1)
                    dve.memset(xrow[:, 0, :, C:ROWLEN], 1.0).then_inc(consts_set, 1)
                    dve.memset(xrow[:, 1, :, C:ROWLEN], 1.0).then_inc(consts_set, 1)
                    dve.memset(eps_s[:, 1:2], EPS).then_inc(consts_set, 1)
                    dve.wait_ge(weights_in, LOADED)
                    dve.tensor_scalar(negu_s[:, :], chan_s[:, FIRST:FIRST + 2], -1.0, None, ALU.mult).then_inc(consts_set, 1)
                    dve.memset(gt[:, :, :], 0.0).then_inc(consts_set, 1)
                    dve.wait_ge(consts_set, CONSTS)

                    stage_t(0)
                    stage_k(0)
                    stage_t(1)
                    def both(i):
                        for j in range(2):
                            p = i + j
                            stage_k(p)
                            wkv(p - 1, j % 2)
                            stage_t(p + 1)
                            stage_w(p - 1)
                            route(p - 1)

                    each_two_pairs(dve, both)
                    stage_k(PAIRS - 1)
                    wkv(PAIRS - 2, 0)
                    stage_w(PAIRS - 2)
                    route(PAIRS - 2)
                    wkv(PAIRS - 1, 1)
                    stage_w(PAIRS - 1)
                    route(PAIRS - 1)

                    n_step = [0]

                    def chain(ins):
                        n_step[0] += 1
                        ins.then_inc(tables, 1)
                        dve.wait_ge(tables, n_step[0])

                    dve.wait_ge(counted, 1)
                    dve.tensor_tensor(cnt[:, :], ps[:, 0, 0:E], ebase_s[:, :], ALU.add).then_inc(fill_pos, 1)
                    dve.wait_ge(fill_pos, 1)
                    chain(dve.tensor_scalar(fposf[:, :], cnt[:, :], lane_s[:, 0:1], None, ALU.add))
                    dve.tensor_copy(fposu[:, :], fposf[:, :]).then_inc(fill_pos, 1)
                    chain(dve.tensor_copy(nt[:, 0, :], ps[0:1, 0, 0:E]))
                    chain(dve.tensor_tensor(gt[:, :, 0:63], nt[:, 0, :].unsqueeze(2).to_broadcast([1, E, 63]),
                                            wide_s[:, 0:63].unsqueeze(1).to_broadcast([1, E, 63]), ALU.is_gt))
                    chain(dve.tensor_reduce(nt[:, 1, :], gt[:, :, :], AX.X, ALU.add))
                    chain(dve.tensor_tensor_scan(nt[:, 2, :], ones_s[0:1, 0:E], nt[:, 1, :], 0.0, ALU.mult, ALU.add))
                    chain(dve.tensor_scalar(nt[:, 3, :], nt[:, 1, :], -128.0, float(SLOTS), ALU.mult, ALU.add))
                    chain(dve.tensor_tensor(past[:, :, :], wide_s[:, 64:64 + BLOCKS].unsqueeze(2).to_broadcast([1, BLOCKS, E]),
                                            nt[:, 2, :].unsqueeze(1).to_broadcast([1, BLOCKS, E]), ALU.is_ge))
                    chain(dve.tensor_tensor(past2[:, :, :], past[:, :, :],
                                            nt[:, 3, :].unsqueeze(1).to_broadcast([1, BLOCKS, E]), ALU.mult))
                    chain(dve.tensor_reduce(tabf[:, 0, :], past[:, :, :], AX.X, ALU.add))
                    chain(dve.tensor_reduce(tabf[:, 1, :], past2[:, :, :], AX.X, ALU.add))
                    chain(dve.tensor_scalar(tabf[:, 0, :], tabf[:, 0, :], float(E - 1), None, ALU.min))
                    chain(dve.tensor_scalar(tabf[:, 2, :], wide_s[:, 64:64 + BLOCKS], 128.0, None, ALU.mult))
                    chain(dve.tensor_tensor(tabf[:, 3, :], tabf[:, 1, :], tabf[:, 2, :], ALU.add))
                    chain(dve.tensor_scalar(tabf[:, 3, :], tabf[:, 3, :], float(SPARE), None, ALU.min))
                    chain(dve.tensor_copy(expert_of[:, 0:BLOCKS], tabf[:, 0, :]))
                    chain(dve.tensor_copy(slot_of[:, 0:BLOCKS], tabf[:, 3, :]))

        with ExitStack() as ctx:
            w1a_s = sb(ctx, "w1a_s", [128, E, F])
            w1b_s = sb(ctx, "w1b_s", [CB + 1, E, F])
            w2_s = sb(ctx, "w2_s", [128, E, FC, C])
            b2_s = sb(ctx, "b2_s", [1, E, C])
            one_s = sb(ctx, "one_s", [1, 128])
            xb = [sb(ctx, f"xb{n}", [128, ROWLEN]) for n in range(4)]
            xbt = [sb(ctx, f"xbt{n}", [128, 256]) for n in range(2)]
            mid = sb(ctx, "mid", [128, F])
            midt = sb(ctx, "midt", [128, FC, 128])
            yb = [sb(ctx, f"yb{n}", [128, C]) for n in range(2)]
            ids = [sb(ctx, f"ids{n}", [128, 1], U32) for n in range(2)]

            experts_in = sem("experts_in")
            one_set = sem("one_set")
            block_in = [sem(f"block_in{n}") for n in range(4)]
            b_xt, b_mid, b_midt, b_y = sem("b_xt"), sem("b_mid"), sem("b_midt"), sem("b_y")
            e_xt, e_mid0, e_mid1, e_midt0, e_midt1, e_y = (sem(n) for n in ("e_xt", "e_mid0", "e_mid1", "e_midt0", "e_midt1", "e_y"))
            id_set, added = sem("id_set"), sem("added")
            XT, MID, MT, Y = 0, (1, 2), (3, 4), 5
            UN = 4
            assert BLOCKS % UN == 0

            def each_block(eng, work):
                for j in range(UN):
                    work(j, 0)
                with eng.Fori(1, BLOCKS // UN) as n:
                    for j in range(UN):
                        work(j, n)

            with nc.Block() as block:
                @block.sync
                def _(sp):
                    for e in range(E):
                        sp.dma_start(w1a_s[:, e, :], w1a[:, e, :]).then_inc(experts_in, 16)
                        sp.dma_start(w1b_s[:, e, :], w1b[:, e, :]).then_inc(experts_in, 16)
                        sp.dma_start(w2_s[:, e, :, :], w2[:, e, :, :]).then_inc(experts_in, 16)
                    sp.dma_start(b2_s[:, :, :], b2).then_inc(experts_in, 16)

                    def load(j, n):
                        i = n * UN + j
                        wait(sp, e_y, i - 3)
                        wait(sp, id_set, i - 3)
                        first = sp.value_load(slot_of[0:1, bass.ds(i, 1)], min_val=0, max_val=SPARE)
                        sp.dma_start(xb[j][:, :], slots[bass.ds(first, 128), :]).then_inc(block_in[j], 16)

                    each_block(sp, load)

                @block.scalar
                def _(act):
                    def half(j, n):
                        i = n * UN + j
                        act.wait_ge(b_xt, i + 1)
                        act.activation(xbt[j % 2][:, 0:128], ps[:, XT, 0:128], ACT.Copy)
                        act.activation(xbt[j % 2][0:CB + 1, 128:256], ps[0:CB + 1, XT, 128:256], ACT.Copy).then_inc(e_xt, 1)
                        act.wait_ge(b_mid, 2 * i + 1)
                        wait(act, b_midt, 2 * i)
                        act.activation(mid[:, 0:F // 2], ps[:, MID[0], 0:F // 2], ACT.Relu).then_inc(e_mid0, 1)
                        act.wait_ge(b_midt, 2 * i + 1)
                        wait(act, b_y, i)
                        act.activation(midt[:, 0:FC // 2, :], ps[:, MT[0], 0:F // 2].rearrange("p (c m) -> p c m", m=128),
                                       ACT.Copy).then_inc(e_midt0, 1)

                    each_block(act, half)

                @block.gpsimd
                def _(pool):
                    def add(j, n):
                        i = n * UN + j
                        pool.wait_ge(block_in[j], 16 * (n + 1))
                        alone(pool)
                        pool.tensor_copy(ids[j % 2][:, :], xb[j][:, TOKEN:TOKEN + 1]).then_inc(id_set, 1)
                        pool.wait_ge(e_y, i + 1)
                        pool.wait_ge(id_set, i + 1)
                        alone(pool)
                        pool.indirect_dma_start(
                            out=out, out_offset=bass.IndirectOffsetOnAxis(ids[j % 2][:, 0:1], 0), in_=yb[j % 2][:, :],
                            in_offset=None, bounds_check=TOKENS + 127, oob_is_err=True,
                            compute_op=ALU.add).then_inc(added, 16)
                        pool.wait_ge(added, 16 * (i + 1))

                    each_block(pool, add)

                @block.tensor
                def _(pe):
                    def turn_in(j, n):
                        i = n * UN + j
                        pe.wait_ge(block_in[j], 16 * (n + 1))
                        wait(pe, e_xt, i)
                        pe.transpose(ps[:, XT, 0:128], xb[j][:, 0:CA], ident[:, :])
                        pe.transpose(ps[0:CB + 1, XT, 128:256], xb[j][:, CA:C + 1], ident[:, :]).then_inc(b_xt, 1)

                    def up(j, i):
                        e = pe.value_load(expert_of[0:1, bass.ds(i, 1)], min_val=0, max_val=E - 1)
                        pe.wait_ge(e_xt, i + 1)
                        for n in range(2):
                            wait(pe, (e_mid0, e_mid1)[n], i)
                            dst, cols = ps[:, MID[n], 0:F // 2], slice(n * F // 2, (n + 1) * F // 2)
                            pe.matmul(dst, xbt[j % 2][:, 0:128], w1a_s[:, bass.ds(e, 1), cols], start=True, stop=False)
                            pe.matmul(dst, xbt[j % 2][0:CB + 1, 128:256], w1b_s[:, bass.ds(e, 1), cols],
                                      start=False, stop=True).then_inc(b_mid, 1)

                    def turn_mid(i):
                        for n in range(2):
                            pe.wait_ge((e_mid0, e_mid1)[n], i + 1)
                            wait(pe, (e_midt0, e_midt1)[n], i)
                            for c in range(FC // 2):
                                mm = pe.transpose(ps[:, MT[n], c * 128:(c + 1) * 128],
                                                  mid[:, (n * FC // 2 + c) * 128:(n * FC // 2 + c + 1) * 128], ident[:, :])
                            mm.then_inc(b_midt, 1)

                    def down(j, i):
                        e = pe.value_load(expert_of[0:1, bass.ds(i, 1)], min_val=0, max_val=E - 1)
                        wait(pe, e_y, i)
                        for c in range(FC):
                            if c % 3 == 0:
                                pe.wait_ge((e_midt0, e_midt1)[c // 3], i + 1)
                            pe.matmul(ps[:, Y, 0:C], midt[:, c, :], w2_s[:, bass.ds(e, 1), c, :], start=(c == 0), stop=False)
                        pe.matmul(ps[:, Y, 0:C], one_s[:, :], b2_s[:, bass.ds(e, 1), :], start=False, stop=True).then_inc(b_y, 1)

                    pe.wait_ge(experts_in, 16 * (3 * E + 1))
                    pe.wait_ge(one_set, 1)
                    turn_in(0, 0)
                    up(0, 0)
                    turn_in(1, 0)
                    turn_mid(0)
                    def four(n):
                        for j in range(1, 1 + UN):
                            i = n * UN + j
                            up(j, i)
                            down(j - 1, i - 1)
                            turn_in((j + 1) % UN, n + (j + 1) // UN)
                            turn_mid(i)

                    four(0)
                    with pe.Fori(1, BLOCKS // UN - 1) as n:
                        four(n)
                    for i in range(BLOCKS - 3, BLOCKS):
                        up(i, i)
                        down(i - 1, i - 1)
                        if i + 1 < BLOCKS:
                            turn_in((i + 1) % UN, (i + 1) // UN)
                        turn_mid(i)
                    down(BLOCKS - 1, BLOCKS - 1)

                @block.vector
                def _(dve):
                    dve.memset(one_s[:, :], 1.0).then_inc(one_set, 1)

                    def half(j, n):
                        i = n * UN + j
                        dve.wait_ge(b_mid, 2 * i + 2)
                        wait(dve, b_midt, 2 * i)
                        dve.tensor_scalar(mid[:, F // 2:F], ps[:, MID[1], 0:F // 2], 0.0, None, ALU.max).then_inc(e_mid1, 1)
                        dve.wait_ge(b_midt, 2 * i + 2)
                        wait(dve, b_y, i)
                        dve.tensor_copy(midt[:, FC // 2:FC, :], ps[:, MT[1], 0:F // 2].rearrange("p (c m) -> p c m", m=128)
                                        ).then_inc(e_midt1, 1)
                        dve.wait_ge(b_y, i + 1)
                        wait(dve, added, 16 * (i - 1))
                        dve.tensor_scalar(yb[j % 2][:, :], ps[:, Y, 0:C], xb[j][:, WEIGHT:WEIGHT + 1], None,
                                          ALU.mult).then_inc(e_y, 1)

                    each_block(dve, half)


def kernel(**inputs):
    import numpy as _np
    import concourse.bacc as _bacc
    from concourse import mybir as _mybir
    from concourse.bass_utils import run_bass_kernel_spmd as _run

    f = {k: _np.ascontiguousarray(v) for k, v in inputs.items()}
    arrays = {"x": f["x"]}

    j = _np.arange(FRAME)
    window = 0.54 - 0.46 * _np.cos(2 * _np.pi * j / (FRAME - 1))
    turn = _np.outer(j, _np.arange(BINS)) % FRAME * (2 * _np.pi / FRAME)
    cs, sn = _np.cos(turn), _np.sin(turn)
    sn[:, 0] = 0.0
    sn[:, BINS - 1] = 0.0
    arrays["dft"] = (_np.concatenate([cs, sn], 1) * window[:, None]).astype(_np.float32)
    arrays["mel"] = _np.concatenate([f["L0_tok_mel_filters"].T] * 2, 0)
    arrays["dct"] = f["L0_tok_dct"]
    arrays["w_proj"] = f["L0_tok_w_proj"]
    arrays["b_proj"] = f["L0_tok_b_proj"].reshape(1, C)

    def two(v):
        v = v.reshape(C)
        return [v[:CA], _np.concatenate([v[CA:], v[CA:]])]

    arrays["chan"] = _np.stack(two(f["L0_attn_time_mix_v"]) + two(f["L0_attn_time_mix_k"]) + two(f["L0_attn_time_mix_r"])
                               + two(f["L0_attn_time_decay"]) + two(f["L0_attn_time_first"]) + two(f["L0_ffn_br1"]), 1)

    def stationary(w):
        t, p = w.T, _np.zeros((6, 128, 128), _np.float32)
        p[0] = t[:CA, :CA]
        p[1, :CB], p[2, CB:] = t[CA:, :CA], t[CA:, :CA]
        p[3, :, :CB], p[4, :, CB:] = t[:CA, CA:], t[:CA, CA:]
        p[5, :CB, :CB], p[5, CB:, CB:] = t[CA:, CA:], t[CA:, CA:]
        return p

    def moving(w):
        t, p = w.T, _np.zeros((3, 128, w.shape[0]), _np.float32)
        p[0], p[1, :CB], p[2, CB:] = t[:CA], t[CA:], t[CA:]
        return p.transpose(1, 0, 2)

    arrays["w4"] = _np.stack([stationary(f[n]) for n in ("L0_attn_Wv", "L0_attn_Wk", "L0_attn_Wr", "L0_ffn_Wr1")]
                             ).transpose(2, 0, 1, 3)
    arrays["wo"] = moving(f["L0_attn_Wo"])
    arrays["wr2"] = moving(f["L0_ffn_Wr2"])
    arrays["br2"] = _np.repeat(f["L0_ffn_br2"].reshape(1, E), ROWS, 0)
    w1t = f["L0_ffn_W1"].transpose(2, 0, 1)
    arrays["w1a"] = w1t[:CA]
    arrays["w1b"] = _np.concatenate([w1t[CA:], f["L0_ffn_b1"][None]], 0)
    arrays["w2"] = f["L0_ffn_W2"].transpose(2, 0, 1).reshape(FC, 128, E, C).transpose(1, 2, 0, 3)
    arrays["b2"] = f["L0_ffn_b2"].reshape(1, E, C)

    k = _np.zeros((128, 612 + ROWLEN), _np.float32)
    k[:, 0:128] = _np.eye(128)
    k[:, 128:256] = _np.triu(_np.ones((128, 128)), 1)
    k[:, 256:384] = 1.0
    k[:, 384] = _np.arange(128)
    k[:, 388:396] = _np.arange(E)
    k[:, 396:404] = _np.arange(E) * SLOTS
    k[:, 404:468] = _np.arange(64) * 128
    k[:, 468:468 + BLOCKS] = _np.arange(BLOCKS)
    k[:, 604:604 + G] = _np.arange(128)[:, None] + ROWS * _np.arange(G)
    k[:, 612 + TOKEN] = TOKENS + _np.arange(128)
    arrays["consts"] = k

    nc = _bacc.Bacc("TRN2", target_bir_lowering=False, num_devices=1)
    maps, args = {}, []
    for name, a in arrays.items():
        a = _np.ascontiguousarray(a)
        maps[f"in_{name}"] = a
        args.append(nc.dram_tensor(f"in_{name}", a.shape, _mybir.dt.from_np(a.dtype), kind="ExternalInput").ap())
    args.append(nc.dram_tensor("out_rows", (TOKENS + 128, C), F32, kind="ExternalOutput").ap())
    audio_tower(nc, *args)
    r = _run(nc, [maps], core_ids=[0])
    return r.results[0]["out_rows"][:TOKENS].reshape(STREAMS, FRAMES, C)
```

```python
from contextlib import ExitStack

import numpy as np

import concourse.bass as bass
from concourse import mybir

F32 = mybir.dt.float32
U32 = mybir.dt.uint32
I32 = mybir.dt.int32
ALU = mybir.AluOpType
ACT = mybir.ActivationFunctionType
AX = mybir.AxisListType

STREAMS, SAMPLES = 16, 80000
FRAME, HOP = 100, 160
FRAMES = 1 + (SAMPLES - FRAME) // HOP
BINS = FRAME // 2 + 1
MELS, COEFS = 40, 13
C = 192
CA, CB = 128, C - 128
PAIRS = STREAMS // 2
ROWS = 125
TILES = FRAMES // ROWS
G = 2 * TILES
TOKENS = STREAMS * FRAMES
E, F = 8, 768
FC = F // 128
ROWLEN = C + 4
ONE, WEIGHT, TOKEN = C, C + 1, C + 2
CONSTS = 12
SLOTS = TOKENS + 128
BLOCKS = (2 * TOKENS + E * 127) // 128
SPARE = E * SLOTS
NEG = -1e38
EPS = 1e-5


class Steps:

    def __init__(self, sem, names):
        self.sem, self.names = sem, names.split()

    def at(self, name, pair):
        return pair * len(self.names) + self.names.index(name) + 1

    def all(self, pairs):
        return pairs * len(self.names)


def wait(eng, sem, value):
    if not isinstance(value, int) or value > 0:
        eng.wait_ge(sem, value)


def before(eng, steps, pair):
    wait(eng, steps.sem, steps.all(pair))


def after(eng, steps, name, pair):
    if not isinstance(pair, int) or pair >= 0:
        eng.wait_ge(steps.sem, steps.at(name, pair))


def audio_tower(nc, x, dft, mel, dct, w_proj, b_proj, chan, w4, wo, wr2, br2, w1a, w1b, w2, b2, consts, out):
    slots = nc.dram_tensor("slots", (SPARE + 128, ROWLEN), F32, kind="Internal").ap()
    frames_v = x.rearrange("b (t q s) -> q (b t) s", q=ROWS, s=HOP)
    out_v = out[0:TOKENS, :].rearrange("(n q) c -> q n c", q=ROWS)

    with ExitStack() as top:
        def sem(name):
            return top.enter_context(nc.semaphore(name))

        def sb(ctx, name, shape, dt=F32):
            return ctx.enter_context(nc.sbuf_tensor(name, shape, dt))

        ps = top.enter_context(nc.psum_tensor("ps", [128, 8, 512], F32))

        def alone(eng):
            eng.sem_inc(passed, 1)

        ident = sb(top, "ident", [128, 128])
        expert_of = sb(top, "expert_of", [1, BLOCKS], I32)
        slot_of = sb(top, "slot_of", [1, BLOCKS], I32)

        weights_in = sem("weights_in")
        consts_set = sem("consts_set")
        passed = sem("passed")
        g_prod, g_set = sem("g_prod"), sem("g_set")
        frames_in = sem("frames_in")
        rows_out = sem("rows_out")
        scattered = sem("scattered")
        filled = sem("filled")
        counted, tables, fill_pos = sem("counted"), sem("tables"), sem("fill_pos")
        tok_pe = Steps(sem("tok_pe"), "frames0 frames1 dft0 dft1 mel0 mel1 h0 h1 h2 h3 xt0 xt1 xt2")
        tok_act = Steps(sem("tok_act"), "frames0 frames1 pow0 pow1 log0 log1 h0 h1 h2 h3 lnv rstd xt0 xt1 xt2")
        tok_vec = Steps(sem("tok_vec"), "stats aggr var n1 n2 n3 rstd norm tails")
        mix_pool = Steps(sem("mix_pool"), "diff")
        mix_vec = Steps(sem("mix_vec"), "v k r")
        mix_pe = Steps(sem("mix_pe"), "v k r")
        mix_act = Steps(sem("mix_act"), "v k r")
        wkv_vec = Steps(sem("wkv_vec"), "max lead clampA clampB clampC clampD q_scan p_scan aq den num newton1 newton2 z")
        wkv_act = Steps(sem("wkv_act"), "a2 b2 a b lnden rden")
        wkv_pool = Steps(sem("wkv_pool"), "b2v ap bv sn")
        att_pe = Steps(sem("att_pe"), "o0 o1 o2 o3 xt0 xt1 xt2 rh0 rh1 rh2 score rank")
        att_vec = Steps(sem("att_vec"), "h0 h1 h2 h3 stats aggr var n1 n2 n3 rstd norm tails")
        att_act = Steps(sem("att_act"), "lnv rstd xt0 xt1 xt2 copy rh0 rh1 rh2 ex")
        rt_vec = Steps(sem("rt_vec"), "score top index indexf hot mask c1 c2 c3 c4 c5 c6 c7 c8 gap "
                       "sum rec w1 w2 ids carry pos pick0 pos0 pick1 pos1 posu")

        with ExitStack() as ctx:
            dft_s = sb(ctx, "dft_s", [FRAME, 2 * BINS])
            mel_s = sb(ctx, "mel_s", [2 * BINS, MELS])
            dct_s = sb(ctx, "dct_s", [COEFS, MELS])
            wproj_s = sb(ctx, "wproj_s", [COEFS, C])
            proj_s = sb(ctx, "proj_s", [MELS + 1, C])
            chan_s = sb(ctx, "chan_s", [128, 12])
            negu_s = sb(ctx, "negu_s", [128, 2])
            w4_s = sb(ctx, "w4_s", [128, 4, 6, 128])
            wo_s = sb(ctx, "wo_s", [128, 3, C])
            wr2_s = sb(ctx, "wr2_s", [128, 3, E])
            br2_s = sb(ctx, "br2_s", [ROWS, E])
            before_s = sb(ctx, "before_s", [ROWS, ROWS])
            ones_s = sb(ctx, "ones_s", [ROWS, 128])
            lane_s = sb(ctx, "lane_s", [128, 4])
            eidx_s = sb(ctx, "eidx_s", [128, E])
            ebase_s = sb(ctx, "ebase_s", [128, E])
            wide_s = sb(ctx, "wide_s", [1, 64 + BLOCKS])
            eps_s = sb(ctx, "eps_s", [128, 2])
            fill_s = sb(ctx, "fill_s", [128, ROWLEN])

            fr = sb(ctx, "fr", [ROWS, G, FRAME])
            pw = sb(ctx, "pw", [2 * BINS, 2, FRAMES])
            ft = pw[0:FRAME, :, :]
            le = sb(ctx, "le", [64, 2, FRAMES])
            h = sb(ctx, "h", [ROWS, 3, G, C])
            xn = sb(ctx, "xn", [ROWS, G, C])
            tails1 = sb(ctx, "tails1", [ROWS, TILES, 2, CB])
            tails2 = sb(ctx, "tails2", [ROWS, TILES, 2, CB])
            st1 = sb(ctx, "st1", [ROWS, G, 6])
            mv1 = sb(ctx, "mv1", [ROWS, G, 2])
            nw1 = sb(ctx, "nw1", [ROWS, 5, G])
            st2 = sb(ctx, "st2", [ROWS, G, 6])
            mv2 = sb(ctx, "mv2", [ROWS, G, 2])
            nw2 = sb(ctx, "nw2", [ROWS, 5, G])
            xt = sb(ctx, "xt", [128, 3, FRAMES + 1])
            diff = sb(ctx, "diff", [128, 3, FRAMES])
            mixed = [sb(ctx, f"mixed{n}", [128, 3, FRAMES]) for n in "vkr"]
            vs = [sb(ctx, f"vs{n}", [128, 3, FRAMES]) for n in range(2)]
            ks = [sb(ctx, f"ks{n}", [128, 3, FRAMES]) for n in range(2)]
            sig = [sb(ctx, f"sig{n}", [128, 3, FRAMES]) for n in range(2)]
            om = sb(ctx, "om", [128, 3, FRAMES + 1])
            a2, b2_, a1, b1_ = (sb(ctx, n, [128, 3, FRAMES]) for n in ("a2", "b2_", "a1", "b1_"))
            pp = sb(ctx, "pp", [128, 3, FRAMES + 1])
            qq = sb(ctx, "qq", [128, 3, FRAMES + 1])
            z = sb(ctx, "z", [128, 3, FRAMES])
            xrow = sb(ctx, "xrow", [ROWS, 2, G, ROWLEN])
            x2t = sb(ctx, "x2t", [128, 3, FRAMES])
            rh = diff
            score = sb(ctx, "score", [ROWS, G, E])
            top8 = sb(ctx, "top8", [ROWS, G, E])
            idx8 = sb(ctx, "idx8", [ROWS, G, E], U32)
            idxf = sb(ctx, "idxf", [ROWS, G, 2])
            hot = sb(ctx, "hot", [ROWS, 2, G, E])
            mask = sb(ctx, "mask", [ROWS, G, E])
            cum = sb(ctx, "cum", [ROWS, G + 1, E])
            tmp = sb(ctx, "tmp", [ROWS, 4, G])
            where = sb(ctx, "where", [ROWS, G, E])
            pick = sb(ctx, "pick", [ROWS, G, E])
            posf = sb(ctx, "posf", [ROWS, 2, G])
            posu = sb(ctx, "posu", [ROWS, 2, G], U32)
            tok_id = sb(ctx, "tok_id", [ROWS, G])
            cnt = sb(ctx, "cnt", [128, E])
            fposf = sb(ctx, "fposf", [128, E])
            fposu = sb(ctx, "fposu", [128, E], U32)
            gt = sb(ctx, "gt", [1, E, 64])
            nt = sb(ctx, "nt", [1, 4, E])
            def scratch(buf, n, inner):
                return buf[0:1, :, :].rearrange("p a b -> p (a b)")[:, 0:n * inner].rearrange("p (n i) -> p n i", i=inner)

            past, past2 = scratch(a2, BLOCKS, E), scratch(b2_, BLOCKS, E)
            tabf = scratch(a1, 4, BLOCKS)

            MIX = {"v": 0, "k": 1, "r": 2}
            MU = {"v": 0, "k": 2, "r": 4}
            DECAY, FIRST, BR1 = 6, 8, 10

            def blockcols(t, col):
                return t[:, col:col + 1], t[:, col + 1:col + 2]

            def hslot(p, g, n=0):
                if isinstance(p, int):
                    return h[:, p % 3, g:g + n, :] if n else h[:, p % 3, g, :]
                v = h[:, bass.ds(p % 3, 1), g:g + max(n, 1), :]
                return v.rearrange("q o g c -> q (o g) c") if n else v.rearrange("q o g c -> q (o g c)")

            LOADS = [(ident[:, :], consts[:, 0:128]), (before_s[:, :], consts[0:ROWS, 128:128 + ROWS]),
                     (ones_s[:, :], consts[0:ROWS, 256:384]), (lane_s[:, :], consts[:, 384:388]),
                     (eidx_s[:, :], consts[:, 388:396]), (ebase_s[:, :], consts[:, 396:404]),
                     (wide_s[:, :], consts[0:1, 404:404 + 64 + BLOCKS]),
                     (tok_id[:, :], consts[0:ROWS, 604:604 + G]), (fill_s[:, :], consts[:, 612:612 + ROWLEN]),
                     (dft_s[:, :], dft), (mel_s[:, :], mel), (dct_s[:, :], dct), (wproj_s[:, :], w_proj),
                     (proj_s[MELS:MELS + 1, :], b_proj), (chan_s[:, :], chan),
                     (w4_s[:, :, :, :], w4), (wo_s[:, :, :], wo), (wr2_s[:, :, :], wr2), (br2_s[:, :], br2)]
            LOADED = 16 * len(LOADS)

            def each_turn(eng, body):
                body(-1, 1, "T")
                body(0, 0, "TK")
                body(1, 1, "TKR")
                body(2, 0, "TKRO")
                with eng.Fori(0, (PAIRS - 4) // 2) as n:
                    body(2 * n + 3, 1, "TKRO")
                    body(2 * n + 4, 0, "TKRO")
                body(PAIRS - 1, 1, "KRO")
                body(PAIRS, 0, "RO")
                body(PAIRS + 1, 1, "O")

            with nc.Block() as block:
                @block.sync
                def _(sp):
                    def load_frames(p):
                        after(sp, tok_pe, "frames1", p - 1)
                        sp.dma_start(fr[:, :, :], frames_v[:, bass.ds(p * G, G), 0:FRAME]).then_inc(frames_in, 16)

                    def store_rows(p):
                        wait(sp, rows_out, 16 * p)
                        after(sp, att_vec, "h3", p)
                        sp.dma_start(out_v[:, bass.ds(p * G, G), :], hslot(p, 0, G)).then_inc(rows_out, 16)

                    load_frames(0)
                    for dst, src in LOADS:
                        sp.dma_start(dst, src).then_inc(weights_in, 16)
                    for p in range(1, 4):
                        load_frames(p)
                    store_rows(0)
                    with sp.Fori(1, PAIRS - 3) as i:
                        load_frames(i + 3)
                        store_rows(i)
                    for p in range(PAIRS - 3, PAIRS):
                        store_rows(p)
                    sp.wait_ge(rows_out, 16 * PAIRS)

                @block.tensor
                def _(pe):
                    def transposes(src, tails, steps, banks):
                        for n, b in enumerate(banks):
                            for t in range(TILES):
                                piece = src[:, n * TILES + t, 0:CA] if n < 2 else tails[:, t, :, :]
                                mm = pe.transpose(ps[:, b, t * ROWS:(t + 1) * ROWS], piece, ident[0:ROWS, 0:ROWS])
                            mm.then_inc(steps.sem, 1)

                    def project(w, src, banks):
                        mms = []
                        for n, b in enumerate(banks):
                            parts = ((0, n), (1 + n, 2)) if n < 2 else ((3, 0), (4, 1), (5, 2))
                            for k, (piece, blk) in enumerate(parts):
                                mm = pe.matmul(ps[:, b, 0:FRAMES], w4_s[:, w, piece, :], src[:, blk, :],
                                               start=(k == 0), stop=(k == len(parts) - 1))
                            mms.append(mm)
                        return mms

                    def body(i, par, stages):
                        t, k, o = i + 1, i, i - 2
                        T, K, O = (c in stages for c in "TKO")
                        if T:
                            pe.wait_ge(frames_in, 16 * (t + 1))
                            after(pe, tok_act, "h3", t - 1)
                            after(pe, att_act, "rh1", t - 4)
                            for s in range(2):
                                for c in range(TILES):
                                    mm = pe.transpose(ps[0:FRAME, 6 + s, c * ROWS:(c + 1) * ROWS],
                                                      fr[:, s * TILES + c, :], ident[0:ROWS, 0:ROWS])
                                mm.then_inc(tok_pe.sem, 1)
                        if O:
                            after(pe, wkv_vec, "z", o)
                            if T or K:
                                after(pe, tok_act, "xt2", i)
                            else:
                                after(pe, mix_act, "r", PAIRS - 1)
                            after(pe, att_act, "xt2", o - 1)
                            for n, b in enumerate((0, 1, 2, 5)):
                                for g in (2 * n, 2 * n + 1):
                                    s, c = divmod(g, TILES)
                                    dst, cols = ps[0:ROWS, b, (g % 2) * C:(g % 2 + 1) * C], slice(c * ROWS, (c + 1) * ROWS)
                                    pe.matmul(dst, z[:, s, cols], wo_s[:, 0, :], start=True, stop=False)
                                    mm = pe.matmul(dst, z[:, 2, cols], wo_s[:, 1 + s, :], start=False, stop=True)
                                mm.then_inc(att_pe.sem, 1)
                        if T:
                            after(pe, mix_act, "k", t - 2)
                            after(pe, att_act, "rh2", t - 4)
                            after(pe, rt_vec, "pos", t - 4)
                            for s in range(2):
                                after(pe, tok_act, f"frames{s}", t)
                                pe.matmul(ps[0:2 * BINS, 3 + s, 0:FRAMES], dft_s[:, :], ft[:, s, :],
                                          start=True, stop=True).then_inc(tok_pe.sem, 1)
                        if K:
                            after(pe, att_vec, "h2", k - 2)
                            after(pe, mix_vec, "v", k)
                            project(0, mixed[0], (0, 1, 2))[-1].then_inc(mix_pe.sem, 1)
                        if T:
                            for s in range(2):
                                after(pe, tok_act, f"pow{s}", t)
                                pe.matmul(ps[0:MELS, 6 + s, 0:FRAMES], mel_s[:, :], pw[:, s, :],
                                          start=True, stop=True).then_inc(tok_pe.sem, 1)
                        if K:
                            after(pe, att_vec, "h3", k - 2)
                            if not T:
                                after(pe, att_act, "rh2", k - 3)
                                after(pe, rt_vec, "pos", k - 3)
                            after(pe, mix_vec, "k", k)
                            project(1, mixed[1], (3, 4, 5))[-1].then_inc(mix_pe.sem, 1)
                        if T:
                            after(pe, mix_act, "v", t - 1)
                            for n, b in enumerate((6, 7, 0, 1)):
                                after(pe, tok_act, "log1", t)
                                for g in (2 * n, 2 * n + 1):
                                    c = g % TILES
                                    mm = pe.matmul(ps[0:ROWS, b, (g % 2) * C:(g % 2 + 1) * C],
                                                   le[0:MELS + 1, n // 2, c * ROWS:(c + 1) * ROWS],
                                                   proj_s[:, :], start=True, stop=True)
                                mm.then_inc(tok_pe.sem, 1)
                        if O:
                            if K:
                                after(pe, mix_act, "k", k)
                            else:
                                after(pe, att_act, "rh2", o - 1)
                                after(pe, rt_vec, "pos", o - 1)
                            after(pe, att_vec, "tails", o)
                            transposes(xrow[:, 0, :, :], tails2, att_pe, (3, 4, 5))
                        if K:
                            after(pe, mix_act, "v", k)
                            if T:
                                after(pe, tok_act, "h3", t)
                            after(pe, mix_vec, "r", k)
                            project(2, mixed[2], (0, 1, 2))[-1].then_inc(mix_pe.sem, 1)
                        if O:
                            if T:
                                after(pe, tok_act, "h3", t)
                            after(pe, att_act, "xt2", o)
                            for mm in project(3, x2t, (6, 7, 3)):
                                mm.then_inc(att_pe.sem, 1)
                            after(pe, att_act, "rh2", o)
                            for g in range(G):
                                s, c = divmod(g, TILES)
                                dst, cols = ps[0:ROWS, 4, g * E:(g + 1) * E], slice(c * ROWS, (c + 1) * ROWS)
                                pe.matmul(dst, rh[:, s, cols], wr2_s[:, 0, :], start=True, stop=False)
                                mm = pe.matmul(dst, rh[:, 2, cols], wr2_s[:, 1 + s, :], start=False, stop=True)
                            mm.then_inc(att_pe.sem, 1)
                        if T:
                            after(pe, mix_act, "r", t - 1)
                            after(pe, tok_vec, "tails", t)
                            transposes(xn, tails1, tok_pe, (0, 1, 2))
                        if O:
                            after(pe, rt_vec, "c8", o)
                            dst = ps[0:ROWS, 4, G * E:2 * G * E]
                            pe.matmul(dst, before_s[:, :], mask[:, :, :], start=True, stop=False)
                            pe.matmul(dst, ones_s[:, 0:ROWS], cum[:, 0:G, :], start=False, stop=True).then_inc(att_pe.sem, 1)

                    pe.wait_ge(weights_in, LOADED)
                    pe.matmul(ps[0:MELS, 0, 0:C], dct_s[:, :], wproj_s[:, :], start=True, stop=True).then_inc(g_prod, 1)
                    pe.wait_ge(g_set, 1)
                    pe.wait_ge(consts_set, CONSTS)
                    each_turn(pe, body)
                    pe.wait_ge(rt_vec.sem, rt_vec.all(PAIRS))
                    pe.matmul(ps[:, 0, 0:E], ones_s[:, :], cum[:, G, :], start=True, stop=True).then_inc(counted, 1)

                @block.scalar
                def _(act):
                    def rsqrt_seed(vec, steps, nw, p):
                        after(act, vec, "var", p)
                        act.activation(nw[:, 1, :], nw[:, 0, :], ACT.Ln).then_inc(steps.sem, 1)
                        after(act, steps, "lnv", p)
                        act.activation(nw[:, 2, :], nw[:, 1, :], ACT.Exp, scale=-0.5).then_inc(steps.sem, 1)

                    def body(i, par, stages):
                        t, k, r, o = i + 1, i, i - 1, i - 2
                        T, K, R, O = (c in stages for c in "TKRO")
                        if T:
                            for s in range(2):
                                after(act, tok_pe, f"frames{s}", t)
                                act.activation(ft[:, s, :], ps[0:FRAME, 6 + s, 0:FRAMES], ACT.Copy).then_inc(tok_act.sem, 1)
                            for s in range(2):
                                after(act, tok_pe, f"dft{s}", t)
                                act.activation(pw[:, s, :], ps[0:2 * BINS, 3 + s, 0:FRAMES], ACT.Square).then_inc(tok_act.sem, 1)
                        if O:
                            rsqrt_seed(att_vec, att_act, nw2, o)
                        if K:
                            before(act, wkv_vec, k - 1)
                            after(act, mix_pe, "v", k)
                            act.activation(vs[par][:, :, :], ps[:, 0:3, 0:FRAMES], ACT.Copy).then_inc(mix_act.sem, 1)
                        if T:
                            for s in range(2):
                                after(act, tok_pe, f"mel{s}", t)
                                act.activation(le[0:MELS, s, :], ps[0:MELS, 6 + s, 0:FRAMES], ACT.Ln,
                                               bias=eps_s[0:MELS, 0:1]).then_inc(tok_act.sem, 1)
                        if R:
                            after(act, wkv_vec, "clampA", r)
                            act.activation(a2[:, :, :], a2[:, :, :], ACT.Exp).then_inc(wkv_act.sem, 1)
                            after(act, wkv_vec, "clampB", r)
                            act.activation(b2_[:, :, :], b2_[:, :, :], ACT.Exp, scale=-1.0).then_inc(wkv_act.sem, 1)
                        if K:
                            after(act, mix_pe, "k", k)
                            act.activation(ks[par][:, :, :], ps[:, 3:6, 0:FRAMES], ACT.Copy).then_inc(mix_act.sem, 1)
                        if R:
                            after(act, wkv_vec, "clampC", r)
                            act.activation(a1[:, :, :], a1[:, :, :], ACT.Exp).then_inc(wkv_act.sem, 1)
                            after(act, wkv_vec, "clampD", r)
                            act.activation(b1_[:, :, :], b1_[:, :, :], ACT.Exp, scale=-1.0).then_inc(wkv_act.sem, 1)
                        if T:
                            before(act, att_vec, t - 2)
                            wait(act, rows_out, 16 * (t - 2))
                            for n, b in enumerate((6, 7, 0, 1)):
                                after(act, tok_pe, f"h{n}", t)
                                act.activation(hslot(t, 2 * n, 2), ps[0:ROWS, b, 0:2 * C].rearrange("q (g c) -> q g c", g=2),
                                               ACT.Copy).then_inc(tok_act.sem, 1)
                        if O:
                            for n, b in enumerate((3, 4, 5)):
                                after(act, att_pe, f"xt{n}", o)
                                act.activation(x2t[:, n, :], ps[:, b, 0:FRAMES], ACT.Copy).then_inc(att_act.sem, 1)
                            act.activation(xrow[:, 1, :, 0:C], xrow[:, 0, :, 0:C], ACT.Copy).then_inc(att_act.sem, 1)
                        if T:
                            rsqrt_seed(tok_vec, tok_act, nw1, t)
                        if K:
                            after(act, mix_pe, "r", k)
                            act.activation(sig[par][:, :, :], ps[:, 0:3, 0:FRAMES], ACT.Sigmoid).then_inc(mix_act.sem, 1)
                        if O:
                            if K:
                                after(act, mix_vec, "r", k)
                            for n, b in enumerate((6, 7, 3)):
                                after(act, att_pe, f"rh{n}", o)
                                act.activation(rh[:, n, :], ps[:, b, 0:FRAMES], ACT.Relu,
                                               bias=blockcols(chan_s, BR1)[n // 2]).then_inc(att_act.sem, 1)
                        if R:
                            after(act, wkv_vec, "den", r)
                            act.activation(b2_[:, :, :], a1[:, :, :], ACT.Ln).then_inc(wkv_act.sem, 1)
                            after(act, wkv_act, "lnden", r)
                            act.activation(b2_[:, :, :], b2_[:, :, :], ACT.Exp, scale=-1.0).then_inc(wkv_act.sem, 1)
                        if T:
                            after(act, mix_vec, "r", t - 1)
                            for n, b in enumerate((0, 1, 2)):
                                after(act, tok_pe, f"xt{n}", t)
                                act.activation(xt[:, n, 1:FRAMES + 1], ps[:, b, 0:FRAMES], ACT.Copy).then_inc(tok_act.sem, 1)
                        if O:
                            after(act, rt_vec, "gap", o)
                            act.activation(tmp[:, 1, :], tmp[:, 0, :], ACT.Exp).then_inc(att_act.sem, 1)

                    act.wait_ge(g_prod, 1)
                    act.activation(proj_s[0:MELS, :], ps[0:MELS, 0, 0:C], ACT.Copy).then_inc(g_set, 1)
                    act.wait_ge(consts_set, CONSTS)
                    each_turn(act, body)

                @block.gpsimd
                def _(pool):
                    def scatter(p):
                        pool.wait_ge(rt_vec.sem, rt_vec.at("posu", p))
                        pool.wait_ge(att_act.sem, att_act.at("copy", p))
                        alone(pool)
                        for k in range(2):
                            for g in range(G):
                                pool.indirect_dma_start(
                                    out=slots, out_offset=bass.IndirectOffsetOnAxis(posu[:, k, g:g + 1], 0),
                                    in_=xrow[:, k, g, :], in_offset=None, bounds_check=SPARE + 127,
                                    oob_is_err=True, compute_op=ALU.bypass).then_inc(scattered, 16)

                    def body(i, par, stages):
                        t, r, v, gate = i + 1, i - 1, vs[1 - par], sig[1 - par]
                        T, R, O = (c in stages for c in "TRO")
                        if O and not (isinstance(i, int) and i == 2):
                            scatter(i - 3)
                        if R:
                            after(pool, wkv_act, "b2", r)
                            after(pool, wkv_vec, "q_scan", r)
                            pool.tensor_tensor(b2_[:, :, :], b2_[:, :, :], v[:, :, :], ALU.mult).then_inc(wkv_pool.sem, 1)
                            after(pool, wkv_vec, "p_scan", r)
                            after(pool, wkv_act, "a", r)
                            pool.tensor_tensor(a2[:, :, :], a1[:, :, :], pp[:, :, 0:FRAMES], ALU.mult).then_inc(wkv_pool.sem, 1)
                            after(pool, wkv_vec, "den", r)
                            pool.tensor_tensor(b1_[:, :, :], b1_[:, :, :], v[:, :, :], ALU.mult).then_inc(wkv_pool.sem, 1)
                            after(pool, wkv_vec, "num", r)
                            after(pool, mix_act, "r", r)
                            pool.tensor_tensor(b1_[:, :, :], a2[:, :, :], gate[:, :, :], ALU.mult).then_inc(wkv_pool.sem, 1)
                        if T:
                            after(pool, tok_act, "xt2", t)
                            after(pool, att_pe, "score", t - 3)
                            pool.tensor_tensor(diff[:, :, :], xt[:, :, 1:], xt[:, :, 0:FRAMES], ALU.subtract).then_inc(mix_pool.sem, 1)

                    pool.wait_ge(consts_set, CONSTS)
                    each_turn(pool, body)
                    scatter(PAIRS - 1)
                    pool.wait_ge(fill_pos, 2)
                    for e in range(E):
                        pool.indirect_dma_start(
                            out=slots, out_offset=bass.IndirectOffsetOnAxis(fposu[:, e:e + 1], 0),
                            in_=fill_s[:, :], in_offset=None, bounds_check=SPARE + 127,
                            oob_is_err=True, compute_op=ALU.bypass).then_inc(filled, 16)
                    pool.dma_start(slots[SPARE:SPARE + 128, :], fill_s[:, :]).then_inc(filled, 16)
                    pool.wait_ge(filled, 16 * (E + 1))
                    pool.wait_ge(scattered, 16 * 2 * G * PAIRS)

                @block.vector
                def _(dve):
                    def row_stats(p, st, mv, nw, steps):
                        alone(dve)
                        for g in range(G):
                            mm = dve.bn_stats(st[:, g, :], hslot(p, g))
                        mm.then_inc(steps.sem, 1)
                        after(dve, steps, "stats", p)
                        alone(dve)
                        for g in range(G):
                            mm = dve.bn_aggr(mv[:, g, :], st[:, g, :])
                        mm.then_inc(steps.sem, 1)
                        after(dve, steps, "aggr", p)
                        dve.tensor_scalar(nw[:, 0, :], mv[:, :, 1], EPS, None, ALU.add).then_inc(steps.sem, 1)

                    def row_norm(p, dst, tails, mv, nw, steps, act_steps):
                        after(dve, act_steps, "rstd", p)
                        dve.tensor_tensor(nw[:, 3, :], nw[:, 0, :], nw[:, 2, :], ALU.mult).then_inc(steps.sem, 1)
                        after(dve, steps, "n1", p)
                        dve.tensor_tensor(nw[:, 3, :], nw[:, 3, :], nw[:, 2, :], ALU.mult).then_inc(steps.sem, 1)
                        after(dve, steps, "n2", p)
                        dve.tensor_scalar(nw[:, 3, :], nw[:, 3, :], -0.5, 1.5, ALU.mult, ALU.add).then_inc(steps.sem, 1)
                        after(dve, steps, "n3", p)
                        dve.tensor_tensor(nw[:, 4, :], nw[:, 3, :], nw[:, 2, :], ALU.mult).then_inc(steps.sem, 1)
                        after(dve, steps, "rstd", p)
                        for g in range(G):
                            mm = dve.tensor_scalar(dst[:, g, 0:C], hslot(p, g), mv[:, g, 0:1], nw[:, 4, g:g + 1],
                                                   ALU.subtract, ALU.mult)
                        mm.then_inc(steps.sem, 1)
                        after(dve, steps, "norm", p)
                        dve.tensor_copy(tails[:, :, :, :].rearrange("q t s c -> q s t c"),
                                        dst[:, :, CA:C].rearrange("q (s t) c -> q s t c", s=2)).then_inc(steps.sem, 1)

                    def mix(p):
                        after(dve, mix_pool, "diff", p)
                        after(dve, mix_pe, "r", p - 1)
                        for name in ("v", "k", "r"):
                            m, (mu_a, mu_b) = mixed[MIX[name]], blockcols(chan_s, MU[name])
                            dve.scalar_tensor_tensor(m[:, 0:2, :], diff[:, 0:2, :], mu_a, xt[:, 0:2, 0:FRAMES],
                                                     ALU.mult, ALU.add)
                            dve.scalar_tensor_tensor(m[:, 2, :], diff[:, 2, :], mu_b, xt[:, 2, 0:FRAMES],
                                                     ALU.mult, ALU.add).then_inc(mix_vec.sem, 1)

                    def exponents(p, k):
                        w, negu = blockcols(chan_s, DECAY), blockcols(negu_s, 0)
                        after(dve, mix_act, "k", p)
                        for n in range(3):
                            mm = dve.tensor_tensor_scan(om[:, n, 1:], w[n // 2].to_broadcast([128, FRAMES]), k[:, n, :],
                                                        NEG, ALU.add, ALU.max)
                        mm.then_inc(wkv_vec.sem, 1)
                        after(dve, wkv_vec, "max", p)
                        after(dve, att_pe, "o3", p - 1)
                        dve.tensor_tensor(z[:, :, :], om[:, :, 0:FRAMES], k[:, :, :], ALU.subtract).then_inc(wkv_vec.sem, 1)
                        after(dve, wkv_vec, "lead", p)
                        for buf, add, op in ((a2, w, ALU.min), (b2_, w, ALU.max), (a1, negu, ALU.min), (b1_, negu, ALU.max)):
                            dve.tensor_scalar(buf[:, 0:2, :], z[:, 0:2, :], add[0], 0.0, ALU.add, op)
                            dve.tensor_scalar(buf[:, 2, :], z[:, 2, :], add[1], 0.0, ALU.add, op).then_inc(wkv_vec.sem, 1)

                    def scan(p, dst, ready):
                        ready()
                        for n in range(3):
                            mm = dve.tensor_tensor_scan(dst[:, n, 1:], a2[:, n, :], b2_[:, n, :], 0.0, ALU.mult, ALU.add)
                        mm.then_inc(wkv_vec.sem, 1)

                    def fraction(p):
                        after(dve, wkv_act, "b", p)
                        after(dve, wkv_vec, "p_scan", p)
                        dve.tensor_tensor(b2_[:, :, :], a1[:, :, :], qq[:, :, 0:FRAMES], ALU.mult).then_inc(wkv_vec.sem, 1)
                        after(dve, wkv_vec, "aq", p)
                        after(dve, wkv_pool, "ap", p)
                        dve.tensor_tensor(a1[:, :, :], b2_[:, :, :], b1_[:, :, :], ALU.add).then_inc(wkv_vec.sem, 1)
                        after(dve, wkv_pool, "bv", p)
                        dve.tensor_tensor(a2[:, :, :], a2[:, :, :], b1_[:, :, :], ALU.add).then_inc(wkv_vec.sem, 1)

                    def divide(p):
                        after(dve, wkv_act, "rden", p)
                        dve.tensor_tensor(z[:, :, :], a1[:, :, :], b2_[:, :, :], ALU.mult).then_inc(wkv_vec.sem, 1)
                        after(dve, wkv_vec, "newton1", p)
                        dve.scalar_tensor_tensor(z[:, :, :], z[:, :, :], 2.0, b2_[:, :, :], ALU.subtract, ALU.mult).then_inc(wkv_vec.sem, 1)
                        after(dve, wkv_vec, "newton2", p)
                        after(dve, wkv_pool, "sn", p)
                        dve.scalar_tensor_tensor(z[:, :, :], z[:, :, :], -1.0, b1_[:, :, :], ALU.mult, ALU.mult).then_inc(wkv_vec.sem, 1)

                    def add_attention(p):
                        for n, b in enumerate((0, 1, 2, 5)):
                            after(dve, att_pe, f"o{n}", p)
                            dve.tensor_tensor(hslot(p, 2 * n, 2), ps[0:ROWS, b, 0:2 * C].rearrange("q (g c) -> q g c", g=2),
                                              hslot(p, 2 * n, 2), ALU.add).then_inc(att_vec.sem, 1)
                        after(dve, att_vec, "h3", p)

                    def choose(p):
                        def done(name):
                            after(dve, rt_vec, name, p)

                        after(dve, att_pe, "score", p)
                        dve.tensor_tensor(score[:, :, :], ps[0:ROWS, 4, 0:G * E].rearrange("q (g e) -> q g e", g=G),
                                          br2_s[:, :].unsqueeze(1).to_broadcast([ROWS, G, E]), ALU.add).then_inc(rt_vec.sem, 1)
                        done("score")
                        alone(dve)
                        for g in range(G):
                            mm = dve.max(top8[:, g, :], score[:, g, :])
                        mm.then_inc(rt_vec.sem, 1)
                        done("top")
                        alone(dve)
                        for g in range(G):
                            mm = dve.max_index(idx8[:, g, :], top8[:, g, :], score[:, g, :])
                        mm.then_inc(rt_vec.sem, 1)
                        done("index")
                        dve.tensor_copy(idxf[:, :, :], idx8[:, :, 0:2]).then_inc(rt_vec.sem, 1)
                        done("indexf")
                        for k in range(2):
                            mm = dve.tensor_tensor(hot[:, k, :, :], eidx_s[0:ROWS, :].unsqueeze(1).to_broadcast([ROWS, G, E]),
                                                   idxf[:, :, k:k + 1].to_broadcast([ROWS, G, E]), ALU.is_equal)
                        mm.then_inc(rt_vec.sem, 1)
                        done("hot")
                        dve.tensor_tensor(mask[:, :, :], hot[:, 0, :, :], hot[:, 1, :, :], ALU.add).then_inc(rt_vec.sem, 1)
                        done("mask")
                        for g in range(G):
                            dve.tensor_tensor(cum[:, g + 1, :], cum[:, g, :], mask[:, g, :], ALU.add).then_inc(rt_vec.sem, 1)
                            done(f"c{g + 1}")
                        dve.tensor_tensor(tmp[:, 0, :], top8[:, :, 1], top8[:, :, 0], ALU.subtract).then_inc(rt_vec.sem, 1)

                    def place(p):
                        def done(name):
                            after(dve, rt_vec, name, p)

                        after(dve, att_act, "ex", p)
                        dve.tensor_scalar(tmp[:, 2, :], tmp[:, 1, :], 1.0, None, ALU.add).then_inc(rt_vec.sem, 1)
                        done("sum")
                        dve.reciprocal(tmp[:, 3, :], tmp[:, 2, :]).then_inc(rt_vec.sem, 1)
                        done("rec")
                        dve.tensor_copy(xrow[:, 0, :, WEIGHT], tmp[:, 3, :]).then_inc(rt_vec.sem, 1)
                        dve.tensor_tensor(xrow[:, 1, :, WEIGHT], tmp[:, 1, :], tmp[:, 3, :], ALU.mult).then_inc(rt_vec.sem, 1)
                        for k in range(2):
                            dve.tensor_copy(xrow[:, k, :, TOKEN], tok_id[:, :])
                        dve.tensor_scalar(tok_id[:, :], tok_id[:, :], float(G * ROWS), None, ALU.add).then_inc(rt_vec.sem, 1)
                        after(dve, att_pe, "rank", p)
                        dve.tensor_copy(cum[:, 0, :], cum[:, G, :]).then_inc(rt_vec.sem, 1)
                        dve.tensor_tensor(where[:, :, :], ps[0:ROWS, 4, G * E:2 * G * E].rearrange("q (g e) -> q g e", g=G),
                                          ebase_s[0:ROWS, :].unsqueeze(1).to_broadcast([ROWS, G, E]), ALU.add).then_inc(rt_vec.sem, 1)
                        for k in range(2):
                            done("pos" if k == 0 else "pos0")
                            dve.tensor_tensor(pick[:, :, :], hot[:, k, :, :], where[:, :, :], ALU.mult).then_inc(rt_vec.sem, 1)
                            done(f"pick{k}")
                            dve.tensor_reduce(posf[:, k, :], pick[:, :, :], AX.X, ALU.add).then_inc(rt_vec.sem, 1)
                        done("pos1")
                        dve.tensor_copy(posu[:, :, :], posf[:, :, :]).then_inc(rt_vec.sem, 1)

                    def body(i, par, stages):
                        t, k, r, o = i + 1, i, i - 1, i - 2
                        T, K, R, O = (c in stages for c in "TKRO")
                        if K:
                            mix(k)
                        if O:
                            add_attention(o)
                            row_stats(o, st2, mv2, nw2, att_vec)
                        if R:
                            exponents(r, ks[1 - par])
                        if O:
                            wait(dve, scattered, 16 * 2 * G * o)
                            row_norm(o, xrow[:, 0, :, :], tails2, mv2, nw2, att_vec, att_act)
                        if R:
                            scan(r, qq, lambda: after(dve, wkv_act, "b2", r))
                        if T:
                            after(dve, tok_act, "h3", t)
                            row_stats(t, st1, mv1, nw1, tok_vec)
                        if R:
                            scan(r, pp, lambda: after(dve, wkv_pool, "b2v", r))
                        if T:
                            row_norm(t, xn, tails1, mv1, nw1, tok_vec, tok_act)
                        if R:
                            fraction(r)
                        if O:
                            choose(o)
                        if R:
                            divide(r)
                        if O:
                            place(o)

                    dve.memset(le[32:64, :, :], 1.0).then_inc(consts_set, 1)
                    dve.memset(xt[:, :, 0:1], 0.0).then_inc(consts_set, 1)
                    dve.memset(om[:, :, 0:1], NEG).then_inc(consts_set, 1)
                    dve.memset(pp[:, :, 0:1], 0.0).then_inc(consts_set, 1)
                    dve.memset(qq[:, :, 0:1], 0.0).then_inc(consts_set, 1)
                    dve.memset(cum[:, 0, :], 0.0).then_inc(consts_set, 1)
                    dve.memset(eps_s[:, 0:1], 1e-6).then_inc(consts_set, 1)
                    dve.memset(xrow[:, 0, :, C:ROWLEN], 1.0).then_inc(consts_set, 1)
                    dve.memset(xrow[:, 1, :, C:ROWLEN], 1.0).then_inc(consts_set, 1)
                    dve.memset(eps_s[:, 1:2], EPS).then_inc(consts_set, 1)
                    dve.wait_ge(weights_in, LOADED)
                    dve.tensor_scalar(negu_s[:, :], chan_s[:, FIRST:FIRST + 2], -1.0, None, ALU.mult).then_inc(consts_set, 1)
                    dve.memset(gt[:, :, :], 0.0).then_inc(consts_set, 1)
                    dve.wait_ge(consts_set, CONSTS)

                    each_turn(dve, body)

                    n_step = [0]

                    def chain(ins):
                        n_step[0] += 1
                        ins.then_inc(tables, 1)
                        dve.wait_ge(tables, n_step[0])

                    dve.wait_ge(counted, 1)
                    dve.tensor_tensor(cnt[:, :], ps[:, 0, 0:E], ebase_s[:, :], ALU.add).then_inc(fill_pos, 1)
                    dve.wait_ge(fill_pos, 1)
                    chain(dve.tensor_scalar(fposf[:, :], cnt[:, :], lane_s[:, 0:1], None, ALU.add))
                    dve.tensor_copy(fposu[:, :], fposf[:, :]).then_inc(fill_pos, 1)
                    chain(dve.tensor_copy(nt[:, 0, :], ps[0:1, 0, 0:E]))
                    chain(dve.tensor_tensor(gt[:, :, 0:63], nt[:, 0, :].unsqueeze(2).to_broadcast([1, E, 63]),
                                            wide_s[:, 0:63].unsqueeze(1).to_broadcast([1, E, 63]), ALU.is_gt))
                    chain(dve.tensor_reduce(nt[:, 1, :], gt[:, :, :], AX.X, ALU.add))
                    chain(dve.tensor_tensor_scan(nt[:, 2, :], ones_s[0:1, 0:E], nt[:, 1, :], 0.0, ALU.mult, ALU.add))
                    chain(dve.tensor_scalar(nt[:, 3, :], nt[:, 1, :], -128.0, float(SLOTS), ALU.mult, ALU.add))
                    chain(dve.tensor_tensor(past[:, :, :], wide_s[:, 64:64 + BLOCKS].unsqueeze(2).to_broadcast([1, BLOCKS, E]),
                                            nt[:, 2, :].unsqueeze(1).to_broadcast([1, BLOCKS, E]), ALU.is_ge))
                    chain(dve.tensor_tensor(past2[:, :, :], past[:, :, :],
                                            nt[:, 3, :].unsqueeze(1).to_broadcast([1, BLOCKS, E]), ALU.mult))
                    chain(dve.tensor_reduce(tabf[:, 0, :], past[:, :, :], AX.X, ALU.add))
                    chain(dve.tensor_reduce(tabf[:, 1, :], past2[:, :, :], AX.X, ALU.add))
                    chain(dve.tensor_scalar(tabf[:, 0, :], tabf[:, 0, :], float(E - 1), None, ALU.min))
                    chain(dve.tensor_scalar(tabf[:, 2, :], wide_s[:, 64:64 + BLOCKS], 128.0, None, ALU.mult))
                    chain(dve.tensor_tensor(tabf[:, 3, :], tabf[:, 1, :], tabf[:, 2, :], ALU.add))
                    chain(dve.tensor_scalar(tabf[:, 3, :], tabf[:, 3, :], float(SPARE), None, ALU.min))
                    chain(dve.tensor_copy(expert_of[:, 0:BLOCKS], tabf[:, 0, :]))
                    chain(dve.tensor_copy(slot_of[:, 0:BLOCKS], tabf[:, 3, :]))

        with ExitStack() as ctx:
            w1a_s = sb(ctx, "w1a_s", [128, E, F])
            w1b_s = sb(ctx, "w1b_s", [CB + 1, E, F])
            w2_s = sb(ctx, "w2_s", [128, E, FC, C])
            b2_s = sb(ctx, "b2_s", [1, E, C])
            one_s = sb(ctx, "one_s", [1, 128])
            xb = [sb(ctx, f"xb{n}", [128, ROWLEN]) for n in range(4)]
            xbt = [sb(ctx, f"xbt{n}", [128, 256]) for n in range(2)]
            mid = sb(ctx, "mid", [128, F])
            midt = sb(ctx, "midt", [128, FC, 128])
            yb = [sb(ctx, f"yb{n}", [128, C]) for n in range(2)]
            ids = [sb(ctx, f"ids{n}", [128, 1], U32) for n in range(2)]

            experts_in = sem("experts_in")
            one_set = sem("one_set")
            block_in = [sem(f"block_in{n}") for n in range(4)]
            b_xt, b_mid, b_midt, b_y = sem("b_xt"), sem("b_mid"), sem("b_midt"), sem("b_y")
            e_xt, e_mid0, e_mid1, e_midt0, e_midt1, e_y = (sem(n) for n in ("e_xt", "e_mid0", "e_mid1", "e_midt0", "e_midt1", "e_y"))
            id_set, added = sem("id_set"), sem("added")
            XT, MID, MT, Y = 0, (1, 2), (3, 4), 5
            UN = 4
            assert BLOCKS % UN == 0

            def each_block(eng, work):
                for j in range(UN):
                    work(j, 0)
                with eng.Fori(1, BLOCKS // UN - 1) as n:
                    for j in range(UN):
                        work(j, n)
                for j in range(UN):
                    work(j, BLOCKS // UN - 1)

            with nc.Block() as block:
                @block.sync
                def _(sp):
                    for e in range(E):
                        sp.dma_start(w1a_s[:, e, :], w1a[:, e, :]).then_inc(experts_in, 16)
                        sp.dma_start(w1b_s[:, e, :], w1b[:, e, :]).then_inc(experts_in, 16)
                        sp.dma_start(w2_s[:, e, :, :], w2[:, e, :, :]).then_inc(experts_in, 16)
                    sp.dma_start(b2_s[:, :, :], b2).then_inc(experts_in, 16)

                    def load(j, n):
                        i = n * UN + j
                        wait(sp, e_y, i - 3)
                        wait(sp, id_set, i - 3)
                        first = sp.value_load(slot_of[0:1, bass.ds(i, 1)], min_val=0, max_val=SPARE)
                        sp.dma_start(xb[j][:, :], slots[bass.ds(first, 128), :]).then_inc(block_in[j], 16)

                    each_block(sp, load)

                @block.scalar
                def _(act):
                    def rows(i, j):
                        act.wait_ge(b_xt, i + 1)
                        act.activation(xbt[j % 2][:, 0:128], ps[:, XT, 0:128], ACT.Copy)
                        act.activation(xbt[j % 2][0:CB + 1, 128:256], ps[0:CB + 1, XT, 128:256], ACT.Copy).then_inc(e_xt, 1)

                    def half(j, n):
                        i = n * UN + j
                        act.wait_ge(b_mid, 2 * i + 1)
                        wait(act, b_midt, 2 * i)
                        act.activation(mid[:, 0:F // 2], ps[:, MID[0], 0:F // 2], ACT.Relu).then_inc(e_mid0, 1)
                        if not (isinstance(i, int) and i == BLOCKS - 1):
                            rows(i + 1, j + 1)
                        act.wait_ge(b_midt, 2 * i + 1)
                        wait(act, b_y, i)
                        act.activation(midt[:, 0:FC // 2, :], ps[:, MT[0], 0:F // 2].rearrange("p (c m) -> p c m", m=128),
                                       ACT.Copy).then_inc(e_midt0, 1)

                    rows(0, 0)
                    each_block(act, half)

                @block.gpsimd
                def _(pool):
                    def add(j, n):
                        i = n * UN + j
                        pool.wait_ge(block_in[j], 16 * (n + 1))
                        alone(pool)
                        pool.tensor_copy(ids[j % 2][:, :], xb[j][:, TOKEN:TOKEN + 1]).then_inc(id_set, 1)
                        pool.wait_ge(e_y, i + 1)
                        pool.wait_ge(id_set, i + 1)
                        alone(pool)
                        pool.indirect_dma_start(
                            out=out, out_offset=bass.IndirectOffsetOnAxis(ids[j % 2][:, 0:1], 0), in_=yb[j % 2][:, :],
                            in_offset=None, bounds_check=TOKENS + 127, oob_is_err=True,
                            compute_op=ALU.add).then_inc(added, 16)
                        pool.wait_ge(added, 16 * (i + 1))

                    each_block(pool, add)

                @block.tensor
                def _(pe):
                    def turn_in(j, n):
                        i = n * UN + j
                        pe.wait_ge(block_in[j], 16 * (n + 1))
                        wait(pe, e_xt, i)
                        pe.transpose(ps[:, XT, 0:128], xb[j][:, 0:CA], ident[:, :])
                        pe.transpose(ps[0:CB + 1, XT, 128:256], xb[j][:, CA:C + 1], ident[:, :]).then_inc(b_xt, 1)

                    def up(j, i):
                        e = pe.value_load(expert_of[0:1, bass.ds(i, 1)], min_val=0, max_val=E - 1)
                        pe.wait_ge(e_xt, i + 1)
                        for n in range(2):
                            wait(pe, (e_mid0, e_mid1)[n], i)
                            dst, cols = ps[:, MID[n], 0:F // 2], slice(n * F // 2, (n + 1) * F // 2)
                            pe.matmul(dst, xbt[j % 2][:, 0:128], w1a_s[:, bass.ds(e, 1), cols], start=True, stop=False)
                            pe.matmul(dst, xbt[j % 2][0:CB + 1, 128:256], w1b_s[:, bass.ds(e, 1), cols],
                                      start=False, stop=True).then_inc(b_mid, 1)

                    def turn_mid(i):
                        for n in range(2):
                            pe.wait_ge((e_mid0, e_mid1)[n], i + 1)
                            wait(pe, (e_midt0, e_midt1)[n], i)
                            for c in range(FC // 2):
                                mm = pe.transpose(ps[:, MT[n], c * 128:(c + 1) * 128],
                                                  mid[:, (n * FC // 2 + c) * 128:(n * FC // 2 + c + 1) * 128], ident[:, :])
                            mm.then_inc(b_midt, 1)

                    def down(j, i):
                        e = pe.value_load(expert_of[0:1, bass.ds(i, 1)], min_val=0, max_val=E - 1)
                        wait(pe, e_y, i)
                        for c in range(FC):
                            if c % 3 == 0:
                                pe.wait_ge((e_midt0, e_midt1)[c // 3], i + 1)
                            pe.matmul(ps[:, Y, 0:C], midt[:, c, :], w2_s[:, bass.ds(e, 1), c, :], start=(c == 0), stop=False)
                        pe.matmul(ps[:, Y, 0:C], one_s[:, :], b2_s[:, bass.ds(e, 1), :], start=False, stop=True).then_inc(b_y, 1)

                    pe.wait_ge(experts_in, 16 * (3 * E + 1))
                    pe.wait_ge(one_set, 1)
                    turn_in(0, 0)
                    up(0, 0)
                    turn_in(1, 0)
                    turn_mid(0)
                    def four(n):
                        for j in range(1, 1 + UN):
                            i = n * UN + j
                            up(j, i)
                            down(j - 1, i - 1)
                            turn_in((j + 1) % UN, n + (j + 1) // UN)
                            turn_mid(i)

                    four(0)
                    with pe.Fori(1, BLOCKS // UN - 1) as n:
                        four(n)
                    for i in range(BLOCKS - 3, BLOCKS):
                        up(i, i)
                        down(i - 1, i - 1)
                        if i + 1 < BLOCKS:
                            turn_in((i + 1) % UN, (i + 1) // UN)
                        turn_mid(i)
                    down(BLOCKS - 1, BLOCKS - 1)

                @block.vector
                def _(dve):
                    dve.memset(one_s[:, :], 1.0).then_inc(one_set, 1)

                    def scale(i, j):
                        dve.wait_ge(b_y, i + 1)
                        wait(dve, added, 16 * (i - 1))
                        dve.tensor_scalar(yb[j % 2][:, :], ps[:, Y, 0:C], xb[j % UN][:, WEIGHT:WEIGHT + 1], None,
                                          ALU.mult).then_inc(e_y, 1)

                    def half(j, n):
                        i = n * UN + j
                        dve.wait_ge(b_mid, 2 * i + 2)
                        wait(dve, b_midt, 2 * i)
                        dve.tensor_scalar(mid[:, F // 2:F], ps[:, MID[1], 0:F // 2], 0.0, None, ALU.max).then_inc(e_mid1, 1)
                        if not (isinstance(i, int) and i == 0):
                            scale(i - 1, j - 1)
                        dve.wait_ge(b_midt, 2 * i + 2)
                        dve.tensor_copy(midt[:, FC // 2:FC, :], ps[:, MT[1], 0:F // 2].rearrange("p (c m) -> p c m", m=128)
                                        ).then_inc(e_midt1, 1)

                    each_block(dve, half)
                    scale(BLOCKS - 1, BLOCKS - 1)


def kernel(**inputs):
    import numpy as _np
    import concourse.bacc as _bacc
    from concourse import mybir as _mybir
    from concourse.bass_utils import run_bass_kernel_spmd as _run

    f = {k: _np.ascontiguousarray(v) for k, v in inputs.items()}
    arrays = {"x": f["x"]}

    j = _np.arange(FRAME)
    window = 0.54 - 0.46 * _np.cos(2 * _np.pi * j / (FRAME - 1))
    turn = _np.outer(j, _np.arange(BINS)) % FRAME * (2 * _np.pi / FRAME)
    cs, sn = _np.cos(turn), _np.sin(turn)
    sn[:, 0] = 0.0
    sn[:, BINS - 1] = 0.0
    arrays["dft"] = (_np.concatenate([cs, sn], 1) * window[:, None]).astype(_np.float32)
    arrays["mel"] = _np.concatenate([f["L0_tok_mel_filters"].T] * 2, 0)
    arrays["dct"] = f["L0_tok_dct"]
    arrays["w_proj"] = f["L0_tok_w_proj"]
    arrays["b_proj"] = f["L0_tok_b_proj"].reshape(1, C)

    def two(v):
        v = v.reshape(C)
        return [v[:CA], _np.concatenate([v[CA:], v[CA:]])]

    arrays["chan"] = _np.stack(two(f["L0_attn_time_mix_v"]) + two(f["L0_attn_time_mix_k"]) + two(f["L0_attn_time_mix_r"])
                               + two(f["L0_attn_time_decay"]) + two(f["L0_attn_time_first"]) + two(f["L0_ffn_br1"]), 1)

    def stationary(w):
        t, p = w.T, _np.zeros((6, 128, 128), _np.float32)
        p[0] = t[:CA, :CA]
        p[1, :CB], p[2, CB:] = t[CA:, :CA], t[CA:, :CA]
        p[3, :, :CB], p[4, :, CB:] = t[:CA, CA:], t[:CA, CA:]
        p[5, :CB, :CB], p[5, CB:, CB:] = t[CA:, CA:], t[CA:, CA:]
        return p

    def moving(w):
        t, p = w.T, _np.zeros((3, 128, w.shape[0]), _np.float32)
        p[0], p[1, :CB], p[2, CB:] = t[:CA], t[CA:], t[CA:]
        return p.transpose(1, 0, 2)

    arrays["w4"] = _np.stack([stationary(f[n]) for n in ("L0_attn_Wv", "L0_attn_Wk", "L0_attn_Wr", "L0_ffn_Wr1")]
                             ).transpose(2, 0, 1, 3)
    arrays["wo"] = moving(f["L0_attn_Wo"])
    arrays["wr2"] = moving(f["L0_ffn_Wr2"])
    arrays["br2"] = _np.repeat(f["L0_ffn_br2"].reshape(1, E), ROWS, 0)
    w1t = f["L0_ffn_W1"].transpose(2, 0, 1)
    arrays["w1a"] = w1t[:CA]
    arrays["w1b"] = _np.concatenate([w1t[CA:], f["L0_ffn_b1"][None]], 0)
    arrays["w2"] = f["L0_ffn_W2"].transpose(2, 0, 1).reshape(FC, 128, E, C).transpose(1, 2, 0, 3)
    arrays["b2"] = f["L0_ffn_b2"].reshape(1, E, C)

    k = _np.zeros((128, 612 + ROWLEN), _np.float32)
    k[:, 0:128] = _np.eye(128)
    k[:, 128:256] = _np.triu(_np.ones((128, 128)), 1)
    k[:, 256:384] = 1.0
    k[:, 384] = _np.arange(128)
    k[:, 388:396] = _np.arange(E)
    k[:, 396:404] = _np.arange(E) * SLOTS
    k[:, 404:468] = _np.arange(64) * 128
    k[:, 468:468 + BLOCKS] = _np.arange(BLOCKS)
    k[:, 604:604 + G] = _np.arange(128)[:, None] + ROWS * _np.arange(G)
    k[:, 612 + TOKEN] = TOKENS + _np.arange(128)
    arrays["consts"] = k

    nc = _bacc.Bacc("TRN2", target_bir_lowering=False, num_devices=1)
    maps, args = {}, []
    for name, a in arrays.items():
        a = _np.ascontiguousarray(a)
        maps[f"in_{name}"] = a
        args.append(nc.dram_tensor(f"in_{name}", a.shape, _mybir.dt.from_np(a.dtype), kind="ExternalInput").ap())
    args.append(nc.dram_tensor("out_rows", (TOKENS + 128, C), F32, kind="ExternalOutput").ap())
    audio_tower(nc, *args)
    r = _run(nc, [maps], core_ids=[0])
    return r.results[0]["out_rows"][:TOKENS].reshape(STREAMS, FRAMES, C)
```

```python
from contextlib import ExitStack

import numpy as np

import concourse.bass as bass
from concourse import mybir

F32 = mybir.dt.float32
R32 = mybir.dt.float32r
U32 = mybir.dt.uint32
I32 = mybir.dt.int32
ALU = mybir.AluOpType
ACT = mybir.ActivationFunctionType
AX = mybir.AxisListType

STREAMS, SAMPLES = 16, 80000
FRAME, HOP = 100, 160
FRAMES = 1 + (SAMPLES - FRAME) // HOP
BINS = FRAME // 2 + 1
MELS, COEFS = 40, 13
C = 192
CA, CB = 128, C - 128
PAIRS = STREAMS // 2
ROWS = 125
TILES = FRAMES // ROWS
G = 2 * TILES
TOKENS = STREAMS * FRAMES
E, F = 8, 768
FC = F // 128
HEAD = 4
ROWLEN = HEAD + C
WEIGHT, TOKEN = 0, 1
CONSTS = 15
TABLE_STEPS = 16
SLOTS = TOKENS + 128
BLOCKS = (2 * TOKENS + E * 127) // 128
SPARE = E * SLOTS
ROWIN = ROWLEN + CB + 4
BIAS = E * (F + C) // 128
MIXED_COLS = -(-(6 * 3 * FRAMES + 3 * (FRAMES + 1) + G * C + 2 * FRAMES) // 8) * 8
WKV_COLS = -(-(7 * 3 * FRAMES + 3 * 3 * (FRAMES + 1) + 2 * FRAMES) // 8) * 8
LATE_COLS = E * (F + FC * C)
NEG = -1e38
LN_EXP = "natural_log_exp_and_others"
EPS = 1e-5


class Steps:

    def __init__(self, sem, names):
        self.sem, self.names = sem, names.split()

    def at(self, name, pair):
        return pair * len(self.names) + self.names.index(name) + 1

    def all(self, pairs):
        return pairs * len(self.names)


def wait(eng, sem, value):
    if not isinstance(value, int) or value > 0:
        eng.wait_ge(sem, value)


def before(eng, steps, pair):
    wait(eng, steps.sem, steps.all(pair))


def after(eng, steps, name, pair):
    if not isinstance(pair, int) or pair >= 0:
        eng.wait_ge(steps.sem, steps.at(name, pair))


def audio_tower(nc, x, dft, mel, dct, w_proj, b_proj, chan, w4, wo, wr2, br2, w1a, w1b, w2, bias, consts, out):
    slots = nc.dram_tensor("slots", (SPARE + 128, ROWLEN), F32, kind="Internal").ap()
    frames_v = x.rearrange("b (t q s) -> q (b t) s", q=ROWS, s=HOP)
    out_v = out[0:TOKENS, :].rearrange("(n q) c -> q n c", q=ROWS)

    with ExitStack() as top:
        def sem(name):
            return top.enter_context(nc.semaphore(name))

        def sb(ctx, name, shape, dt=F32):
            return ctx.enter_context(nc.sbuf_tensor(name, shape, dt))

        ps = top.enter_context(nc.psum_tensor("ps", [128, 8, 512], F32))

        def alone(eng):
            eng.sem_inc(passed, 1)

        ident = sb(top, "ident", [128, 128])
        expert_of = sb(top, "expert_of", [1, BLOCKS], I32)
        slot_of = sb(top, "slot_of", [1, BLOCKS], I32)

        weights_in = sem("weights_in")
        later_in = sem("later_in")
        consts_set = sem("consts_set")
        passed = sem("passed")
        g_prod, g_set = sem("g_prod"), sem("g_set")
        frames_in = sem("frames_in")
        rows_out = sem("rows_out")
        scattered = [sem("scattered_first"), sem("scattered_second")]
        filled = sem("filled")
        counted, tables, fill_pos = sem("counted"), sem("tables"), sem("fill_pos")
        frame_pe = Steps(sem("frame_pe"), "frames0 frames1 dft0 dft1")
        frame_act = Steps(sem("frame_act"), "frames0 frames1 pow0 pow1")
        tok_pe = Steps(sem("tok_pe"), "mel0 mel1 h0 h1 h2 h3 xt0 xt1 xt2")
        tok_act = Steps(sem("tok_act"), "log0 log1 h0 h1 h2 h3 lnv rstd xt0 xt1 xt2")
        tok_vec = Steps(sem("tok_vec"), "stats aggr var n1 n2 rstd norm tails")
        mix_pool = Steps(sem("mix_pool"), "diff")
        mix_vec = Steps(sem("mix_vec"), "v k r")
        mix_pe = Steps(sem("mix_pe"), "v k r")
        mix_act = Steps(sem("mix_act"), "v k r")
        wkv_vec = Steps(sem("wkv_vec"), "max lead q_scan b2v p_scan aq den num newton1 newton2 z")
        wkv_act = Steps(sem("wkv_act"), "ea2 a2 eb2 b2 ea a eb b lnden rden")
        wkv_pool = Steps(sem("wkv_pool"), "ap bv sn")
        ao_pe = Steps(sem("ao_pe"), "o0 o1 o2 o3")
        rank_pe = Steps(sem("rank_pe"), "rank")
        att_pe = Steps(sem("att_pe"), "xt0 xt1 xt2 rh0 rh1 rh2 score")
        att_vec = Steps(sem("att_vec"), "h0 h1 h2 h3 stats aggr var n1 n2 rstd norm tails")
        att_act = Steps(sem("att_act"), "lnv rstd xt0 xt1 xt2 copy rh0 rh1 rh2 ex")
        raw_k, raw_r = sem("raw_k"), sem("raw_r")
        bias_split, bias_in = sem("bias_split"), sem("bias_in")
        hi_set, lo_set = sem("hi_set"), sem("lo_set")
        w1b_set = sem("w1b_set")
        block_in = [sem(f"block_in{n}") for n in range(4)]
        b_xt, b_mid, b_midt, b_y = sem("b_xt"), sem("b_mid"), sem("b_midt"), sem("b_y")
        e_dup, e_hi, e_lo, e_cross = (sem(n) for n in ("e_dup", "e_hi", "e_lo", "e_cross"))
        e_mid0, e_mid1, e_thi, e_tlo, e_y = (sem(n) for n in ("e_mid0", "e_mid1", "e_thi", "e_tlo", "e_y"))
        id_set, added = sem("id_set"), sem("added")
        rt_vec = Steps(sem("rt_vec"), "score top gap index indexf hot mask sums "
                       "sum rec w1 w2 ids carry pos pick slot posu")

        x_hi, x_lo = ([sb(top, f"x_{p}{n}", [128, 256], R32) for n in range(2)] for p in ("hi", "lo"))
        pick_b2 = sb(top, "pick_b2", [CB + 4, 128], R32)
        ids = [sb(top, f"ids{n}", [128, 1], U32) for n in range(2)]
        bias_s = sb(top, "bias_s", [128, BIAS])
        bias_hi, bias_lo = (sb(top, n, [128, BIAS], R32) for n in ("bias_hi", "bias_lo"))
        chan_s = sb(top, "chan_s", [128, 12])

        with ExitStack() as ctx:
            region = {name: sb(ctx, name, [128, cols]) for name, cols in
                      (("mixed_cols", MIXED_COLS), ("wkv_cols", WKV_COLS), ("late_cols", LATE_COLS))}
            used = {name: 0 for name in region}

            def take(name, shape):
                size = int(np.prod(shape[1:]))
                at = used[name]
                used[name] = at + size
                assert used[name] <= region[name].shape[1]
                v = region[name][0:shape[0], at:at + size]
                if len(shape) == 2:
                    return v
                if len(shape) == 3:
                    return v.rearrange("p (a b) -> p a b", b=shape[2])
                return v.rearrange("p (a b c) -> p a b c", b=shape[2], c=shape[3])

            mixed = [take("mixed_cols", [128, 3, FRAMES]) for _ in "vkr"]
            xt = take("mixed_cols", [128, 3, FRAMES + 1])
            xn = take("mixed_cols", [ROWS, G, C])
            pw = take("mixed_cols", [2 * BINS, 2, FRAMES])
            ft = pw[0:FRAME, :, :]
            vs, ks, sig = ([take("mixed_cols", [128, 3, FRAMES]), take("wkv_cols", [128, 3, FRAMES])] for _ in "vkr")
            le = take("wkv_cols", [64, 2, FRAMES])
            om, pp, qq = (take("wkv_cols", [128, 3, FRAMES + 1]) for _ in range(3))
            a2, b2_, a1, b1_ = (take("wkv_cols", [128, 3, FRAMES]) for _ in range(4))
            w4_s = take("late_cols", [128, 4, 6, 128])
            wo_s = take("late_cols", [128, 3, C])
            fr = take("late_cols", [ROWS, G, FRAME])
            tails1 = take("late_cols", [ROWS, TILES, 2, CB])
            tails2 = take("late_cols", [ROWS, TILES, 2, CB])
            dft_s = take("late_cols", [FRAME, 2 * BINS])
            mel_s = take("late_cols", [2 * BINS, MELS])
            dct_s = take("late_cols", [COEFS, MELS])
            wproj_s = take("late_cols", [COEFS, C])
            proj_s = take("late_cols", [MELS + 1, C])
            before_s = take("late_cols", [ROWS, ROWS])
            h = take("late_cols", [ROWS, 3, G * C]).rearrange("q s (g c) -> q s g c", c=C)
            x2t = take("late_cols", [128, 3, FRAMES])
            z = take("late_cols", [128, 3, FRAMES])
            diff = take("late_cols", [128, 3, FRAMES])
            rows_s = sb(ctx, "rows_s", [128, 2 * G * ROWLEN])
            xrow = rows_s[0:ROWS, :].rearrange("q (k g c) -> q k g c", k=2, g=G)
            neg_s = sb(ctx, "neg_s", [128, 4])
            wr2_s = sb(ctx, "wr2_s", [128, 3, E])
            br2_s = sb(ctx, "br2_s", [ROWS, E])
            ones_s = sb(ctx, "ones_s", [ROWS, 128])
            eidx_s = sb(ctx, "eidx_s", [128, E])
            ebase_s = sb(ctx, "ebase_s", [128, E])
            wide_s = sb(ctx, "wide_s", [1, 64 + BLOCKS])
            eps_s = sb(ctx, "eps_s", [128, 2])
            fill_s = sb(ctx, "fill_s", [128, ROWLEN])

            st1 = sb(ctx, "st1", [ROWS, G, 6])
            mv1 = sb(ctx, "mv1", [ROWS, G, 2])
            nw1 = sb(ctx, "nw1", [ROWS, 5, G])
            st2 = sb(ctx, "st2", [ROWS, G, 6])
            mv2 = sb(ctx, "mv2", [ROWS, G, 2])
            nw2 = sb(ctx, "nw2", [ROWS, 5, G])
            rh = diff
            score = sb(ctx, "score", [ROWS, G, E])
            top8 = sb(ctx, "top8", [ROWS, G, E])
            idx8 = sb(ctx, "idx8", [ROWS, G, E], U32)
            idxf = sb(ctx, "idxf", [ROWS, G, 2])
            hot = sb(ctx, "hot", [ROWS, 2, G, E])
            mask = sb(ctx, "mask", [ROWS, E, G])
            carry = sb(ctx, "carry", [ROWS, E])
            sums, anew = (sb(ctx, n, [ROWS, E, G]) for n in ("sums", "anew"))
            tmp = sb(ctx, "tmp", [ROWS, 4, G])
            where = sb(ctx, "where", [ROWS, G, E])
            pick = sb(ctx, "pick", [ROWS, 2, G, E])
            posf = sb(ctx, "posf", [ROWS, 2, G])
            posu = sb(ctx, "posu", [ROWS, 2, G], U32)
            tok_id = sb(ctx, "tok_id", [ROWS, G])
            cnt = sb(ctx, "cnt", [1, E])
            fill_first = sb(ctx, "fill_first", [1, E], I32)
            gt = sb(ctx, "gt", [1, E, 64])
            nt = sb(ctx, "nt", [1, 4, E])
            def scratch(buf, n, inner):
                return buf[0:1, :, :].rearrange("p a b -> p (a b)")[:, 0:n * inner].rearrange("p (n i) -> p n i", i=inner)

            past, past2, tabf = scratch(x2t, BLOCKS, E), scratch(z, BLOCKS, E), scratch(diff, 4, BLOCKS)

        with ExitStack() as ctx:
            w1a_lo = sb(ctx, "w1a_lo", [128, E, F], R32)
            w1b_hl = sb(ctx, "w1b_hl", [128, E, F], R32)
            xb = [sb(ctx, f"xb{n}", [128, ROWIN]) for n in range(2)]
            sb(ctx, "gap0", [128, MIXED_COLS - 2 * E * F - 2 * ROWIN])
            w1b_hb = sb(ctx, "w1b_hb", [128, E, F], R32)
            b2_rows = w1b_hb[:, 0:E * C // F, :].rearrange("p a b -> p (a b)").rearrange("p (e d) -> p e d", d=C)
            xb += [sb(ctx, f"xb{n}", [128, ROWIN]) for n in range(2, 4)]
            sb(ctx, "gap1", [128, WKV_COLS - E * F - 2 * ROWIN - E * FC * C])
            w2_s = sb(ctx, "w2_s", [128, 2, E, FC, C], R32)
            w2_lo, w2_hi = w2_s[:, 0, :, :, :], w2_s[:, 1, :, :, :]
            w1a_hi = sb(ctx, "w1a_hi", [128, E, F], R32)
            mid = sb(ctx, "mid", [128, F])
            midt_hi, midt_lo = (sb(ctx, n, [128, FC, 128], R32) for n in ("midt_hi", "midt_lo"))
            yb = [sb(ctx, f"yb{n}", [128, C]) for n in range(2)]
            y_lo = sb(ctx, "y_lo", [128, C])

            MIX = {"v": 0, "k": 1, "r": 2}
            MU = {"v": 0, "k": 2, "r": 4}
            DECAY, FIRST, BR1 = 6, 8, 10

            def blockcols(t, col):
                return t[:, col:col + 1], t[:, col + 1:col + 2]

            def hslot(p, g, n=0):
                if isinstance(p, int):
                    return h[:, p % 3, g:g + n, :] if n else h[:, p % 3, g, :]
                v = h[:, bass.ds(p % 3, 1), g:g + max(n, 1), :]
                return v.rearrange("q o g c -> q (o g) c") if n else v.rearrange("q o g c -> q (o g c)")

            LOADS = [(ident[:, :], consts[:, 0:128]), (before_s[:, :], consts[0:ROWS, 128:128 + ROWS]),
                     (ones_s[:, :], consts[0:ROWS, 256:384]), (eidx_s[:, :], consts[:, 388:396]), (ebase_s[:, :], consts[:, 396:404]),
                     (wide_s[:, :], consts[0:1, 404:404 + 64 + BLOCKS]),
                     (tok_id[:, :], consts[0:ROWS, 604:604 + G]), (fill_s[:, :], consts[:, 612:612 + ROWLEN]),
                     (dft_s[:, :], dft), (mel_s[:, :], mel), (dct_s[:, :], dct), (wproj_s[:, :], w_proj),
                     (proj_s[MELS:MELS + 1, :], b_proj), (chan_s[:, :], chan), (bias_s[:, :], bias)]
            LATER = [(w4_s[:, :, :, :], w4), (wo_s[:, :, :], wo), (wr2_s[:, :, :], wr2), (br2_s[:, :], br2)]
            LOADED = 16 * len(LOADS)

            O_BANKS = (6, 7, 3, 5)
            XT, MID, MT, Y = 0, (1, 2), (3, 4), 5
            UN = 4
            LONG = 3
            PASSES = (BLOCKS // UN - 2) // LONG
            assert BLOCKS % UN == 0

            def each_stretch(eng, stretch):
                stretch(0, UN)
                with eng.Fori(0, PASSES) as m:
                    stretch(m * LONG + 1, LONG * UN)
                stretch(PASSES * LONG + 1, BLOCKS - UN - PASSES * LONG * UN)

            def each_block(eng, work):
                def stretch(n, count):
                    for j in range(count):
                        work(j % UN, n + j // UN)

                each_stretch(eng, stretch)

            def there(i):
                return not isinstance(i, int) or 0 <= i < BLOCKS

            def each_turn(eng, body):
                body(-2, 0, "F")
                body(-1, 1, "FT")
                body(0, 0, "FTK")
                body(1, 1, "FTKR")
                body(2, 0, "FTKRO")
                with eng.Fori(0, (PAIRS - 4) // 2) as n:
                    body(2 * n + 3, 1, "FTKRO")
                    body(2 * n + 4, 0, "FTKRO")
                body(PAIRS - 1, 1, "KRO")
                body(PAIRS, 0, "RO")
                body(PAIRS + 1, 1, "O")

            with nc.Block() as block:
                @block.sync
                def _(sp):
                    def load_frames(p):
                        after(sp, frame_pe, "frames1", p - 1)
                        q = PAIRS - 1 if isinstance(p, int) and p == PAIRS else p
                        sp.dma_start(fr[:, :, :], frames_v[:, bass.ds(q * G, G), 0:FRAME]).then_inc(frames_in, 16)

                    def store_rows(p):
                        wait(sp, rows_out, 16 * p)
                        after(sp, att_vec, "h3", p)
                        sp.dma_start(out_v[:, bass.ds(p * G, G), :], hslot(p, 0, G)).then_inc(rows_out, 16)

                    load_frames(0)
                    for dst, src in LOADS:
                        sp.dma_start(dst, src).then_inc(weights_in, 16)
                    for dst, src in LATER:
                        sp.dma_start(dst, src).then_inc(later_in, 16)
                    for p in range(1, 4):
                        load_frames(p)
                    store_rows(0)
                    with sp.Fori(1, PAIRS - 3) as i:
                        load_frames(i + 3)
                        store_rows(i)
                    load_frames(PAIRS)
                    store_rows(PAIRS - 3)
                    sp.wait_ge(mix_pe.sem, mix_pe.all(PAIRS))
                    sp.wait_ge(tok_pe.sem, tok_pe.all(PAIRS))
                    sp.wait_ge(frame_act.sem, frame_act.all(PAIRS + 1))
                    sp.wait_ge(wkv_vec.sem, wkv_vec.all(PAIRS - 1))
                    for e in range(0, E, 2):
                        sp.dma_start(w1b_hl[:, e:e + 2, :].bitcast(F32), w1b[:, e:e + 2, :]).then_inc(raw_k, 16)
                    for e in range(0, E, 2):
                        sp.dma_start(w1a_lo[:, e:e + 2, :].bitcast(F32), w1a[:, e:e + 2, :]).then_inc(raw_k, 16)
                    store_rows(PAIRS - 2)
                    sp.wait_ge(wkv_vec.sem, wkv_vec.all(PAIRS))
                    for e in range(0, E, 2):
                        sp.dma_start(w2_lo[:, e:e + 2, :, :].bitcast(F32), w2[:, e:e + 2, :, :]).then_inc(raw_r, 16)
                    store_rows(PAIRS - 1)
                    sp.dma_start(slots[SPARE:SPARE + 128, :], fill_s[:, :]).then_inc(filled, 16)
                    sp.wait_ge(fill_pos, 1)
                    with sp.Fori(0, E) as e:
                        first = sp.value_load(fill_first[0:1, bass.ds(e, 1)], min_val=0, max_val=SPARE - 128)
                        sp.dma_start(slots[bass.ds(first, 128), :], fill_s[:, :]).then_inc(filled, 16)

                    sp.wait_ge(lo_set, 2)
                    sp.wait_ge(bias_split, 2)
                    for n, part in enumerate((bias_hi, bias_lo)):
                        sp.dma_start(w1b_hb[CB + n:CB + n + 1, :, :].bitcast(F32), part[:, 0:E * F // 128].bitcast(F32)).then_inc(bias_in, 16)
                        sp.dma_start(b2_rows[CB + 2 + n:CB + 3 + n, :, :].bitcast(F32), part[:, E * F // 128:BIAS].bitcast(F32)).then_inc(bias_in, 16)
                    sp.wait_ge(rows_out, 16 * PAIRS)

                    sp.wait_ge(filled, 16 * (E + 1))
                    for k in range(2):
                        sp.wait_ge(scattered[k], 16 * G * PAIRS)
                    sp.wait_ge(tables, TABLE_STEPS)

                    def load(j, n):
                        i = n * UN + j
                        wait(sp, e_y, i - 3)
                        wait(sp, id_set, i - 3)
                        first = sp.value_load(slot_of[0:1, bass.ds(i, 1)], min_val=0, max_val=SPARE)
                        sp.dma_start(xb[j][:, 0:ROWLEN], slots[bass.ds(first, 128), :]).then_inc(block_in[j], 16)

                    each_block(sp, load)
                    sp.wait_ge(added, 16 * BLOCKS)

                @block.tensor
                def _(pe):
                    def transposes(src, tails, steps, banks):
                        for n, b in enumerate(banks):
                            for t in range(TILES):
                                piece = src[:, n * TILES + t, 0:CA] if n < 2 else tails[:, t, :, :]
                                mm = pe.transpose(ps[:, b, t * ROWS:(t + 1) * ROWS], piece, ident[0:ROWS, 0:ROWS])
                            mm.then_inc(steps.sem, 1)

                    def project(w, src, banks):
                        mms = []
                        for n, b in enumerate(banks):
                            parts = ((0, n), (1 + n, 2)) if n < 2 else ((3, 0), (4, 1), (5, 2))
                            for k, (piece, blk) in enumerate(parts):
                                mm = pe.matmul(ps[:, b, 0:FRAMES], w4_s[:, w, piece, :], src[:, blk, :],
                                               start=(k == 0), stop=(k == len(parts) - 1))
                            mms.append(mm)
                        return mms

                    def rank(o):
                        after(pe, rt_vec, "mask", o)
                        dst = ps[0:ROWS, 4, G * E:2 * G * E]
                        pe.matmul(dst, before_s[:, :], mask[:, :, :].rearrange("q e g -> q g e"), start=True, stop=False)
                        after(pe, rt_vec, "sums", o)
                        pe.matmul(dst[:, E:], ones_s[:, 0:ROWS], sums[:, :, 0:G - 1].rearrange("q e g -> q g e"),
                                  start=False, stop=False)
                        pe.matmul(dst, ones_s[:, 0:ROWS], carry[:, :].unsqueeze(1).to_broadcast([ROWS, G, E]),
                                  start=False, stop=True).then_inc(rank_pe.sem, 1)

                    def body(i, par, stages):
                        f, t, k, o = i + 2, i + 1, i, i - 2
                        frames_too, T, K, O = (c in stages for c in "FTKO")
                        if O:
                            if isinstance(i, int) and i >= PAIRS:
                                after(pe, att_act, "rh2", o - 1)
                            else:
                                after(pe, frame_act, "pow1", i + 1)
                            after(pe, wkv_vec, "z", o)
                            for n, b in enumerate(O_BANKS):
                                for g in (2 * n, 2 * n + 1):
                                    s, c = divmod(g, TILES)
                                    dst, cols = ps[0:ROWS, b, (g % 2) * C:(g % 2 + 1) * C], slice(c * ROWS, (c + 1) * ROWS)
                                    pe.matmul(dst, z[:, s, cols], wo_s[:, 0, :], start=True, stop=False)
                                    mm = pe.matmul(dst, z[:, 2, cols], wo_s[:, 1 + s, :], start=False, stop=True)
                                mm.then_inc(ao_pe.sem, 1)
                            if not (isinstance(o, int) and o == 0):
                                rank(o - 1)
                        if K and isinstance(k, int) and k == 0:
                            pe.wait_ge(later_in, 16 * len(LATER))
                        if K:
                            after(pe, mix_act, "r", k - 1)
                            after(pe, tok_act, "xt2", k)
                            after(pe, mix_vec, "v", k)
                            project(0, mixed[0], (0, 1, 2))[-1].then_inc(mix_pe.sem, 1)
                        if T:
                            if O:
                                after(pe, att_vec, "h1", o)
                            for s in range(2):
                                after(pe, frame_act, f"pow{s}", t)
                                pe.matmul(ps[0:MELS, 6 + s, 0:FRAMES], mel_s[:, :], pw[:, s, :],
                                          start=True, stop=True).then_inc(tok_pe.sem, 1)
                        if K:
                            after(pe, mix_act, "k", k - 1)
                            if O:
                                after(pe, att_vec, "h3", o)
                                after(pe, rt_vec, "pos", o - 1)
                            after(pe, mix_vec, "k", k)
                            project(1, mixed[1], (3, 4, 5))[-1].then_inc(mix_pe.sem, 1)
                        if T:
                            if K:
                                after(pe, mix_act, "v", k)
                            after(pe, tok_act, "log1", t)
                            for n, b in enumerate((6, 7, 0, 1)):
                                for g in (2 * n, 2 * n + 1):
                                    c = g % TILES
                                    mm = pe.matmul(ps[0:ROWS, b, (g % 2) * C:(g % 2 + 1) * C],
                                                   le[0:MELS + 1, n // 2, c * ROWS:(c + 1) * ROWS],
                                                   proj_s[:, :], start=True, stop=True)
                                mm.then_inc(tok_pe.sem, 1)
                        if O:
                            if K:
                                after(pe, mix_act, "k", k)
                            else:
                                after(pe, rt_vec, "pos", o - 1)
                            after(pe, att_vec, "tails", o)
                            transposes(xrow[:, 0, :, HEAD:ROWLEN], tails2, att_pe, (3, 4, 5))
                        if K:
                            after(pe, mix_act, "v", k)
                            if T:
                                after(pe, tok_act, "h3", t)
                            after(pe, mix_vec, "r", k)
                            project(2, mixed[2], (0, 1, 2))[-1].then_inc(mix_pe.sem, 1)
                        if O:
                            if T:
                                after(pe, tok_act, "h3", t)
                            after(pe, att_act, "xt2", o)
                            for mm in project(3, x2t, (6, 7, 3)):
                                mm.then_inc(att_pe.sem, 1)
                        if T:
                            after(pe, mix_act, "r", k)
                            after(pe, tok_vec, "tails", t)
                            transposes(xn, tails1, tok_pe, (0, 1, 2))
                        if frames_too:
                            pe.wait_ge(frames_in, 16 * (f + 1))
                            if T:
                                after(pe, tok_act, "h3", t)
                            if O:
                                after(pe, att_act, "rh1", o)
                            for s in range(2):
                                for c in range(TILES):
                                    mm = pe.transpose(ps[0:FRAME, 6 + s, c * ROWS:(c + 1) * ROWS],
                                                      fr[:, s * TILES + c, :], ident[0:ROWS, 0:ROWS])
                                mm.then_inc(frame_pe.sem, 1)
                        if O:
                            after(pe, att_act, "rh2", o)
                            for g in range(G):
                                s, c = divmod(g, TILES)
                                dst, cols = ps[0:ROWS, 4, g * E:(g + 1) * E], slice(c * ROWS, (c + 1) * ROWS)
                                pe.matmul(dst, rh[:, s, cols], wr2_s[:, 0, :], start=True, stop=False)
                                mm = pe.matmul(dst, rh[:, 2, cols], wr2_s[:, 1 + s, :], start=False, stop=True)
                            mm.then_inc(att_pe.sem, 1)
                        if frames_too:
                            if K:
                                after(pe, mix_act, "k", k)
                            if O:
                                after(pe, att_act, "rh2", o)
                            for s, b in enumerate((3, 5)):
                                after(pe, frame_act, f"frames{s}", f)
                                pe.matmul(ps[0:2 * BINS, b, 0:FRAMES], dft_s[:, :], ft[:, s, :],
                                          start=True, stop=True).then_inc(frame_pe.sem, 1)
                    pe.wait_ge(weights_in, LOADED)
                    pe.matmul(ps[0:MELS, 0, 0:C], dct_s[:, :], wproj_s[:, :], start=True, stop=True).then_inc(g_prod, 1)
                    pe.wait_ge(g_set, 1)
                    pe.wait_ge(consts_set, CONSTS)
                    each_turn(pe, body)
                    rank(PAIRS - 1)
                    pe.wait_ge(rt_vec.sem, rt_vec.all(PAIRS))
                    pe.matmul(ps[:, 0, 0:E], ones_s[:, :], carry[:, :], start=True, stop=True).then_inc(counted, 1)

                    def turn_in(j, n):
                        i = n * UN + j
                        pe.wait_ge(e_dup, i + 1)
                        wait(pe, e_hi, i)
                        wait(pe, e_lo, i)
                        pe.transpose(ps[:, XT, 0:128], xb[j][:, HEAD:HEAD + CA], ident[:, :])
                        pe.transpose(ps[:, XT, 128:256], xb[j][:, HEAD + CA:ROWLEN + CB], ident[:, :]).then_inc(b_xt, 1)

                    def up(j, n, e):
                        i = n * UN + j
                        xh, xl = x_hi[j % 2], x_lo[j % 2]
                        pe.wait_ge(e_hi, i + 1)
                        pe.wait_ge(e_lo, i + 1)
                        for half in range(2):
                            wait(pe, (e_mid0, e_mid1)[half], i)
                            dst, cols = ps[:, MID[half], 0:F // 2], slice(half * F // 2, (half + 1) * F // 2)
                            for k, (x_part, w_part) in enumerate((
                                    (xh[:, 0:128], w1a_hi), (xh[:, 0:128], w1a_lo), (xh[:, 128:256], w1b_hl),
                                    (xl[:, 0:128], w1a_hi), (xl[0:CB + 2, 128:256], w1b_hb[0:CB + 2, :, :]))):
                                mm = pe.matmul(dst, x_part, w_part[:, bass.ds(e, 1), cols], start=(k == 0), stop=(k == 4))
                            mm.then_inc(b_mid, 1)

                    def turn_mid(j, n):
                        i = n * UN + j
                        for half in range(2):
                            pe.wait_ge((e_mid0, e_mid1)[half], i + 1)
                            wait(pe, e_thi, 2 * i)
                            wait(pe, e_tlo, 2 * i)
                            for c in range(FC // 2):
                                mm = pe.transpose(ps[:, MT[half], c * 128:(c + 1) * 128],
                                                  mid[:, (half * FC // 2 + c) * 128:(half * FC // 2 + c + 1) * 128], ident[:, :])
                            mm.then_inc(b_midt, 1)

                    def down(j, n, e):
                        i = n * UN + j
                        wait(pe, e_y, i)
                        both, main = ps[:, Y, 0:2 * C], ps[:, Y, C:2 * C]
                        for half in range(2):
                            part = range(half * FC // 2, (half + 1) * FC // 2)
                            pe.wait_ge(e_thi, 2 * i + half + 1)
                            for c in part:
                                pe.matmul(both, midt_hi[:, c, :], w2_s[:, :, bass.ds(e, 1), c, :], start=(c == 0), stop=False)
                            pe.wait_ge(e_tlo, 2 * i + half + 1)
                            for c in part:
                                pe.matmul(main, midt_lo[:, c, :], w2_s[:, 1, bass.ds(e, 1), c, :], start=False, stop=False)
                        pe.matmul(main, pick_b2[:, :], b2_rows[0:CB + 4, bass.ds(e, 1), :], start=False, stop=True).then_inc(b_y, 1)

                    def turns(n, count):
                        experts = {}

                        def expert(j):
                            if j not in experts:
                                experts[j] = pe.value_load(expert_of[0:1, bass.ds(n * UN + j, 1)], min_val=0, max_val=E - 1)
                            return experts[j]

                        for j in range(count):
                            i = n * UN + j
                            before_e = expert(j - 1) if there(i - 1) else None
                            next_e = expert(j + 1) if there(i + 1) else None
                            if there(i + 1):
                                turn_in((j + 1) % UN, n + (j + 1) // UN)
                            if there(i - 1):
                                down((j - 1) % UN, n + (j - 1) // UN, before_e)
                            turn_mid(j, n)
                            if there(i + 1):
                                up((j + 1) % UN, n + (j + 1) // UN, next_e)

                    pe.wait_ge(tables, TABLE_STEPS)
                    pe.wait_ge(consts_set, CONSTS + 4)
                    pe.wait_ge(w1b_set, 2)
                    turn_in(0, 0)
                    pe.wait_ge(bias_in, 16 * 4)
                    pe.wait_ge(hi_set, 6)
                    pe.wait_ge(lo_set, 6)
                    up(0, 0, pe.value_load(expert_of[0:1, 0:1], min_val=0, max_val=E - 1))
                    each_stretch(pe, turns)
                    down(UN - 1, BLOCKS // UN - 1,
                         pe.value_load(expert_of[0:1, BLOCKS - 1:BLOCKS], min_val=0, max_val=E - 1))

                @block.scalar
                def _(act):
                    def rsqrt_seed(vec, steps, nw, p):
                        after(act, vec, "var", p)
                        act.activation(nw[:, 1, :], nw[:, 0, :], ACT.Ln).then_inc(steps.sem, 1)
                        after(act, steps, "lnv", p)
                        act.activation(nw[:, 2, :], nw[:, 1, :], ACT.Exp, scale=-0.5).then_inc(steps.sem, 1)

                    def clamped_exp(name, p, dst, sign, add):
                        act.activation(dst[:, 0:2, :], b1_[:, 0:2, :], ACT.Relu, scale=sign, bias=add[0])
                        act.activation(dst[:, 2, :], b1_[:, 2, :], ACT.Relu, scale=sign, bias=add[1]).then_inc(wkv_act.sem, 1)
                        after(act, wkv_act, "e" + name, p)
                        act.activation(dst[:, :, :], dst[:, :, :], ACT.Exp, scale=-1.0).then_inc(wkv_act.sem, 1)

                    def hidden(p, n, bank):
                        after(act, att_pe, f"rh{n}", p)
                        act.activation(rh[:, n, :], ps[:, bank, 0:FRAMES], ACT.Relu,
                                       bias=blockcols(chan_s, BR1)[n // 2]).then_inc(att_act.sem, 1)

                    def body(i, par, stages):
                        f, t, k, r, o = i + 2, i + 1, i, i - 1, i - 2
                        frames_too, T, K, R, O = (c in stages for c in "FTKRO")
                        if R:
                            after(act, wkv_vec, "lead", r)
                            clamped_exp("a2", r, a2, -1.0, blockcols(neg_s, 0))
                            clamped_exp("b2", r, b2_, 1.0, blockcols(chan_s, DECAY))
                        if O and not R:
                            act.wait_ge(raw_k, 16 * E)
                            act.wait_ge(wkv_vec.sem, wkv_vec.all(PAIRS))
                            for e in (0, E // 2):
                                act.activation(w1b_hb[:, e:e + E // 2, :], w1b_hl[:, e:e + E // 2, :].bitcast(F32),
                                               ACT.Copy).then_inc(hi_set, 1)
                        if K:
                            before(act, wkv_vec, k - 1)
                            after(act, mix_pe, "v", k)
                            act.activation(vs[par][:, :, :], ps[:, 0:3, 0:FRAMES], ACT.Copy).then_inc(mix_act.sem, 1)
                        if O:
                            rsqrt_seed(att_vec, att_act, nw2, o)
                        if T:
                            for s in range(2):
                                after(act, tok_pe, f"mel{s}", t)
                                act.activation(le[0:MELS, s, :], ps[0:MELS, 6 + s, 0:FRAMES], ACT.Ln,
                                               bias=eps_s[0:MELS, 0:1]).then_inc(tok_act.sem, 1)
                        if R:
                            clamped_exp("a", r, a1, -1.0, blockcols(chan_s, FIRST))
                        if K:
                            after(act, mix_pe, "k", k)
                            act.activation(ks[par][:, :, :], ps[:, 3:6, 0:FRAMES], ACT.Copy).then_inc(mix_act.sem, 1)
                        if T:
                            before(act, att_vec, t - 2)
                            wait(act, rows_out, 16 * (t - 2))
                            for n, b in enumerate((6, 7, 0, 1)):
                                after(act, tok_pe, f"h{n}", t)
                                act.activation(hslot(t, 2 * n, 2), ps[0:ROWS, b, 0:2 * C].rearrange("q (g c) -> q g c", g=2),
                                               ACT.Copy).then_inc(tok_act.sem, 1)
                        if O:
                            for n, b in enumerate((3, 4, 5)):
                                after(act, att_pe, f"xt{n}", o)
                                act.activation(x2t[:, n, :], ps[:, b, 0:FRAMES], ACT.Copy).then_inc(att_act.sem, 1)
                        if O:
                            after(act, att_vec, "norm", o)
                            wait(act, scattered[1], 16 * G * o)
                            act.activation(xrow[:, 1, :, HEAD:ROWLEN], xrow[:, 0, :, HEAD:ROWLEN], ACT.Copy).then_inc(att_act.sem, 1)
                        if T:
                            rsqrt_seed(tok_vec, tok_act, nw1, t)
                        if R:
                            clamped_exp("b", r, b1_, 1.0, blockcols(neg_s, 2))
                        if K:
                            after(act, mix_pe, "r", k)
                            act.activation(sig[par][:, :, :], ps[:, 0:3, 0:FRAMES], ACT.Sigmoid).then_inc(mix_act.sem, 1)
                            act.preload_act_table_set(LN_EXP)
                        if O:
                            if K:
                                after(act, mix_vec, "r", k)
                            hidden(o, 0, 6)
                            hidden(o, 1, 7)
                        if R:
                            after(act, wkv_vec, "den", r)
                            act.activation(b2_[:, :, :], a1[:, :, :], ACT.Ln).then_inc(wkv_act.sem, 1)
                        if O:
                            hidden(o, 2, 3)
                        if R:
                            after(act, wkv_act, "lnden", r)
                            act.activation(b2_[:, :, :], b2_[:, :, :], ACT.Exp, scale=-1.0).then_inc(wkv_act.sem, 1)
                        if T:
                            after(act, mix_vec, "r", t - 1)
                            for n, b in enumerate((0, 1, 2)):
                                after(act, tok_pe, f"xt{n}", t)
                                act.activation(xt[:, n, 1:FRAMES + 1], ps[:, b, 0:FRAMES], ACT.Copy).then_inc(tok_act.sem, 1)
                        if frames_too:
                            for s in range(2):
                                after(act, frame_pe, f"frames{s}", f)
                                act.activation(ft[:, s, :], ps[0:FRAME, 6 + s, 0:FRAMES], ACT.Copy).then_inc(frame_act.sem, 1)
                        if frames_too:
                            for s, b in enumerate((3, 5)):
                                after(act, frame_pe, f"dft{s}", f)
                                act.activation(pw[:, s, :], ps[0:2 * BINS, b, 0:FRAMES], ACT.Square).then_inc(frame_act.sem, 1)
                        if O:
                            after(act, rt_vec, "gap", o)
                            act.activation(tmp[:, 1, :], tmp[:, 0, :], ACT.Exp).then_inc(att_act.sem, 1)

                    act.preload_act_table_set(LN_EXP)
                    act.wait_ge(g_prod, 1)
                    act.activation(proj_s[0:MELS, :], ps[0:MELS, 0, 0:C], ACT.Copy).then_inc(g_set, 1)
                    act.wait_ge(consts_set, CONSTS)
                    act.activation(bias_hi[:, :], bias_s[:, :], ACT.Copy).then_inc(bias_split, 1)
                    each_turn(act, body)

                    act.wait_ge(rank_pe.sem, rank_pe.all(PAIRS))
                    act.wait_ge(rows_out, 16 * PAIRS)
                    act.wait_ge(raw_r, 16 * E // 2)
                    for e in (0, E // 2):
                        act.activation(w2_hi[:, e:e + E // 2, :, :], w2_lo[:, e:e + E // 2, :, :].bitcast(F32),
                                       ACT.Copy).then_inc(hi_set, 1)
                    act.wait_ge(att_vec.sem, att_vec.all(PAIRS))
                    act.wait_ge(tables, TABLE_STEPS)
                    for e in (0, E // 2):
                        act.activation(w1a_hi[:, e:e + E // 2, :], w1a_lo[:, e:e + E // 2, :].bitcast(F32),
                                       ACT.Copy).then_inc(hi_set, 1)

                    def dup(j, n):
                        i = n * UN + j
                        act.wait_ge(block_in[j], 16 * (n + 1))
                        act.activation(xb[j][:, ROWLEN:ROWLEN + CB], xb[j][:, ROWLEN - CB:ROWLEN], ACT.Copy).then_inc(e_dup, 1)

                    def rows_hi(j, n):
                        i = n * UN + j
                        act.wait_ge(b_xt, i + 1)
                        wait(act, b_mid, 2 * (i - 1))
                        act.activation(x_hi[j % 2][:, :], ps[:, XT, 0:256], ACT.Copy).then_inc(e_hi, 1)

                    def cross(j, n):
                        i = n * UN + j
                        act.wait_ge(b_y, i + 1)
                        wait(act, e_y, i)
                        act.activation(y_lo[:, :], ps[:, Y, 0:C], ACT.Copy, scale=xb[j][:, WEIGHT:WEIGHT + 1]).then_inc(e_cross, 1)

                    def turn(j, n):
                        i = n * UN + j
                        act.wait_ge(b_mid, 2 * i + 1)
                        wait(act, b_midt, 2 * i)
                        act.activation(mid[:, 0:F // 2], ps[:, MID[0], 0:F // 2], ACT.Relu).then_inc(e_mid0, 1)
                        if there(i + 1):
                            rows_hi((j + 1) % UN, n + (j + 1) // UN)
                        for half in range(2):
                            act.wait_ge(b_midt, 2 * i + half + 1)
                            wait(act, b_y, i)
                            act.activation(midt_hi[:, half * FC // 2:(half + 1) * FC // 2, :],
                                           ps[:, MT[half], 0:F // 2].rearrange("p (c m) -> p c m", m=128),
                                           ACT.Copy).then_inc(e_thi, 1)
                        if there(i - 1):
                            cross((j - 1) % UN, n + (j - 1) // UN)
                        if there(i + 2):
                            dup((j + 2) % UN, n + (j + 2) // UN)

                    dup(0, 0)
                    dup(1, 0)
                    rows_hi(0, 0)
                    each_block(act, turn)
                    cross(UN - 1, BLOCKS // UN - 1)

                @block.gpsimd
                def _(pool):
                    def scatter(p):
                        pool.wait_ge(rt_vec.sem, rt_vec.at("posu", p))
                        pool.wait_ge(att_act.sem, att_act.at("copy", p))
                        alone(pool)
                        for k in range(2):
                            for g in range(G):
                                pool.indirect_dma_start(
                                    out=slots, out_offset=bass.IndirectOffsetOnAxis(posu[:, k, g:g + 1], 0),
                                    in_=xrow[:, k, g, :], in_offset=None, bounds_check=SPARE + 127,
                                    oob_is_err=True, compute_op=ALU.bypass).then_inc(scattered[k], 16)

                    def body(i, par, stages):
                        t, r, v, gate = i + 1, i - 1, vs[1 - par], sig[1 - par]
                        T, R, O = (c in stages for c in "TRO")
                        if O and not (isinstance(i, int) and i == 2):
                            scatter(i - 3)
                        if R:
                            after(pool, wkv_vec, "p_scan", r)
                            after(pool, wkv_act, "a", r)
                            pool.tensor_tensor(a2[:, :, :], a1[:, :, :], pp[:, :, 0:FRAMES], ALU.mult).then_inc(wkv_pool.sem, 1)
                            after(pool, wkv_vec, "aq", r)
                            after(pool, wkv_act, "b", r)
                            pool.tensor_tensor(qq[:, :, 1:], b1_[:, :, :], v[:, :, :], ALU.mult).then_inc(wkv_pool.sem, 1)
                            after(pool, wkv_vec, "num", r)
                            after(pool, mix_act, "r", r)
                            pool.tensor_tensor(b1_[:, :, :], a2[:, :, :], gate[:, :, :], ALU.mult).then_inc(wkv_pool.sem, 1)
                        if T:
                            after(pool, tok_act, "xt2", t)
                            after(pool, att_pe, "score", t - 3)
                            pool.tensor_tensor(diff[:, :, :], xt[:, :, 1:], xt[:, :, 0:FRAMES], ALU.subtract).then_inc(mix_pool.sem, 1)

                    pool.wait_ge(consts_set, CONSTS)
                    each_turn(pool, body)
                    scatter(PAIRS - 1)
                    for k in range(2):
                        pool.wait_ge(scattered[k], 16 * G * PAIRS)

                    def note(j, n):
                        pool.wait_ge(block_in[j], 16 * (n + 1))
                        alone(pool)
                        pool.tensor_copy(ids[j % 2][:, :], xb[j][:, TOKEN:TOKEN + 1]).then_inc(id_set, 1)

                    def add(j, n):
                        i = n * UN + j
                        pool.wait_ge(e_y, i + 1)
                        pool.wait_ge(id_set, i + 1)
                        alone(pool)
                        pool.indirect_dma_start(
                            out=out, out_offset=bass.IndirectOffsetOnAxis(ids[j % 2][:, 0:1], 0), in_=yb[j % 2][:, :],
                            in_offset=None, bounds_check=TOKENS + 127, oob_is_err=True,
                            compute_op=ALU.add).then_inc(added, 16)
                        if there(i + 1):
                            note((j + 1) % UN, n + (j + 1) // UN)
                        pool.wait_ge(added, 16 * (i + 1))

                    note(0, 0)
                    pool.wait_ge(rows_out, 16 * PAIRS)
                    each_block(pool, add)

                @block.vector
                def _(dve):
                    def row_stats(p, st, mv, nw, steps):
                        alone(dve)
                        for g in range(G):
                            mm = dve.bn_stats(st[:, g, :], hslot(p, g))
                        mm.then_inc(steps.sem, 1)
                        after(dve, steps, "stats", p)
                        alone(dve)
                        for g in range(G):
                            mm = dve.bn_aggr(mv[:, g, :], st[:, g, :])
                        mm.then_inc(steps.sem, 1)
                        after(dve, steps, "aggr", p)
                        dve.tensor_scalar(nw[:, 0, :], mv[:, :, 1], EPS, None, ALU.add).then_inc(steps.sem, 1)

                    def row_norm(p, dst, tails, mv, nw, steps, act_steps):
                        after(dve, act_steps, "rstd", p)
                        dve.tensor_tensor(nw[:, 3, :], nw[:, 2, :], nw[:, 2, :], ALU.mult).then_inc(steps.sem, 1)
                        after(dve, steps, "n1", p)
                        dve.scalar_tensor_tensor(nw[:, 3, :], nw[:, 3, :], -0.5, nw[:, 0, :], ALU.mult, ALU.mult).then_inc(steps.sem, 1)
                        after(dve, steps, "n2", p)
                        dve.scalar_tensor_tensor(nw[:, 4, :], nw[:, 3, :], 1.5, nw[:, 2, :], ALU.add, ALU.mult).then_inc(steps.sem, 1)
                        after(dve, steps, "rstd", p)
                        for g in range(G):
                            mm = dve.tensor_scalar(dst[:, g, 0:C], hslot(p, g), mv[:, g, 0:1], nw[:, 4, g:g + 1],
                                                   ALU.subtract, ALU.mult)
                        mm.then_inc(steps.sem, 1)
                        after(dve, steps, "norm", p)
                        dve.tensor_copy(tails[:, :, :, :].rearrange("q t s c -> q s t c"),
                                        dst[:, :, CA:C].rearrange("q (s t) c -> q s t c", s=2)).then_inc(steps.sem, 1)

                    def mix(name, p):
                        m, (mu_a, mu_b) = mixed[MIX[name]], blockcols(chan_s, MU[name])
                        dve.scalar_tensor_tensor(m[:, 0:2, :], diff[:, 0:2, :], mu_a, xt[:, 0:2, 0:FRAMES], ALU.mult, ALU.add)
                        dve.scalar_tensor_tensor(m[:, 2, :], diff[:, 2, :], mu_b, xt[:, 2, 0:FRAMES],
                                                 ALU.mult, ALU.add).then_inc(mix_vec.sem, 1)

                    def running_max(p, k):
                        w = blockcols(chan_s, DECAY)
                        after(dve, mix_act, "k", p)
                        for n in range(3):
                            mm = dve.tensor_tensor_scan(om[:, n, 1:], w[n // 2].to_broadcast([128, FRAMES]), k[:, n, :],
                                                        NEG, ALU.add, ALU.max)
                        mm.then_inc(wkv_vec.sem, 1)

                    def lead(p, k):
                        after(dve, wkv_vec, "max", p)
                        dve.tensor_tensor(b1_[:, :, :], om[:, :, 0:FRAMES], k[:, :, :], ALU.subtract).then_inc(wkv_vec.sem, 1)
                        after(dve, wkv_vec, "lead", p)

                    def scan(p, dst, ready):
                        ready()
                        for n in range(3):
                            mm = dve.tensor_tensor_scan(dst[:, n, 1:], a2[:, n, :], b2_[:, n, :], 0.0, ALU.mult, ALU.add)
                        mm.then_inc(wkv_vec.sem, 1)

                    def a_q(p):
                        after(dve, wkv_act, "a", p)
                        after(dve, wkv_vec, "p_scan", p)
                        dve.tensor_tensor(b2_[:, :, :], a1[:, :, :], qq[:, :, 0:FRAMES], ALU.mult).then_inc(wkv_vec.sem, 1)

                    def denominator(p):
                        after(dve, wkv_vec, "aq", p)
                        after(dve, wkv_pool, "ap", p)
                        after(dve, wkv_act, "b", p)
                        dve.tensor_tensor(a1[:, :, :], b2_[:, :, :], b1_[:, :, :], ALU.add).then_inc(wkv_vec.sem, 1)

                    def numerator(p):
                        after(dve, wkv_pool, "bv", p)
                        dve.tensor_tensor(a2[:, :, :], a2[:, :, :], qq[:, :, 1:], ALU.add).then_inc(wkv_vec.sem, 1)

                    def newton1(p):
                        after(dve, wkv_act, "rden", p)
                        after(dve, ao_pe, "o3", p - 1)
                        dve.tensor_tensor(z[:, :, :], a1[:, :, :], b2_[:, :, :], ALU.mult).then_inc(wkv_vec.sem, 1)

                    def newton2(p):
                        after(dve, wkv_vec, "newton1", p)
                        dve.scalar_tensor_tensor(z[:, :, :], z[:, :, :], 2.0, b2_[:, :, :], ALU.subtract, ALU.mult).then_inc(wkv_vec.sem, 1)

                    def gated(p):
                        after(dve, wkv_vec, "newton2", p)
                        after(dve, wkv_pool, "sn", p)
                        dve.scalar_tensor_tensor(z[:, :, :], z[:, :, :], -1.0, b1_[:, :, :], ALU.mult, ALU.mult).then_inc(wkv_vec.sem, 1)

                    def add_attention(p):
                        for n, b in enumerate(O_BANKS):
                            after(dve, ao_pe, f"o{n}", p)
                            dve.tensor_tensor(hslot(p, 2 * n, 2), ps[0:ROWS, b, 0:2 * C].rearrange("q (g c) -> q g c", g=2),
                                              hslot(p, 2 * n, 2), ALU.add).then_inc(att_vec.sem, 1)

                    def done(name, p):
                        after(dve, rt_vec, name, p)

                    def top_two(p):
                        after(dve, att_pe, "score", p)
                        if isinstance(p, int) and p == 0:
                            dve.wait_ge(later_in, 16 * len(LATER))
                        dve.tensor_tensor(score[:, :, :], ps[0:ROWS, 4, 0:G * E].rearrange("q (g e) -> q g e", g=G),
                                          br2_s[:, :].unsqueeze(1).to_broadcast([ROWS, G, E]), ALU.add).then_inc(rt_vec.sem, 1)
                        done("score", p)
                        alone(dve)
                        for g in range(G):
                            mm = dve.max(top8[:, g, :], score[:, g, :])
                        mm.then_inc(rt_vec.sem, 1)

                    def their_experts(p):
                        done("top", p)
                        dve.tensor_tensor(tmp[:, 0, :], top8[:, :, 1], top8[:, :, 0], ALU.subtract).then_inc(rt_vec.sem, 1)
                        alone(dve)
                        for g in range(G):
                            mm = dve.max_index(idx8[:, g, :], top8[:, g, :], score[:, g, :])
                        mm.then_inc(rt_vec.sem, 1)

                    def as_numbers(p):
                        done("index", p)
                        dve.tensor_copy(idxf[:, :, :], idx8[:, :, 0:2]).then_inc(rt_vec.sem, 1)

                    def one_hot(p):
                        done("indexf", p)
                        for k in range(2):
                            mm = dve.tensor_tensor(hot[:, k, :, :], eidx_s[0:ROWS, :].unsqueeze(1).to_broadcast([ROWS, G, E]),
                                                   idxf[:, :, k:k + 1].to_broadcast([ROWS, G, E]), ALU.is_equal)
                        mm.then_inc(rt_vec.sem, 1)
                        done("hot", p)
                        dve.tensor_tensor(mask[:, :, :], hot[:, 0, :, :].rearrange("q g e -> q e g"), hot[:, 1, :, :].rearrange("q g e -> q e g"),
                                          ALU.add).then_inc(rt_vec.sem, 1)

                    def flat(buf):
                        return buf[:, :, :].rearrange("q e g -> q (e g)")

                    def count(p):
                        done("mask", p)
                        dve.tensor_tensor_scan(flat(sums), flat(anew), flat(mask), 0.0,
                                               ALU.mult, ALU.add).then_inc(rt_vec.sem, 1)

                    def weight_sum(p):
                        after(dve, att_act, "ex", p)
                        dve.tensor_scalar(tmp[:, 2, :], tmp[:, 1, :], 1.0, None, ALU.add).then_inc(rt_vec.sem, 1)

                    def weight_rec(p):
                        done("sum", p)
                        dve.reciprocal(tmp[:, 3, :], tmp[:, 2, :]).then_inc(rt_vec.sem, 1)

                    def label(p):
                        done("rec", p)
                        after(dve, att_act, "copy", p)
                        dve.tensor_copy(xrow[:, 0, :, WEIGHT], tmp[:, 3, :]).then_inc(rt_vec.sem, 1)
                        dve.tensor_tensor(xrow[:, 1, :, WEIGHT], tmp[:, 1, :], tmp[:, 3, :], ALU.mult).then_inc(rt_vec.sem, 1)
                        for k in range(2):
                            dve.tensor_copy(xrow[:, k, :, TOKEN], tok_id[:, :])
                        dve.tensor_scalar(tok_id[:, :], tok_id[:, :], float(G * ROWS), None, ALU.add).then_inc(rt_vec.sem, 1)
                        after(dve, rank_pe, "rank", p)
                        dve.tensor_tensor(carry[:, :], carry[:, :], sums[:, :, G - 1], ALU.add).then_inc(rt_vec.sem, 1)
                        dve.tensor_tensor(where[:, :, :], ps[0:ROWS, 4, G * E:2 * G * E].rearrange("q (g e) -> q g e", g=G),
                                          ebase_s[0:ROWS, :].unsqueeze(1).to_broadcast([ROWS, G, E]), ALU.add).then_inc(rt_vec.sem, 1)

                    def pick_slots(p):
                        done("pos", p)
                        dve.tensor_tensor(pick[:, :, :, :], hot[:, :, :, :], where[:, :, :].unsqueeze(1).to_broadcast([ROWS, 2, G, E]),
                                          ALU.mult).then_inc(rt_vec.sem, 1)
                        done("pick", p)
                        dve.tensor_reduce(posf[:, :, :], pick[:, :, :, :], AX.X, ALU.add).then_inc(rt_vec.sem, 1)
                        done("slot", p)
                        dve.tensor_copy(posu[:, :, :], posf[:, :, :]).then_inc(rt_vec.sem, 1)

                    def body(i, par, stages):
                        t, k, r, o = i + 1, i, i - 1, i - 2
                        T, K, R, O = (c in stages for c in "TKRO")
                        placing = O and not (isinstance(o, int) and o == 0)
                        if K:
                            after(dve, mix_pool, "diff", k)
                            after(dve, mix_pe, "r", k - 1)
                            mix("v", k)
                        if placing:
                            label(o - 1)
                            pick_slots(o - 1)
                        if O:
                            add_attention(o)
                        if O:
                            after(dve, att_vec, "h3", o)
                            row_stats(o, st2, mv2, nw2, att_vec)
                        if K:
                            mix("k", k)
                            mix("r", k)
                        if R:
                            scan(r, qq, lambda: after(dve, wkv_act, "b2", r))
                        if O:
                            wait(dve, scattered[0], 16 * G * o)
                            row_norm(o, xrow[:, 0, :, HEAD:ROWLEN], tails2, mv2, nw2, att_vec, att_act)
                        if O and not R:
                            for n, e in enumerate((0, E // 2)):
                                dve.wait_ge(hi_set, n + 1)
                                part = slice(e, e + E // 2)
                                dve.tensor_tensor(w1b_hl[CB:128, part, :], w1b_hl[CB:128, part, :].bitcast(F32),
                                                  w1b_hb[CB:128, part, :].bitcast(F32), ALU.subtract).then_inc(lo_set, 1)
                                dve.tensor_copy(w1b_hl[0:CB, part, :], w1b_hb[0:CB, part, :].bitcast(F32)).then_inc(w1b_set, 1)
                        if R:
                            after(dve, wkv_vec, "q_scan", r)
                            dve.tensor_tensor(b2_[:, :, :], b2_[:, :, :], vs[1 - par][:, :, :], ALU.mult).then_inc(wkv_vec.sem, 1)
                            scan(r, pp, lambda: after(dve, wkv_vec, "b2v", r))
                        if T:
                            after(dve, tok_act, "h3", t)
                            row_stats(t, st1, mv1, nw1, tok_vec)
                        if R:
                            a_q(r)
                        if T:
                            row_norm(t, xn, tails1, mv1, nw1, tok_vec, tok_act)
                        if R:
                            denominator(r)
                            numerator(r)
                            newton1(r)
                            newton2(r)
                            gated(r)
                        if O:
                            top_two(o)
                            their_experts(o)
                            as_numbers(o)
                            one_hot(o)
                            count(o)
                        if K:
                            running_max(k, ks[par])
                            lead(k, ks[par])
                        if O:
                            weight_sum(o)
                            weight_rec(o)
                    dve.memset(le[32:64, :, :], 1.0).then_inc(consts_set, 1)
                    dve.memset(xt[:, :, 0:1], 0.0).then_inc(consts_set, 1)
                    dve.memset(om[:, :, 0:1], NEG).then_inc(consts_set, 1)
                    dve.memset(pp[:, :, 0:1], 0.0).then_inc(consts_set, 1)
                    dve.memset(qq[:, :, 0:1], 0.0).then_inc(consts_set, 1)
                    dve.memset(carry[:, :], 0.0).then_inc(consts_set, 1)
                    dve.memset(anew[:, :, :], 1.0).then_inc(consts_set, 1)
                    dve.memset(eps_s[:, 0:1], 1e-6).then_inc(consts_set, 1)
                    dve.memset(xrow[:, 0, :, 0:HEAD], 1.0).then_inc(consts_set, 1)
                    dve.memset(xrow[:, 1, :, 0:HEAD], 1.0).then_inc(consts_set, 1)
                    dve.memset(eps_s[:, 1:2], EPS).then_inc(consts_set, 1)
                    dve.wait_ge(weights_in, LOADED)
                    dve.tensor_scalar(neg_s[:, :], chan_s[:, DECAY:FIRST + 2], -1.0, None, ALU.mult).then_inc(consts_set, 1)
                    dve.memset(gt[:, :, :], 0.0).then_inc(consts_set, 1)
                    dve.memset(pick_b2[0:CB, :].bitcast(F32), 0.0).then_inc(consts_set, 1)
                    dve.memset(pick_b2[CB:CB + 4, :].bitcast(F32), 1.0).then_inc(consts_set, 1)
                    dve.wait_ge(consts_set, CONSTS)
                    dve.memset(anew[:, :, 0:1], 0.0).then_inc(consts_set, 1)
                    dve.wait_ge(consts_set, CONSTS + 1)
                    for n in range(2):
                        dve.memset(x_lo[n][CB:CB + 2, 128:256].bitcast(F32), 1.0).then_inc(consts_set, 1)
                    dve.memset(pick_b2[CB:CB + 2, :].bitcast(F32), 0.0).then_inc(consts_set, 1)
                    dve.wait_ge(bias_split, 1)
                    dve.tensor_tensor(bias_lo[:, :], bias_s[:, :], bias_hi[:, :].bitcast(F32), ALU.subtract).then_inc(bias_split, 1)

                    each_turn(dve, body)
                    label(PAIRS - 1)
                    pick_slots(PAIRS - 1)

                    n_step = [0]

                    def chain(ins):
                        n_step[0] += 1
                        ins.then_inc(tables, 1)
                        dve.wait_ge(tables, n_step[0])

                    dve.wait_ge(counted, 1)
                    chain(dve.tensor_tensor(cnt[:, :], ps[0:1, 0, 0:E], ebase_s[0:1, :], ALU.add))
                    dve.tensor_copy(fill_first[:, :], cnt[:, :]).then_inc(fill_pos, 1)
                    chain(dve.tensor_copy(nt[:, 0, :], ps[0:1, 0, 0:E]))
                    chain(dve.tensor_tensor(gt[:, :, 0:63], nt[:, 0, :].unsqueeze(2).to_broadcast([1, E, 63]),
                                            wide_s[:, 0:63].unsqueeze(1).to_broadcast([1, E, 63]), ALU.is_gt))
                    chain(dve.tensor_reduce(nt[:, 1, :], gt[:, :, :], AX.X, ALU.add))
                    chain(dve.tensor_tensor_scan(nt[:, 2, :], ones_s[0:1, 0:E], nt[:, 1, :], 0.0, ALU.mult, ALU.add))
                    chain(dve.tensor_scalar(nt[:, 3, :], nt[:, 1, :], -128.0, float(SLOTS), ALU.mult, ALU.add))
                    chain(dve.tensor_tensor(past[:, :, :], wide_s[:, 64:64 + BLOCKS].unsqueeze(2).to_broadcast([1, BLOCKS, E]),
                                            nt[:, 2, :].unsqueeze(1).to_broadcast([1, BLOCKS, E]), ALU.is_ge))
                    chain(dve.tensor_tensor(past2[:, :, :], past[:, :, :],
                                            nt[:, 3, :].unsqueeze(1).to_broadcast([1, BLOCKS, E]), ALU.mult))
                    chain(dve.tensor_reduce(tabf[:, 0, :], past[:, :, :], AX.X, ALU.add))
                    chain(dve.tensor_reduce(tabf[:, 1, :], past2[:, :, :], AX.X, ALU.add))
                    chain(dve.tensor_scalar(tabf[:, 0, :], tabf[:, 0, :], float(E - 1), None, ALU.min))
                    chain(dve.tensor_scalar(tabf[:, 2, :], wide_s[:, 64:64 + BLOCKS], 128.0, None, ALU.mult))
                    chain(dve.tensor_tensor(tabf[:, 3, :], tabf[:, 1, :], tabf[:, 2, :], ALU.add))
                    chain(dve.tensor_scalar(tabf[:, 3, :], tabf[:, 3, :], float(SPARE), None, ALU.min))
                    chain(dve.tensor_copy(expert_of[:, 0:BLOCKS], tabf[:, 0, :]))
                    chain(dve.tensor_copy(slot_of[:, 0:BLOCKS], tabf[:, 3, :]))
                    assert n_step[0] == TABLE_STEPS

                    for n, (hi, lo) in enumerate((
                            (w2_hi[:, 0:E // 2, :, :], w2_lo[:, 0:E // 2, :, :]), (w2_hi[:, E // 2:, :, :], w2_lo[:, E // 2:, :, :]),
                            (w1a_hi[:, 0:E // 2, :], w1a_lo[:, 0:E // 2, :]), (w1a_hi[:, E // 2:, :], w1a_lo[:, E // 2:, :]))):
                        dve.wait_ge(hi_set, n + 3)
                        dve.tensor_tensor(lo, lo.bitcast(F32), hi.bitcast(F32), ALU.subtract).then_inc(lo_set, 1)

                    def rows_lo(j, n):
                        i = n * UN + j
                        hi, lo = x_hi[j % 2], x_lo[j % 2]
                        dve.wait_ge(e_hi, i + 1)
                        dve.tensor_tensor(lo[:, 0:128], ps[:, XT, 0:128], hi[:, 0:128].bitcast(F32), ALU.subtract)
                        dve.tensor_tensor(lo[0:CB, 128:256], ps[0:CB, XT, 128:256], hi[0:CB, 128:256].bitcast(F32),
                                          ALU.subtract).then_inc(e_lo, 1)

                    def scale(j, n):
                        i = n * UN + j
                        dve.wait_ge(e_cross, i + 1)
                        wait(dve, added, 16 * (i - 1))
                        dve.scalar_tensor_tensor(yb[j % 2][:, :], ps[:, Y, C:2 * C], xb[j][:, WEIGHT:WEIGHT + 1], y_lo[:, :],
                                                 ALU.mult, ALU.add).then_inc(e_y, 1)

                    def turn(j, n):
                        i = n * UN + j
                        dve.wait_ge(b_mid, 2 * i + 2)
                        wait(dve, b_midt, 2 * i)
                        dve.tensor_scalar(mid[:, F // 2:F], ps[:, MID[1], 0:F // 2], 0.0, None, ALU.max).then_inc(e_mid1, 1)
                        if there(i + 1):
                            rows_lo((j + 1) % UN, n + (j + 1) // UN)
                        if there(i - 1):
                            scale((j - 1) % UN, n + (j - 1) // UN)
                        for half in range(2):
                            part = slice(half * FC // 2, (half + 1) * FC // 2)
                            dve.wait_ge(e_thi, 2 * i + half + 1)
                            dve.tensor_tensor(midt_lo[:, part, :], ps[:, MT[half], 0:F // 2].rearrange("p (c m) -> p c m", m=128),
                                              midt_hi[:, part, :].bitcast(F32), ALU.subtract).then_inc(e_tlo, 1)

                    rows_lo(0, 0)
                    each_block(dve, turn)
                    scale(UN - 1, BLOCKS // UN - 1)


def kernel(**inputs):
    import numpy as _np
    import concourse.bacc as _bacc
    from concourse import mybir as _mybir
    from concourse.bass_utils import run_bass_kernel_spmd as _run

    f = {k: _np.ascontiguousarray(v) for k, v in inputs.items()}
    arrays = {"x": f["x"]}

    j = _np.arange(FRAME)
    window = 0.54 - 0.46 * _np.cos(2 * _np.pi * j / (FRAME - 1))
    turn = _np.outer(j, _np.arange(BINS)) % FRAME * (2 * _np.pi / FRAME)
    cs, sn = _np.cos(turn), _np.sin(turn)
    sn[:, 0] = 0.0
    sn[:, BINS - 1] = 0.0
    arrays["dft"] = (_np.concatenate([cs, sn], 1) * window[:, None]).astype(_np.float32)
    arrays["mel"] = _np.concatenate([f["L0_tok_mel_filters"].T] * 2, 0)
    arrays["dct"] = f["L0_tok_dct"]
    arrays["w_proj"] = f["L0_tok_w_proj"]
    arrays["b_proj"] = f["L0_tok_b_proj"].reshape(1, C)

    def two(v):
        v = v.reshape(C)
        return [v[:CA], _np.concatenate([v[CA:], v[CA:]])]

    arrays["chan"] = _np.stack(two(f["L0_attn_time_mix_v"]) + two(f["L0_attn_time_mix_k"]) + two(f["L0_attn_time_mix_r"])
                               + two(f["L0_attn_time_decay"]) + two(f["L0_attn_time_first"]) + two(f["L0_ffn_br1"]), 1)

    def stationary(w):
        t, p = w.T, _np.zeros((6, 128, 128), _np.float32)
        p[0] = t[:CA, :CA]
        p[1, :CB], p[2, CB:] = t[CA:, :CA], t[CA:, :CA]
        p[3, :, :CB], p[4, :, CB:] = t[:CA, CA:], t[:CA, CA:]
        p[5, :CB, :CB], p[5, CB:, CB:] = t[CA:, CA:], t[CA:, CA:]
        return p

    def moving(w):
        t, p = w.T, _np.zeros((3, 128, w.shape[0]), _np.float32)
        p[0], p[1, :CB], p[2, CB:] = t[:CA], t[CA:], t[CA:]
        return p.transpose(1, 0, 2)

    arrays["w4"] = _np.stack([stationary(f[n]) for n in ("L0_attn_Wv", "L0_attn_Wk", "L0_attn_Wr", "L0_ffn_Wr1")]
                             ).transpose(2, 0, 1, 3)
    arrays["wo"] = moving(f["L0_attn_Wo"])
    arrays["wr2"] = moving(f["L0_ffn_Wr2"])
    arrays["br2"] = _np.repeat(f["L0_ffn_br2"].reshape(1, E), ROWS, 0)
    w1t = f["L0_ffn_W1"].transpose(2, 0, 1)
    arrays["w1a"] = w1t[:CA]
    arrays["w1b"] = _np.concatenate([w1t[CA:], w1t[CA:]], 0)
    arrays["w2"] = f["L0_ffn_W2"].transpose(2, 0, 1).reshape(FC, 128, E, C).transpose(1, 2, 0, 3)
    arrays["bias"] = _np.concatenate([f["L0_ffn_b1"].reshape(128, E * F // 128), f["L0_ffn_b2"].reshape(128, E * C // 128)], 1)

    k = _np.zeros((128, 612 + ROWLEN), _np.float32)
    k[:, 0:128] = _np.eye(128)
    k[:, 128:256] = _np.triu(_np.ones((128, 128)), 1)
    k[:, 256:384] = 1.0
    k[:, 388:396] = _np.arange(E)
    k[:, 396:404] = _np.arange(E) * SLOTS
    k[:, 404:468] = _np.arange(64) * 128
    k[:, 468:468 + BLOCKS] = _np.arange(BLOCKS)
    k[:, 604:604 + G] = _np.arange(128)[:, None] + ROWS * _np.arange(G)
    k[:, 612 + TOKEN] = TOKENS + _np.arange(128)
    arrays["consts"] = k

    nc = _bacc.Bacc("TRN2", target_bir_lowering=False, num_devices=1)
    maps, args = {}, []
    for name, a in arrays.items():
        a = _np.ascontiguousarray(a)
        maps[f"in_{name}"] = a
        args.append(nc.dram_tensor(f"in_{name}", a.shape, _mybir.dt.from_np(a.dtype), kind="ExternalInput").ap())
    args.append(nc.dram_tensor("out_rows", (TOKENS + 128, C), F32, kind="ExternalOutput").ap())
    audio_tower(nc, *args)
    r = _run(nc, [maps], core_ids=[0])
    return r.results[0]["out_rows"][:TOKENS].reshape(STREAMS, FRAMES, C)
```
